# Optimizing a Trainium2 kernel written in Bass

```python
import numpy as np
import jax
import jax.numpy as jnp

def _softmax(x, axis=-1):
    return jax.nn.softmax(x, axis=axis)

def _gelu(x):
    return jax.nn.gelu(x, approximate=True)

def _silu(x):
    return jax.nn.silu(x)

def _sigmoid(x):
    return jax.nn.sigmoid(x)

def _layernorm(x, axis=-1, eps=1e-05):
    m = jnp.mean(x, axis=axis, keepdims=True)
    v = jnp.var(x, axis=axis, keepdims=True)
    return (x - m) / jnp.sqrt(v + eps)

def _scatter_add(tgt, idx, src, axis=0):
    return tgt.at[idx].add(src)

def _segment_sum(src, seg, n):
    return jax.ops.segment_sum(src, seg, n)
kernel_name = 'mk_prb_d2_jaxref_r4_6f8ba7'

def setup_inputs(seed: int=0):
    np.random.seed(seed)
    _w = jnp.asarray

    def _L0_attn_setup():
        import jax, jax.numpy as jnp
        import numpy as np
        B, T, D = (2, 512, 256)
        H = 8
        KD = 128
        VD = 64
        KEY_DIM = H * KD
        VAL_DIM = H * VD
        KS = 4
        EPS_NORM = 1e-06
        EPS_RMS = 1e-05

        def _xavier(key, shape):
            fan_in, fan_out = (shape[0], shape[1])
            lim = np.sqrt(6.0 / (fan_in + fan_out))
            return jax.random.uniform(key, shape, jnp.float32, -lim, lim)

        def _causal_dw_conv_silu(x, w):
            C = x.shape[-1]
            y = jax.lax.conv_general_dilated(jnp.swapaxes(x, 1, 2), w[:, None, :], window_strides=(1,), padding=[(KS - 1, 0)], feature_group_count=C)
            return jax.nn.silu(jnp.swapaxes(y, 1, 2))

        def _l2norm(x):
            n = jnp.sqrt(jnp.sum(x * x, axis=-1, keepdims=True))
            return x / jnp.maximum(n, EPS_NORM)

        def _gdn_forward(x, Wq, Wk, Wv, Wa, Wb, Wg, Wo, A_log, dt_bias, conv_q, conv_k, conv_v, o_norm_w):
            bsz, seq_len, _ = x.shape
            beta = jax.nn.sigmoid(x @ Wb) * 2.0
            g = -jnp.exp(A_log)[None, None, :] * jax.nn.softplus(x @ Wa + dt_bias[None, None, :])
            alpha = jnp.exp(g)
            q = _causal_dw_conv_silu(x @ Wq, conv_q).reshape(bsz, seq_len, H, KD)
            k = _causal_dw_conv_silu(x @ Wk, conv_k).reshape(bsz, seq_len, H, KD)
            v = _causal_dw_conv_silu(x @ Wv, conv_v).reshape(bsz, seq_len, H, VD)
            q = _l2norm(q)
            k = _l2norm(k)
            qT = jnp.swapaxes(q, 0, 1)
            kT = jnp.swapaxes(k, 0, 1)
            vT = jnp.swapaxes(v, 0, 1)
            aT = jnp.swapaxes(alpha, 0, 1)
            bT = jnp.swapaxes(beta, 0, 1)

            def step(state, inp):
                q_t, k_t, v_t, a_t, b_t = inp
                retained = jnp.einsum('bhvk,bhk->bhv', state, k_t)
                a4 = a_t[..., None, None]
                b4 = b_t[..., None, None]
                rk = retained[..., None] * k_t[:, :, None, :]
                vk = v_t[..., None] * k_t[:, :, None, :]
                state = a4 * (state - b4 * rk) + b4 * vk
                o_t = jnp.einsum('bhvk,bhk->bhv', state, q_t)
                return (state, o_t)
            state0 = jnp.zeros((bsz, H, VD, KD), jnp.float32)
            _, outT = jax.lax.scan(step, state0, (qT, kT, vT, aT, bT))
            out = jnp.swapaxes(outT, 0, 1)
            gate = (x @ Wg).reshape(bsz, seq_len, H, VD)
            rms = jax.lax.rsqrt(jnp.mean(out * out, axis=-1, keepdims=True) + EPS_RMS)
            out = out * rms * o_norm_w * jax.nn.silu(gate)
            out = out.reshape(bsz, seq_len, VAL_DIM)
            return out @ Wo
        key = jax.random.key(seed)
        ks = jax.random.split(key, 16)
        x = jax.random.normal(ks[0], (B, T, D), jnp.float32)
        Wq = _xavier(ks[1], (D, KEY_DIM))
        Wk = _xavier(ks[2], (D, KEY_DIM))
        Wv = _xavier(ks[3], (D, VAL_DIM))
        Wa = _xavier(ks[4], (D, H))
        Wb = _xavier(ks[5], (D, H))
        Wg = _xavier(ks[6], (D, VAL_DIM))
        Wo = _xavier(ks[7], (VAL_DIM, D))
        A_log = jnp.log(jax.random.uniform(ks[8], (H,), jnp.float32, 0.5, 16.0))
        dt = jnp.exp(jax.random.uniform(ks[9], (H,), jnp.float32, np.log(0.001), np.log(0.1)))
        dt = jnp.clip(dt, 0.0001, None)
        dt_bias = dt + jnp.log(-jnp.expm1(-dt))

        def conv_w(k, c):
            lim = np.sqrt(6.0 / (1 + KS))
            return jax.random.uniform(k, (c, KS), jnp.float32, -lim, lim)
        conv_q = conv_w(ks[10], KEY_DIM)
        conv_k = conv_w(ks[11], KEY_DIM)
        conv_v = conv_w(ks[12], VAL_DIM)
        o_norm_w = jnp.ones((VD,), jnp.float32)
        return dict(x=x, Wq=Wq, Wk=Wk, Wv=Wv, Wa=Wa, Wb=Wb, Wg=Wg, Wo=Wo, A_log=A_log, dt_bias=dt_bias, conv_q=conv_q, conv_k=conv_k, conv_v=conv_v, o_norm_w=o_norm_w)
    _L0_attn_in = _L0_attn_setup()

    def _L0_ffn_setup():
        import jax, jax.numpy as jnp
        import numpy as np
        D = 256
        LW = 16
        DEPTH = 8
        NN = 2 ** DEPTH - 1
        NL = 2 ** DEPTH
        B, S = (2, 256)

        def _fff(x, nw, nb, w1, b1, w2, b2, act):
            node = jnp.zeros(x.shape[:2], dtype=jnp.int32)
            for _ in range(DEPTH):
                logit = jnp.einsum('bsd,bsd->bs', x, nw[node]) + nb[node]
                node = 2 * node + 1 + (logit > 0).astype(jnp.int32)
            leaf = node - NN
            h = act(jnp.einsum('bsd,bsdl->bsl', x, w1[leaf]) + b1[leaf])
            return jnp.einsum('bsl,bsld->bsd', h, w2[leaf]) + b2[leaf]

        def _forward(x, q_nw, q_nb, q_w1, q_b1, q_w2, q_b2, k_nw, k_nb, k_w1, k_b1, k_w2, k_b2, v_nw, v_nb, v_w1, v_b1, v_w2, v_b2, f_nw, f_nb, f_w1, f_b1, f_w2, f_b2):
            mu = jnp.mean(x, -1, keepdims=True)
            sd = jnp.std(x, -1, ddof=1, keepdims=True)
            xn = (x - mu) / jnp.sqrt(sd + 1e-05)
            relu = jax.nn.relu
            q = _fff(xn, q_nw, q_nb, q_w1, q_b1, q_w2, q_b2, relu)
            k = _fff(xn, k_nw, k_nb, k_w1, k_b1, k_w2, k_b2, relu)
            v = _fff(xn, v_nw, v_nb, v_w1, v_b1, v_w2, v_b2, relu)
            att = jax.nn.softmax(jnp.einsum('bqd,bkd->bqk', q, k) / jnp.sqrt(jnp.float32(D)), axis=-1)
            y = xn + jnp.einsum('bqk,bkd->bqd', att, v)
            gelu = lambda t: jax.nn.gelu(t, approximate=False)
            return y + _fff(y, f_nw, f_nb, f_w1, f_b1, f_w2, f_b2, gelu)

        def _make_fff_params(key, scale_in, scale_leaf):
            ks = jax.random.split(key, 4)
            nw = jax.random.normal(ks[0], (NN, D), jnp.float32) * scale_in
            nb = jnp.zeros((NN,), jnp.float32)
            w1 = jax.random.normal(ks[1], (NL, D, LW), jnp.float32) * scale_in
            b1 = jax.random.normal(ks[2], (NL, LW), jnp.float32) * 0.01
            w2 = jax.random.normal(ks[3], (NL, LW, D), jnp.float32) * scale_leaf
            b2 = jnp.zeros((NL, D), jnp.float32)
            return (nw, nb, w1, b1, w2, b2)
        key = jax.random.key(seed)
        kx, kq, kk, kv, kf = jax.random.split(key, 5)
        s_in = 1.0 / np.sqrt(D)
        s_lf = 1.0 / np.sqrt(LW)
        inp = {'x': jax.random.normal(kx, (B, S, D), jnp.float32)}
        for name, kk_ in (('q', kq), ('k', kk), ('v', kv), ('f', kf)):
            nw, nb, w1, b1, w2, b2 = _make_fff_params(kk_, s_in, s_lf)
            inp.update({f'{name}_nw': nw, f'{name}_nb': nb, f'{name}_w1': w1, f'{name}_b1': b1, f'{name}_w2': w2, f'{name}_b2': b2})
        return inp
    _L0_ffn_in = _L0_ffn_setup()

    def _L1_attn_setup():
        import jax, jax.numpy as jnp
        import numpy as np
        from jax import lax
        B, T, D = (4, 1024, 256)
        H, d = (4, 64)
        EPS = 1e-06

        def pos_unit(x):
            p = jax.nn.elu(x) + 1.0
            return p / (jnp.linalg.norm(p, axis=-1, keepdims=True) + EPS)

        def _reference_tuple_inner(x, Wq, Wk, Wv, Wo):
            Bx, Tx, Dx = x.shape
            q = (x @ Wq.T).reshape(Bx, Tx, H, d)
            k = (x @ Wk.T).reshape(Bx, Tx, H, d)
            v = (x @ Wv.T).reshape(Bx, Tx, H, d)
            q = pos_unit(q)
            k = pos_unit(k)
            qT = jnp.transpose(q, (1, 0, 2, 3))
            kT = jnp.transpose(k, (1, 0, 2, 3))
            vT = jnp.transpose(v, (1, 0, 2, 3))
            kv0 = jnp.zeros((Bx, H, d, d), dtype=x.dtype)
            kc0 = jnp.zeros((Bx, H, d), dtype=x.dtype)

            def step(carry, inp):
                kv_cum, k_cum = carry
                qt, kt, vt = inp
                kv_cum = kv_cum + jnp.einsum('bhd,bhj->bhjd', kt, vt)
                k_cum = k_cum + kt
                num = jnp.einsum('bhd,bhjd->bhj', qt, kv_cum)
                den = jnp.einsum('bhd,bhd->bh', qt, k_cum)[..., None] + EPS
                return ((kv_cum, k_cum), num / den)
            (kv_f, kc_f), yT = lax.scan(step, (kv0, kc0), (qT, kT, vT))
            y = jnp.transpose(yT, (1, 0, 2, 3)).reshape(Bx, Tx, H * d)
            y = y @ Wo.T
            return (y, kv_f, kc_f)
        key = jax.random.key(seed)
        ks = jax.random.split(key, 5)
        s_in = 1.0 / np.sqrt(D)
        s_hd = 1.0 / np.sqrt(H * d)
        return {'x': jax.random.normal(ks[0], (B, T, D), dtype=jnp.float32), 'Wq': jax.random.normal(ks[1], (H * d, D), dtype=jnp.float32) * s_in, 'Wk': jax.random.normal(ks[2], (H * d, D), dtype=jnp.float32) * s_in, 'Wv': jax.random.normal(ks[3], (H * d, D), dtype=jnp.float32) * s_in, 'Wo': jax.random.normal(ks[4], (D, H * d), dtype=jnp.float32) * s_hd}
    _L1_attn_in = _L1_attn_setup()

    def _L1_ffn_setup():
        import jax, jax.numpy as jnp
        import numpy as np
        N_HEADS = 16
        N_KV_HEADS = 4
        N_EMBD = 256
        HEAD_DIM = N_EMBD // N_HEADS
        N_EXPERTS = 8
        TOP_K = 2
        EPS = 1e-06

        def _rmsnorm(x, w):
            xf = x.astype(jnp.float32)
            n = xf * jax.lax.rsqrt(jnp.mean(xf * xf, axis=-1, keepdims=True) + EPS)
            return n.astype(x.dtype) * w

        def _gqa(x, wq, wk, wv, wo):
            B, S, C = x.shape
            n_rep = N_HEADS // N_KV_HEADS
            q = (x @ wq.T).reshape(B, S, N_HEADS, HEAD_DIM)
            k = (x @ wk.T).reshape(B, S, N_KV_HEADS, HEAD_DIM)
            v = (x @ wv.T).reshape(B, S, N_KV_HEADS, HEAD_DIM)
            k = jnp.repeat(k, n_rep, axis=2)
            v = jnp.repeat(v, n_rep, axis=2)
            scale = 1.0 / np.sqrt(HEAD_DIM).astype(np.float32)
            attn = jnp.einsum('bqhd,bkhd->bhqk', q, k) * scale
            causal = jnp.tril(jnp.ones((S, S), dtype=bool))
            attn = jnp.where(causal, attn, jnp.float32(-jnp.inf))
            attn = jax.nn.softmax(attn, axis=-1)
            out = jnp.einsum('bhqk,bkhd->bqhd', attn, v).reshape(B, S, C)
            return out @ wo.T

        def _moe(x, gate_w, expert_w):
            B, S, C = x.shape
            t = x.reshape(B * S, C)
            logits = t @ gate_w.T
            w, sel = jax.lax.top_k(logits, TOP_K)
            w = jax.nn.softmax(w.astype(jnp.float32), axis=1).astype(t.dtype)
            comb = jnp.sum(w[..., None] * jax.nn.one_hot(sel, N_EXPERTS, dtype=t.dtype), axis=1)
            out = jnp.zeros_like(t)
            for e in range(N_EXPERTS):
                out = out + comb[:, e, None] * (t @ expert_w[e].T)
            return out.reshape(B, S, C)
        key = jax.random.key(seed)
        ks = jax.random.split(key, 10)
        B, S, C = (4, 512, N_EMBD)
        s = 0.02
        return {'x': jax.random.normal(ks[0], (B, S, C), dtype=jnp.float32), 'attn_norm_w': jnp.ones((C,), dtype=jnp.float32), 'ffn_norm_w': jnp.ones((C,), dtype=jnp.float32), 'wq': jax.random.normal(ks[1], (C, C), dtype=jnp.float32) * s, 'wk': jax.random.normal(ks[2], (N_KV_HEADS * HEAD_DIM, C), dtype=jnp.float32) * s, 'wv': jax.random.normal(ks[3], (N_KV_HEADS * HEAD_DIM, C), dtype=jnp.float32) * s, 'wo': jax.random.normal(ks[4], (C, C), dtype=jnp.float32) * s, 'gate_w': jax.random.normal(ks[5], (N_EXPERTS, C), dtype=jnp.float32) * s, 'expert_w': jax.random.normal(ks[6], (N_EXPERTS, C, C), dtype=jnp.float32) * s}
    _L1_ffn_in = _L1_ffn_setup()
    _d = {'L0_attn_x': _L0_attn_in['x'], 'L0_attn_Wq': _L0_attn_in['Wq'], 'L0_attn_Wk': _L0_attn_in['Wk'], 'L0_attn_Wv': _L0_attn_in['Wv'], 'L0_attn_Wa': _L0_attn_in['Wa'], 'L0_attn_Wb': _L0_attn_in['Wb'], 'L0_attn_Wg': _L0_attn_in['Wg'], 'L0_attn_Wo': _L0_attn_in['Wo'], 'L0_attn_A_log': _L0_attn_in['A_log'], 'L0_attn_dt_bias': _L0_attn_in['dt_bias'], 'L0_attn_conv_q': _L0_attn_in['conv_q'], 'L0_attn_conv_k': _L0_attn_in['conv_k'], 'L0_attn_conv_v': _L0_attn_in['conv_v'], 'L0_attn_o_norm_w': _L0_attn_in['o_norm_w'], 'L0_ffn_q_nw': _L0_ffn_in['q_nw'], 'L0_ffn_q_nb': _L0_ffn_in['q_nb'], 'L0_ffn_q_w1': _L0_ffn_in['q_w1'], 'L0_ffn_q_b1': _L0_ffn_in['q_b1'], 'L0_ffn_q_w2': _L0_ffn_in['q_w2'], 'L0_ffn_q_b2': _L0_ffn_in['q_b2'], 'L0_ffn_k_nw': _L0_ffn_in['k_nw'], 'L0_ffn_k_nb': _L0_ffn_in['k_nb'], 'L0_ffn_k_w1': _L0_ffn_in['k_w1'], 'L0_ffn_k_b1': _L0_ffn_in['k_b1'], 'L0_ffn_k_w2': _L0_ffn_in['k_w2'], 'L0_ffn_k_b2': _L0_ffn_in['k_b2'], 'L0_ffn_v_nw': _L0_ffn_in['v_nw'], 'L0_ffn_v_nb': _L0_ffn_in['v_nb'], 'L0_ffn_v_w1': _L0_ffn_in['v_w1'], 'L0_ffn_v_b1': _L0_ffn_in['v_b1'], 'L0_ffn_v_w2': _L0_ffn_in['v_w2'], 'L0_ffn_v_b2': _L0_ffn_in['v_b2'], 'L0_ffn_f_nw': _L0_ffn_in['f_nw'], 'L0_ffn_f_nb': _L0_ffn_in['f_nb'], 'L0_ffn_f_w1': _L0_ffn_in['f_w1'], 'L0_ffn_f_b1': _L0_ffn_in['f_b1'], 'L0_ffn_f_w2': _L0_ffn_in['f_w2'], 'L0_ffn_f_b2': _L0_ffn_in['f_b2'], 'L1_attn_Wq': _L1_attn_in['Wq'], 'L1_attn_Wk': _L1_attn_in['Wk'], 'L1_attn_Wv': _L1_attn_in['Wv'], 'L1_attn_Wo': _L1_attn_in['Wo'], 'L1_ffn_attn_norm_w': _L1_ffn_in['attn_norm_w'], 'L1_ffn_ffn_norm_w': _L1_ffn_in['ffn_norm_w'], 'L1_ffn_wq': _L1_ffn_in['wq'], 'L1_ffn_wk': _L1_ffn_in['wk'], 'L1_ffn_wv': _L1_ffn_in['wv'], 'L1_ffn_wo': _L1_ffn_in['wo'], 'L1_ffn_gate_w': _L1_ffn_in['gate_w'], 'L1_ffn_expert_w': _L1_ffn_in['expert_w']}
    _x0 = _d['L0_attn_x']
    _d['L0_attn_x'] = jax.random.normal(jax.random.fold_in(jax.random.key(seed), 1), (8, 512, 256), dtype=_x0.dtype)
    del _x0
    return _d

def reference(L0_attn_x, L0_attn_Wq, L0_attn_Wk, L0_attn_Wv, L0_attn_Wa, L0_attn_Wb, L0_attn_Wg, L0_attn_Wo, L0_attn_A_log, L0_attn_dt_bias, L0_attn_conv_q, L0_attn_conv_k, L0_attn_conv_v, L0_attn_o_norm_w, L0_ffn_q_nw, L0_ffn_q_nb, L0_ffn_q_w1, L0_ffn_q_b1, L0_ffn_q_w2, L0_ffn_q_b2, L0_ffn_k_nw, L0_ffn_k_nb, L0_ffn_k_w1, L0_ffn_k_b1, L0_ffn_k_w2, L0_ffn_k_b2, L0_ffn_v_nw, L0_ffn_v_nb, L0_ffn_v_w1, L0_ffn_v_b1, L0_ffn_v_w2, L0_ffn_v_b2, L0_ffn_f_nw, L0_ffn_f_nb, L0_ffn_f_w1, L0_ffn_f_b1, L0_ffn_f_w2, L0_ffn_f_b2, L1_attn_Wq, L1_attn_Wk, L1_attn_Wv, L1_attn_Wo, L1_ffn_attn_norm_w, L1_ffn_ffn_norm_w, L1_ffn_wq, L1_ffn_wk, L1_ffn_wv, L1_ffn_wo, L1_ffn_gate_w, L1_ffn_expert_w):

    def _L0_attn_ref(x, Wq, Wk, Wv, Wa, Wb, Wg, Wo, A_log, dt_bias, conv_q, conv_k, conv_v, o_norm_w):
        import jax, jax.numpy as jnp
        import numpy as np
        B, T, D = (2, 512, 256)
        H = 8
        KD = 128
        VD = 64
        KEY_DIM = H * KD
        VAL_DIM = H * VD
        KS = 4
        EPS_NORM = 1e-06
        EPS_RMS = 1e-05

        def _xavier(key, shape):
            fan_in, fan_out = (shape[0], shape[1])
            lim = np.sqrt(6.0 / (fan_in + fan_out))
            return jax.random.uniform(key, shape, jnp.float32, -lim, lim)

        def _causal_dw_conv_silu(x, w):
            C = x.shape[-1]
            y = jax.lax.conv_general_dilated(jnp.swapaxes(x, 1, 2), w[:, None, :], window_strides=(1,), padding=[(KS - 1, 0)], feature_group_count=C)
            return jax.nn.silu(jnp.swapaxes(y, 1, 2))

        def _l2norm(x):
            n = jnp.sqrt(jnp.sum(x * x, axis=-1, keepdims=True))
            return x / jnp.maximum(n, EPS_NORM)

        def _gdn_forward(x, Wq, Wk, Wv, Wa, Wb, Wg, Wo, A_log, dt_bias, conv_q, conv_k, conv_v, o_norm_w):
            bsz, seq_len, _ = x.shape
            beta = jax.nn.sigmoid(x @ Wb) * 2.0
            g = -jnp.exp(A_log)[None, None, :] * jax.nn.softplus(x @ Wa + dt_bias[None, None, :])
            alpha = jnp.exp(g)
            q = _causal_dw_conv_silu(x @ Wq, conv_q).reshape(bsz, seq_len, H, KD)
            k = _causal_dw_conv_silu(x @ Wk, conv_k).reshape(bsz, seq_len, H, KD)
            v = _causal_dw_conv_silu(x @ Wv, conv_v).reshape(bsz, seq_len, H, VD)
            q = _l2norm(q)
            k = _l2norm(k)
            qT = jnp.swapaxes(q, 0, 1)
            kT = jnp.swapaxes(k, 0, 1)
            vT = jnp.swapaxes(v, 0, 1)
            aT = jnp.swapaxes(alpha, 0, 1)
            bT = jnp.swapaxes(beta, 0, 1)

            def step(state, inp):
                q_t, k_t, v_t, a_t, b_t = inp
                retained = jnp.einsum('bhvk,bhk->bhv', state, k_t)
                a4 = a_t[..., None, None]
                b4 = b_t[..., None, None]
                rk = retained[..., None] * k_t[:, :, None, :]
                vk = v_t[..., None] * k_t[:, :, None, :]
                state = a4 * (state - b4 * rk) + b4 * vk
                o_t = jnp.einsum('bhvk,bhk->bhv', state, q_t)
                return (state, o_t)
            state0 = jnp.zeros((bsz, H, VD, KD), jnp.float32)
            _, outT = jax.lax.scan(step, state0, (qT, kT, vT, aT, bT))
            out = jnp.swapaxes(outT, 0, 1)
            gate = (x @ Wg).reshape(bsz, seq_len, H, VD)
            rms = jax.lax.rsqrt(jnp.mean(out * out, axis=-1, keepdims=True) + EPS_RMS)
            out = out * rms * o_norm_w * jax.nn.silu(gate)
            out = out.reshape(bsz, seq_len, VAL_DIM)
            return out @ Wo
        return _gdn_forward(x, Wq, Wk, Wv, Wa, Wb, Wg, Wo, A_log, dt_bias, conv_q, conv_k, conv_v, o_norm_w)

    def _L0_ffn_ref(x, q_nw, q_nb, q_w1, q_b1, q_w2, q_b2, k_nw, k_nb, k_w1, k_b1, k_w2, k_b2, v_nw, v_nb, v_w1, v_b1, v_w2, v_b2, f_nw, f_nb, f_w1, f_b1, f_w2, f_b2):
        import jax, jax.numpy as jnp
        import numpy as np
        D = 256
        LW = 16
        DEPTH = 8
        NN = 2 ** DEPTH - 1
        NL = 2 ** DEPTH
        B, S = (2, 256)

        def _fff(x, nw, nb, w1, b1, w2, b2, act):
            node = jnp.zeros(x.shape[:2], dtype=jnp.int32)
            for _ in range(DEPTH):
                logit = jnp.einsum('bsd,bsd->bs', x, nw[node]) + nb[node]
                node = 2 * node + 1 + (logit > 0).astype(jnp.int32)
            leaf = node - NN
            h = act(jnp.einsum('bsd,bsdl->bsl', x, w1[leaf]) + b1[leaf])
            return jnp.einsum('bsl,bsld->bsd', h, w2[leaf]) + b2[leaf]

        def _forward(x, q_nw, q_nb, q_w1, q_b1, q_w2, q_b2, k_nw, k_nb, k_w1, k_b1, k_w2, k_b2, v_nw, v_nb, v_w1, v_b1, v_w2, v_b2, f_nw, f_nb, f_w1, f_b1, f_w2, f_b2):
            mu = jnp.mean(x, -1, keepdims=True)
            sd = jnp.std(x, -1, ddof=1, keepdims=True)
            xn = (x - mu) / jnp.sqrt(sd + 1e-05)
            relu = jax.nn.relu
            q = _fff(xn, q_nw, q_nb, q_w1, q_b1, q_w2, q_b2, relu)
            k = _fff(xn, k_nw, k_nb, k_w1, k_b1, k_w2, k_b2, relu)
            v = _fff(xn, v_nw, v_nb, v_w1, v_b1, v_w2, v_b2, relu)
            att = jax.nn.softmax(jnp.einsum('bqd,bkd->bqk', q, k) / jnp.sqrt(jnp.float32(D)), axis=-1)
            y = xn + jnp.einsum('bqk,bkd->bqd', att, v)
            gelu = lambda t: jax.nn.gelu(t, approximate=False)
            return y + _fff(y, f_nw, f_nb, f_w1, f_b1, f_w2, f_b2, gelu)

        def _make_fff_params(key, scale_in, scale_leaf):
            ks = jax.random.split(key, 4)
            nw = jax.random.normal(ks[0], (NN, D), jnp.float32) * scale_in
            nb = jnp.zeros((NN,), jnp.float32)
            w1 = jax.random.normal(ks[1], (NL, D, LW), jnp.float32) * scale_in
            b1 = jax.random.normal(ks[2], (NL, LW), jnp.float32) * 0.01
            w2 = jax.random.normal(ks[3], (NL, LW, D), jnp.float32) * scale_leaf
            b2 = jnp.zeros((NL, D), jnp.float32)
            return (nw, nb, w1, b1, w2, b2)
        return _forward(x, q_nw, q_nb, q_w1, q_b1, q_w2, q_b2, k_nw, k_nb, k_w1, k_b1, k_w2, k_b2, v_nw, v_nb, v_w1, v_b1, v_w2, v_b2, f_nw, f_nb, f_w1, f_b1, f_w2, f_b2)

    def _L1_attn_ref(x, Wq, Wk, Wv, Wo):
        import jax, jax.numpy as jnp
        import numpy as np
        from jax import lax
        B, T, D = (4, 1024, 256)
        H, d = (4, 64)
        EPS = 1e-06

        def pos_unit(x):
            p = jax.nn.elu(x) + 1.0
            return p / (jnp.linalg.norm(p, axis=-1, keepdims=True) + EPS)

        def _reference_tuple_inner(x, Wq, Wk, Wv, Wo):
            Bx, Tx, Dx = x.shape
            q = (x @ Wq.T).reshape(Bx, Tx, H, d)
            k = (x @ Wk.T).reshape(Bx, Tx, H, d)
            v = (x @ Wv.T).reshape(Bx, Tx, H, d)
            q = pos_unit(q)
            k = pos_unit(k)
            qT = jnp.transpose(q, (1, 0, 2, 3))
            kT = jnp.transpose(k, (1, 0, 2, 3))
            vT = jnp.transpose(v, (1, 0, 2, 3))
            kv0 = jnp.zeros((Bx, H, d, d), dtype=x.dtype)
            kc0 = jnp.zeros((Bx, H, d), dtype=x.dtype)

            def step(carry, inp):
                kv_cum, k_cum = carry
                qt, kt, vt = inp
                kv_cum = kv_cum + jnp.einsum('bhd,bhj->bhjd', kt, vt)
                k_cum = k_cum + kt
                num = jnp.einsum('bhd,bhjd->bhj', qt, kv_cum)
                den = jnp.einsum('bhd,bhd->bh', qt, k_cum)[..., None] + EPS
                return ((kv_cum, k_cum), num / den)
            (kv_f, kc_f), yT = lax.scan(step, (kv0, kc0), (qT, kT, vT))
            y = jnp.transpose(yT, (1, 0, 2, 3)).reshape(Bx, Tx, H * d)
            y = y @ Wo.T
            return (y, kv_f, kc_f)
        return _reference_tuple_inner(x, Wq, Wk, Wv, Wo)[0]

    def _L1_ffn_ref(x, attn_norm_w, ffn_norm_w, wq, wk, wv, wo, gate_w, expert_w):
        import jax, jax.numpy as jnp
        import numpy as np
        N_HEADS = 16
        N_KV_HEADS = 4
        N_EMBD = 256
        HEAD_DIM = N_EMBD // N_HEADS
        N_EXPERTS = 8
        TOP_K = 2
        EPS = 1e-06

        def _rmsnorm(x, w):
            xf = x.astype(jnp.float32)
            n = xf * jax.lax.rsqrt(jnp.mean(xf * xf, axis=-1, keepdims=True) + EPS)
            return n.astype(x.dtype) * w

        def _gqa(x, wq, wk, wv, wo):
            B, S, C = x.shape
            n_rep = N_HEADS // N_KV_HEADS
            q = (x @ wq.T).reshape(B, S, N_HEADS, HEAD_DIM)
            k = (x @ wk.T).reshape(B, S, N_KV_HEADS, HEAD_DIM)
            v = (x @ wv.T).reshape(B, S, N_KV_HEADS, HEAD_DIM)
            k = jnp.repeat(k, n_rep, axis=2)
            v = jnp.repeat(v, n_rep, axis=2)
            scale = 1.0 / np.sqrt(HEAD_DIM).astype(np.float32)
            attn = jnp.einsum('bqhd,bkhd->bhqk', q, k) * scale
            causal = jnp.tril(jnp.ones((S, S), dtype=bool))
            attn = jnp.where(causal, attn, jnp.float32(-jnp.inf))
            attn = jax.nn.softmax(attn, axis=-1)
            out = jnp.einsum('bhqk,bkhd->bqhd', attn, v).reshape(B, S, C)
            return out @ wo.T

        def _moe(x, gate_w, expert_w):
            B, S, C = x.shape
            t = x.reshape(B * S, C)
            logits = t @ gate_w.T
            w, sel = jax.lax.top_k(logits, TOP_K)
            w = jax.nn.softmax(w.astype(jnp.float32), axis=1).astype(t.dtype)
            comb = jnp.sum(w[..., None] * jax.nn.one_hot(sel, N_EXPERTS, dtype=t.dtype), axis=1)
            out = jnp.zeros_like(t)
            for e in range(N_EXPERTS):
                out = out + comb[:, e, None] * (t @ expert_w[e].T)
            return out.reshape(B, S, C)
        h = x + _gqa(_rmsnorm(x, attn_norm_w), wq, wk, wv, wo)
        out = h + _moe(_rmsnorm(h, ffn_norm_w), gate_w, expert_w)
        return out
    x = L0_attn_x
    xn = _layernorm(x, axis=-1)
    x = x + _L0_attn_ref(xn, L0_attn_Wq, L0_attn_Wk, L0_attn_Wv, L0_attn_Wa, L0_attn_Wb, L0_attn_Wg, L0_attn_Wo, L0_attn_A_log, L0_attn_dt_bias, L0_attn_conv_q, L0_attn_conv_k, L0_attn_conv_v, L0_attn_o_norm_w) + _L0_ffn_ref(xn, L0_ffn_q_nw, L0_ffn_q_nb, L0_ffn_q_w1, L0_ffn_q_b1, L0_ffn_q_w2, L0_ffn_q_b2, L0_ffn_k_nw, L0_ffn_k_nb, L0_ffn_k_w1, L0_ffn_k_b1, L0_ffn_k_w2, L0_ffn_k_b2, L0_ffn_v_nw, L0_ffn_v_nb, L0_ffn_v_w1, L0_ffn_v_b1, L0_ffn_v_w2, L0_ffn_v_b2, L0_ffn_f_nw, L0_ffn_f_nb, L0_ffn_f_w1, L0_ffn_f_b1, L0_ffn_f_w2, L0_ffn_f_b2)
    xn = _layernorm(x, axis=-1)
    x = x + _L1_attn_ref(xn, L1_attn_Wq, L1_attn_Wk, L1_attn_Wv, L1_attn_Wo) + _L1_ffn_ref(xn, L1_ffn_attn_norm_w, L1_ffn_ffn_norm_w, L1_ffn_wq, L1_ffn_wk, L1_ffn_wv, L1_ffn_wo, L1_ffn_gate_w, L1_ffn_expert_w)
    return x

_drawn_inputs = setup_inputs


def setup_inputs(seed=0):
    import zlib

    import numpy as np

    out = dict(_drawn_inputs(seed))
    spreads = {'L0_attn_o_norm_w': (1.0, 0.2),
     'L0_ffn_q_nb': (0.0, 0.1),
     'L0_ffn_q_b2': (0.0, 0.1),
     'L0_ffn_k_nb': (0.0, 0.1),
     'L0_ffn_k_b2': (0.0, 0.1),
     'L0_ffn_v_nb': (0.0, 0.1),
     'L0_ffn_v_b2': (0.0, 0.1),
     'L0_ffn_f_nb': (0.0, 0.1),
     'L0_ffn_f_b2': (0.0, 0.1),
     'L1_ffn_attn_norm_w': (1.0, 0.6),
     'L1_ffn_ffn_norm_w': (1.0, 0.6)}
    factors = {'L0_ffn_q_b1': 6.181,
     'L0_ffn_k_b1': 6.287,
     'L0_ffn_v_b1': 6.707,
     'L0_ffn_f_b1': 8.0,
     'L1_attn_Wq': 64.0,
     'L1_attn_Wk': 64.0,
     'L1_ffn_wq': 8.0,
     'L1_ffn_wk': 8.0,
     'L1_ffn_wv': 7.225,
     'L1_ffn_wo': 7.281,
     'L1_attn_Wv': 3.29,
     'L1_attn_Wo': 3.291}
    for name, (base, spread) in spreads.items():
        noise = np.random.default_rng([zlib.crc32(name.encode()), seed]).standard_normal(out[name].shape)
        drawn = base * np.exp(spread * noise) if base else spread * noise
        out[name] = jnp.asarray(drawn.astype(out[name].dtype))
    for name, factor in factors.items():
        out[name] = (out[name] * factor).astype(out[name].dtype)
    return out
```

```python
import numpy as np
import concourse.bass as bass
from concourse import mybir
from concourse.alu_op_type import AluOpType as ALU
from contextlib import ExitStack

F32 = mybir.dt.float32
BF16 = mybir.dt.bfloat16
I32 = mybir.dt.int32
U32 = mybir.dt.uint32
ACT = mybir.ActivationFunctionType
AX = mybir.AxisListType
ds = bass.ds

P = 128
N_BATCH, SEQ, DIM = 8, 512, 256
TOKENS = N_BATCH * SEQ
TILES = TOKENS // P
TPB = SEQ // P
KC = DIM // P
START = 8192


def start(key):
    return 0 if key[0] == "g" and len(key) > 1 else START


class Stage:

    def __init__(self, name, count):
        self.name, self.count = name, count
        self.queue = {e: [] for e in "tvsgy"}
        self.producers = {}
        self.stores = []

    def op(self, engine, fn, after=(), name=None, alone=False):
        entry = dict(fn=fn, after=after, name=name, alone=alone, dma=None)
        self.queue[engine].append(entry)
        if name:
            assert name not in self.producers, name
            self.producers[name] = (engine, entry)
        return entry

    def dma(self, engine, fn, after=(), name=None):
        entry = self.op(engine, fn, after, name, alone=True)
        entry["dma"] = (engine, len(self.stores))
        self.stores.append(entry)
        return entry


class Slots:

    def __init__(self, stage):
        self.stage, self.reader = stage, {}

    def free(self, slot):
        return self.reader.get(slot, (f"last reader of {slot}", 1))

    def read(self, slot, by):
        self.reader[slot] = by

    def close(self):
        for slot, by in self.reader.items():
            self.stage.producers[f"last reader of {slot}"] = self.stage.producers[by]


class Program:

    def __init__(self, nc, ctx):
        self.nc, self.ctx, self.groups = nc, ctx, []

    def group(self, times=1):
        self.groups.append((times, []))

    def stage(self, name, count=1):
        s = Stage(name, count)
        self.groups[-1][1].append(s)
        return s

    def number(self):
        self.sems = {}
        self.idle = self.ctx.enter_context(self.nc.semaphore("idle"))
        level = {}
        for times, stages in self.groups:
            first = dict(level)
            for s in stages:
                names = {p if isinstance(p, str) else p[0] for e in "tvsgy" for o in s.queue[e] for p in o["after"]}
                assert names <= set(s.producers), (s.name, names - set(s.producers))
                wanted = {id(s.producers[p][1]) for p in names}
                s.step, s.base = {}, {}
                for e in "tvsg":
                    mine = [o for o in s.queue[e] if o["dma"] is None]
                    n = 0
                    for o in mine:
                        o["rank"] = None
                        if id(o) in wanted or o is mine[-1]:
                            n += 1
                            o["rank"] = n
                    s.step[e] = n
                for o in s.stores:
                    s.step[o["dma"]] = 16
                    o["rank"] = 16
                for key, n in s.step.items():
                    s.base[key] = level.setdefault(key, start(key))
                    level[key] += n * s.count
            for s in stages:
                s.per_time = {k: level[k] - first.get(k, start(k)) for k in level}
            for k in level:
                level[k] = first.get(k, start(k)) + times * (level[k] - first.get(k, start(k)))
        for key in level:
            self.sems[key] = self.ctx.enter_context(self.nc.semaphore("progress_" + "".join(map(str, key))))

    def ends(self, s, f):
        for key, n in s.step.items():
            if n:
                yield key, s.base[key] + s.count * n + f * s.per_time[key]

    def emit(self, eng, e):
        previous = None
        for key in self.sems:
            if start(key) and (key == e or (e == "y" and key[0] == "y")):
                eng.sem_inc(self.sems[key], START)
        for times, stages in self.groups:
            def body(f, previous):
                for n, s in enumerate(stages):
                    waits = []
                    if n == 0:
                        if previous is not None:
                            waits += self.ends(*previous)
                        if times > 1:
                            waits += self.ends(stages[-1], f - 1)
                    else:
                        waits += self.ends(stages[n - 1], f)
                    for key, value in waits:
                        eng.wait_ge(self.sems[key], value)
                        if times > 1:
                            eng.sem_inc(self.idle, 1)
                    if s.queue[e]:
                        if s.count > 1:
                            with eng.Fori(0, s.count) as i:
                                self.run(eng, e, s, i, f)
                        else:
                            self.run(eng, e, s, 0, f)
            if times > 1:
                with eng.Fori(0, times) as f:
                    body(f, previous)
            else:
                body(0, previous)
            previous = (stages[-1], times - 1)
        if e == "y":
            for key, value in self.ends(*previous):
                eng.wait_ge(self.sems[key], value)

    def run(self, eng, e, s, i, f):
        waited = {}
        for o in s.queue[e]:
            need = {}
            for p in o["after"]:
                p, lag = p if isinstance(p, tuple) else (p, 0)
                pe, po = s.producers[p]
                if lag and s.count == 1:
                    continue
                key = po["dma"] if po["dma"] is not None else pe
                value = s.base[key] + po["rank"] - lag * s.step[key]
                if value > need.get(key, 0):
                    need[key] = value
            some = False
            for key, value in need.items():
                if value > waited.get(key, 0):
                    waited[key] = value
                    v = value + i * s.step[key]
                    if not isinstance(f, int):
                        v = v + f * s.per_time[key]
                    eng.wait_ge(self.sems[key], v)
                    if e == "y":
                        eng.sem_inc(self.idle, 1)
                    some = True
            if some and o["alone"] and e != "y":
                eng.sem_inc(self.idle, 1)
            ins = o["fn"](eng, i, f)
            if o["dma"] is not None:
                ins.then_inc(self.sems[o["dma"]], 16)
            elif o["rank"] is not None:
                ins.then_inc(self.sems[e], 1)

HEADS = 8
KINDS = 7


def rows(ap, b):
    return ap[ds(b * SEQ, SEQ), :].rearrange("(t p) d -> p t d", p=P)


def cols(ap, b):
    return ap[:, :, ds(b * SEQ, SEQ)].rearrange("c p n -> p c n")


class Kernel:

    def __init__(self, nc, pg, ctx, dram):
        self.nc, self.pg, self.ctx, self.dram = nc, pg, ctx, dram
        self.open = None
        self.bank = [ctx.enter_context(nc.psum_tensor(f"bank{b}", [P, 512], F32)) for b in range(8)]

    def keep(self, name, shape, dt=F32):
        return self.ctx.enter_context(self.nc.sbuf_tensor(name, shape, dt))

    def scoped(self):
        if self.open is not None:
            self.open.close()
        self.open = ExitStack()
        return lambda name, shape, dt=F32: self.open.enter_context(self.nc.sbuf_tensor("s_" + name, shape, dt))

    def load_constants(self):
        self.pg.group()
        s = self.pg.stage("constants", 1)

        def const(name, shape, dt=F32, view=None):
            t = self.keep("c_" + name, shape, dt)
            src = self.dram[name]
            if view == "row":
                src = src[None, :].broadcast_to((P, shape[1]))
            s.dma("y", lambda e, i, f: e.dma_start(t[:], src), [], name)
            return t

        self.ident = const("ident", [P, P])
        self.upper = const("upper", [P, P])
        self.ones = const("ones", [P, P])
        self.mask = const("mask", [P, 7, 2, P], U32)
        self.lvw = const("lvw", [P, 256], view="row")
        self.iota = const("iota", [P, 64], view="row")
        self.iota128 = const("iota128", [P, 64], view="row")
        self.wab = const("wab", [P, KC, 16])
        self.dtb = const("L0_attn_dt_bias", [P, 8], view="row")
        self.alog = const("L0_attn_A_log", [P, 8], view="row")
        self.onw = const("L0_attn_o_norm_w", [P, 64], view="row")

        def rounded(name, source):
            t = self.keep("c_" + name, [P, P], BF16)
            s.op("v", lambda e, i, f: e.tensor_copy(t[:], source[:]), [source_name[id(source)]])
            return t

        negm, negl = const("negm", [P, P]), const("negl", [P, P])
        source_name = {id(self.ident): "ident", id(self.ones): "ones", id(self.upper): "upper", id(negm): "negm", id(negl): "negl"}
        self.identb, self.onesb, self.upperb = rounded("identb", self.ident), rounded("onesb", self.ones), rounded("upperb", self.upper)
        self.negm, self.negl = rounded("negmb", negm), rounded("neglb", negl)
        self.ea = self.keep("ea", [P, 8])
        self.eps5 = self.keep("eps5", [P, 1])
        self.eps6 = self.keep("eps6", [P, 1])
        self.one = self.keep("one", [P, 1])
        s.op("v", lambda e, i, f: e.memset(self.eps5[:], 1e-5))
        s.op("v", lambda e, i, f: e.memset(self.eps6[:], 1e-6))
        s.op("v", lambda e, i, f: e.memset(self.one[:], 1.0))

def norms(g, st):
    nc, pg, sb, D = g.nc, g.pg, g.scoped(), g.dram
    pg.group()
    s = pg.stage("norms", N_BATCH)
    x = sb("x_in", [P, TPB, DIM])
    xn = sb("xn_rows", [P, TPB, DIM])
    xf = sb("xf_rows", [P, TPB, DIM])
    xnT = sb("xn_cols", [P, KC, SEQ])
    xfT = sb("xf_cols", [P, KC, SEQ])
    stat = sb("stat", [P, TPB, 6])
    mv = sb("mv", [P, TPB, 2])
    stat2 = sb("stat2", [P, TPB, 6])
    mv2 = sb("mv2", [P, TPB, 2])
    rs = sb("rs", [P, TPB, 4])
    ab = sb("ab", [P, TPB, 2 * HEADS])
    bk = g.bank
    s.dma("y", lambda e, i, f: e.dma_start(x[:], rows(D["x"], i)), [("sub", 1)], "x")
    for t in range(TPB):
        s.op("v", lambda e, i, f, t=t: e.bn_stats(stat[:, t, :], x[:, t, :]), ["x"], f"st{t}", alone=True)
    for t in range(TPB):
        s.op("v", lambda e, i, f, t=t: e.bn_aggr(mv[:, t, :], stat[:, t, :]), [f"st{t}"], f"ag{t}", alone=True)
    s.op("s", lambda e, i, f: e.activation(rs[:, :, 0:1], mv[:, :, 1:2], ACT.Sqrt, bias=g.eps5[:, 0:1]), [f"ag{TPB-1}"], "sd")
    s.op("v", lambda e, i, f: e.reciprocal(rs[:, :, 1:2], rs[:, :, 0:1]), ["sd"], "rstd")
    for t in range(TPB):
        s.op("v", lambda e, i, f, t=t: e.tensor_scalar(xn[:, t, :], x[:, t, :], mv[:, t, 0:1], rs[:, t, 1:2], ALU.subtract, ALU.mult),
             ["rstd", ("tn3", 1)], f"xn{t}" if t < 3 else "sub")
    for t in range(TPB):
        s.op("v", lambda e, i, f, t=t: e.bn_stats(stat2[:, t, :], xn[:, t, :]), [f"xn{t}" if t < 3 else "sub"], f"st2{t}", alone=True)
    for t in range(TPB):
        s.op("v", lambda e, i, f, t=t: e.bn_aggr(mv2[:, t, :], stat2[:, t, :]), [f"st2{t}"], f"ag2{t}", alone=True)
    s.op("s", lambda e, i, f: e.activation(rs[:, :, 2:3], mv2[:, :, 1:2], ACT.Sqrt, scale=DIM / (DIM - 1.0)), [f"ag2{TPB-1}"], "sd2")
    s.op("s", lambda e, i, f: e.activation(rs[:, :, 2:3], rs[:, :, 2:3], ACT.Sqrt, bias=g.eps5[:, 0:1]), ["sd2"], "rsd2")
    s.op("v", lambda e, i, f: e.reciprocal(rs[:, :, 3:4], rs[:, :, 2:3]), ["rsd2"], "rstd2")
    for t in range(TPB):
        s.op("v", lambda e, i, f, t=t: e.tensor_scalar(xf[:, t, :], xn[:, t, :], mv2[:, t, 0:1], rs[:, t, 3:4], ALU.subtract, ALU.mult),
             ["rstd2", ("tf3", 1), ("store_xf", 1)], f"xf{t}")
    s.dma("y", lambda e, i, f: e.dma_start(rows(D["xf"], i), xf[:]), [f"xf{TPB-1}"], "store_xf")
    for c in range(KC):
        for t in range(TPB):
            s.op("t", lambda e, i, f, c=c, t=t: e.transpose(bk[c][:, t * P:(t + 1) * P], xn[:, t, c * P:(c + 1) * P], g.ident[:]),
                 ["sub", (f"exn{c}", 1)], f"tn{c * TPB + t}" if c == 0 else f"tn{c*TPB+t}")
    for c in range(KC):
        s.op("s", lambda e, i, f, c=c: e.activation(xnT[:, c, :], bk[c][:], ACT.Copy), [f"tn{c * TPB + 3}", ("store_xnT", 1), ("ab3", 1)], f"exn{c}")
    for c in range(KC):
        for t in range(TPB):
            s.op("t", lambda e, i, f, c=c, t=t: e.transpose(bk[2 + c][:, t * P:(t + 1) * P], xf[:, t, c * P:(c + 1) * P], g.ident[:]),
                 [f"xf{TPB-1}", (f"exf{c}", 1)], f"tf{c * TPB + t}")
    for c in range(KC):
        s.op("v", lambda e, i, f, c=c: e.tensor_copy(xfT[:, c, :], bk[2 + c][:]), [f"tf{c * TPB + 3}", ("store_xfT", 1)], f"exf{c}")
    s.dma("y", lambda e, i, f: e.dma_start(cols(D["xnT"], i), xnT[:]), ["exn1"], "store_xnT")
    s.dma("y", lambda e, i, f: e.dma_start(cols(D["xfT"], i), xfT[:]), ["exf1"], "store_xfT")
    for t in range(TPB):
        for c in range(KC):
            s.op("t", lambda e, i, f, c=c, t=t: e.matmul(bk[4][:, t * 16:(t + 1) * 16], xnT[:, c, t * P:(t + 1) * P], g.wab[:, c, :], start=(c == 0), stop=(c == KC - 1)),
                 ["exn1", ("eab", 1)], f"ab{t}" if c else None)
    s.op("v", lambda e, i, f: e.tensor_copy(ab[:], bk[4][:, 0:64].rearrange("p (t n) -> p t n", n=16)), ["ab3", ("store_ab", 1)], "eab")
    s.dma("y", lambda e, i, f: e.dma_start(D["ab"][ds(i, 1)].rearrange("a p n -> p (a n)"), ab[:].rearrange("p t n -> p (t n)")), ["eab"], "store_ab")


def decays(g):
    nc, pg, sb, D = g.nc, g.pg, g.scoped(), g.dram
    pg.group()
    s = pg.stage("decays", 1)
    N = N_BATCH * TPB * HEADS
    ab = sb("ab_all", [P, N_BATCH, TPB, 2, HEADS])
    z, m, az, sp, gg = (sb(n, [P, N]) for n in ("z", "m", "az", "sp", "gg"))
    out = sb("kinds", [P, 2, KINDS, TILES, 4])
    bk = g.bank
    a_in = ab[:, :, :, 0, :].rearrange("p b t h -> p (b t) h")
    b_in = ab[:, :, :, 1, :].rearrange("p b t h -> p (b t) h")
    v3 = lambda t: t[:].rearrange("p (n h) -> p n h", h=HEADS)
    bc = lambda t: t[:, None, :].broadcast_to((P, N // HEADS, HEADS))
    s.dma("y", lambda e, i, f: e.dma_start(ab[:].rearrange("p b t k h -> p b (t k h)"), D["ab"].rearrange("b p n -> p b n")), [], "ab")
    s.op("v", lambda e, i, f: e.tensor_tensor(v3(z), a_in, bc(g.dtb), ALU.add), ["ab"], "z")
    s.op("v", lambda e, i, f: e.tensor_scalar(m[:], z[:], -1.0, None, ALU.mult), ["z"], "m0")
    s.op("v", lambda e, i, f: e.tensor_tensor(az[:], z[:], m[:], ALU.min), ["m0"], "az")
    s.op("s", lambda e, i, f: e.activation(az[:], az[:], ACT.Exp), ["az"], "e1")
    s.op("s", lambda e, i, f: e.activation(sp[:], az[:], ACT.Ln, bias=g.one[:, 0:1]), ["e1"], "l1")
    s.op("v", lambda e, i, f: e.scalar_tensor_tensor(sp[:], z[:], 0.0, sp[:], ALU.max, ALU.add), ["l1"], "sp")
    s.op("s", lambda e, i, f: e.activation(g.ea[:], g.alog[:], ACT.Exp), [], "ea")
    s.op("v", lambda e, i, f: e.tensor_tensor(v3(gg), v3(sp), bc(g.ea), ALU.mult), ["sp", "ea"], "g0")
    s.op("v", lambda e, i, f: e.tensor_scalar(gg[:], gg[:], -1.0, None, ALU.mult), ["g0"], "g")
    s.op("t", lambda e, i, f: e.matmul(bk[0][:, 0:N], g.upper[:], gg[:], start=True, stop=True), ["g"], None)
    s.op("t", lambda e, i, f: e.matmul(bk[1][:, 0:N], g.ones[:], gg[:], start=True, stop=True), ["g"], "cum")
    def kind(k):
        return out[:, :, k]
    def src(t):
        return t.rearrange("p (n q h) -> p q n h", q=2, h=4)
    s.op("s", lambda e, i, f: e.activation(m[:], b_in, ACT.Sigmoid) if 0 else e.activation(m[:].rearrange("p (n h) -> p n h", h=HEADS), b_in, ACT.Sigmoid), ["az"], "sig")
    s.op("v", lambda e, i, f: e.tensor_copy(az[:], bk[0][:, 0:N]), ["cum", "l1"], "G")
    s.op("v", lambda e, i, f: e.tensor_copy(z[:], bk[1][:, 0:N]), ["cum", "sp"], "GC")
    s.op("v", lambda e, i, f: e.tensor_tensor(sp[:], z[:], az[:], ALU.subtract), ["G", "g0", "GC"], "GC-G")
    for q in range(2):
        v = lambda k, q=q: kind(k)[:, q]
        w = lambda t, q=q: src(t)[:, q]
        s.op("v", lambda e, i, f, v=v, w=w: e.tensor_copy(v(0), w(gg[:])), ["g"])
        s.op("v", lambda e, i, f, v=v, w=w: e.tensor_scalar(v(1), w(az[:]), -1.0, None, ALU.mult), ["G"])
        s.op("v", lambda e, i, f, v=v, w=w: e.tensor_scalar(v(2), w(m[:]), -2.0, None, ALU.mult), ["sig"])
        s.op("v", lambda e, i, f, v=v, w=w: e.tensor_scalar(v(3), w(m[:]), 2.0, None, ALU.mult), ["sig"], f"k3{q}")
        s.op("s", lambda e, i, f, v=v, w=w: e.activation(v(4), w(az[:]), ACT.Exp), ["G"])
        s.op("s", lambda e, i, f, v=v, w=w: e.activation(v(5), w(sp[:]), ACT.Exp), ["GC-G"])
        s.op("s", lambda e, i, f, v=v, w=w: e.activation(v(6), w(z[:]), ACT.Exp), ["GC"], f"k6{q}")
        s.dma("y", lambda e, i, f, q=q: e.dma_start(D["kinds"][q].rearrange("p k t h -> p (k t h)"), out[:, q].rearrange("p k t h -> p (k t h)")), [f"k3{q}", f"k6{q}"], f"store{q}")


def delta(g):
    nc, pg, sb, D = g.nc, g.pg, g.scoped(), g.dram
    pg.group(times=2)
    bk = g.bank
    H = 4
    w = sb("w_qkvg", [P, KC, 1536])
    cw = sb("conv_w", [P, 40])
    xT = sb("d_xT", [P, KC, SEQ])
    kd = sb("d_kinds", [P, KINDS, TPB, H])
    kq = sb("d_kq", [P, H, 2, SEQ])
    vT = sb("d_vT", [P, 2, SEQ])
    sgw = sb("d_gate", [P, TPB, 256])
    sq = [sb(f"d_sq{j}", [P, SEQ]) for j in range(3)]
    nr = [sb(f"d_nr{j}", [P, SEQ]) for j in range(3)]
    kdec = sb("d_kdec", [P, TPB, H, P])
    v = sb("d_v", [P, TPB, H, 64])
    E, M, X, Pm, W, Dm = ([sb(f"d_{n}{j}", [P, H, P]) for j in range(2)] for n in ("E", "M", "X", "P", "W", "D"))
    Dm = [sb(f"d_DD{j}", [P, H, P]) for j in range(4)]
    Pf = [sb(f"d_Pf{j}", [P, H, P]) for j in range(4)]
    S = sb("d_S", [P, H, 64])
    R, U, T1 = (sb(n, [P, H, 64]) for n in ("d_R", "d_U", "d_T1"))
    o = sb("d_o", [P, TPB, H, 64])
    o2 = sb("d_o2", [P, TPB, H, 64])
    ss = sb("d_ss", [P, TPB * H])

    s = pg.stage("delta weights", 1)
    s.dma("y", lambda e, i, f: e.dma_start(w[:].rearrange("p c n -> p (c n)"), D["w_qkvg"][ds(f, 1)].rearrange("a p c n -> p (a c n)")), [], "w")
    s.dma("y", lambda e, i, f: e.dma_start(cw[:], D["conv_w"][ds(f, 1)].rearrange("a p n -> p (a n)")), [], "cw")

    s = pg.stage("delta", N_BATCH)
    sl = Slots(s)
    s.dma("y", lambda e, i, f: e.dma_start(xT[:], cols(D["xnT"], i)), [("gate3", 1)], "xT")
    s.dma("y", lambda e, i, f: e.dma_start(kd[:].rearrange("p k t h -> p k (t h)"), D["kinds"][ds(f, 1), :, :, ds(i * TPB, TPB)].rearrange("a p k t h -> p (a k) (t h)")),
          [("sdec3", 1), ("org3", 1), ("E33", 1)], "kd")

    tiles = [("v", 0), ("v", 1)] + [(n, h) for h in range(H) for n in "kq"]
    def dest(n, h):
        return vT[:, h, :] if n == "v" else kq[:, h, 0 if n == "k" else 1, :]
    col = {"q": 0, "k": 512, "v": 1024}
    ccol = {"q": 0, "k": 16, "v": 32}
    for j, (n, h) in enumerate(tiles):
        b, id_ = j % 4, f"{n}{h}"
        for c in range(KC):
            s.op("t", lambda e, i, f, b=b, n=n, h=h, c=c: e.matmul(bk[b][:], w[:, c, col[n] + h * P:col[n] + (h + 1) * P], xT[:, c, :], start=(c == 0), stop=(c == 1)),
                 ["xT", sl.free(f"bank{b}")], f"proj_{id_}" if c else None)
        d, k0 = dest(n, h), ccol[n] + 4 * h
        s.op("s", lambda e, i, f, b=b, d=d, k0=k0: e.activation(d, bk[b][:], ACT.Copy, scale=cw[:, k0 + 3:k0 + 4]),
             [f"proj_{id_}", (f"done_{n}", 1)], f"c0_{id_}")
        for a in (1, 2, 3):
            s.op("v", lambda e, i, f, b=b, d=d, k0=k0, a=a: e.scalar_tensor_tensor(d[:, a:], bk[b][:, 0:SEQ - a], cw[:, k0 + 3 - a:k0 + 4 - a], d[:, a:], ALU.mult, ALU.add),
                 [f"c{a-1}_{id_}"], f"c{a}_{id_}")
        sl.read(f"bank{b}", f"c3_{id_}")
        s.op("s", lambda e, i, f, d=d: e.activation(d, d, ACT.Silu), [f"c3_{id_}"], f"silu_{id_}")
    for t in range(TPB):
        b = 4 + t // 2
        for c in range(KC):
            s.op("t", lambda e, i, f, b=b, t=t, c=c: e.matmul(bk[b][:, (t % 2) * 256:(t % 2) * 256 + 256], xT[:, c, t * P:(t + 1) * P], w[:, c, 1280:1536], start=(c == 0), stop=(c == 1)),
                 ["xT", sl.free(f"bank{b}")], f"gate{t}" if c else None)
    for t in (0, 2):
        b = 4 + t // 2
        s.op("s", lambda e, i, f, b=b, t=t: e.activation(sgw[:, t:t + 2, :], bk[b][:].rearrange("p (t n) -> p t n", t=2), ACT.Silu), [f"gate{t+1}", ("og", 1)], f"sg{t}")
        sl.read(f"bank{b}", f"sg{t}")
    s.op("g", lambda e, i, f: e.tensor_tensor(sgw[:].rearrange("p t (h v) -> p (t h) v", v=64), sgw[:].rearrange("p t (h v) -> p (t h) v", v=64), g.onw[:, None, :].broadcast_to((P, 16, 64)), ALU.mult), ["sg2", "sg0"], "sgw")
    for j, (n, h) in enumerate(tiles[2:]):
        id_, b, d, k = f"{n}{h}", 6 + j % 2, dest(n, h), j % 3
        s.op("g", lambda e, i, f, d=d, k=k: e.tensor_tensor(sq[k][:], d, d, ALU.mult), [f"silu_{id_}", sl.free(f"sq{k}")], f"sq_{id_}")
        s.op("t", lambda e, i, f, b=b, k=k: e.matmul(bk[b][:], g.ones[:], sq[k][:], start=True, stop=True), [f"sq_{id_}", sl.free(f"bank{b}")], f"ss_{id_}")
        sl.read(f"sq{k}", f"ss_{id_}")
        s.op("s", lambda e, i, f, b=b, k=k: e.activation(nr[k][:], bk[b][:], ACT.Sqrt), [f"ss_{id_}", sl.free(f"nr{k}")], f"nrm_{id_}")
        sl.read(f"bank{b}", f"nrm_{id_}")
        s.op("v", lambda e, i, f, k=k: e.reciprocal(nr[k][:], nr[k][:]), [f"nrm_{id_}"], f"rn_{id_}")
        s.op("v", lambda e, i, f, d=d, k=k: e.scalar_tensor_tensor(d, nr[k][:], 1e6, d, ALU.min, ALU.mult), [f"rn_{id_}"], f"n_{id_}")
        sl.read(f"nr{k}", f"n_{id_}")
    for t in range(TPB):
        b = t % 4
        for h in range(2):
            s.op("t", lambda e, i, f, b=b, t=t, h=h: e.transpose(bk[b][:, h * P:(h + 1) * P], vT[:, h, t * P:(t + 1) * P], g.ident[:]),
                 [f"silu_v{h}", sl.free(f"bank{b}")], f"tv{t}{h}")
        s.op("v", lambda e, i, f, b=b, t=t: e.tensor_copy(v[:, t], bk[b][:, 0:256].rearrange("p (h n) -> p h n", h=H)), [f"tv{t}1", ("R3", 1)], f"v{t}")
        sl.read(f"bank{b}", f"v{t}")
    s.producers["done_v"] = s.producers["tv31"]
    for t in range(TPB):
        b = t % 4
        for h in range(H):
            s.op("t", lambda e, i, f, b=b, t=t, h=h: e.transpose(bk[b][:, h * P:(h + 1) * P], kq[:, h, 0, t * P:(t + 1) * P], g.ident[:]),
                 [f"n_k{h}", sl.free(f"bank{b}")], f"tk{t}{h}")
        s.op("v", lambda e, i, f, b=b, t=t: e.tensor_tensor(kdec[:, t], bk[b][:].rearrange("p (h n) -> p h n", h=H), kd[:, 5, t, :, None].broadcast_to((P, H, P)), ALU.mult),
             [f"tk{t}3", "kd", ("dS3", 1)], f"kdec{t}")
        sl.read(f"bank{b}", f"kdec{t}")

    def setup(t, p):
        B = [p * 4 + j for j in range(3)]
        s.op("t", lambda e, i, f: e.matmul(bk[B[0]][:].rearrange("p (h n) -> p h n", h=H), g.identb[:], g.negm[:, None, :].broadcast_to((P, H, P)), start=True, stop=False, skip_group_check=True),
             [sl.free(f"bank{B[0]}")])
        for h in range(H):
            s.op("t", lambda e, i, f, h=h: e.matmul(bk[B[0]][:, h * P:(h + 1) * P], kd[:, 0, t, h:h + 1].broadcast_to((P, P)), g.upper[:], start=False, stop=True, skip_group_check=True),
                 ["kd"], f"G{t}{h}")
        for h in range(H):
            s.op("s", lambda e, i, f, h=h: e.activation(E[p][:, h, :], bk[B[0]][:, h * P:(h + 1) * P], ACT.Exp, bias=kd[:, 1, t, h:h + 1]),
                 [f"G{t}3", sl.free(f"E{p}")], f"E{t}{h}")
        sl.read(f"bank{B[0]}", f"E{t}3")
        for h in range(H):
            b = B[1] + h // 2
            s.op("t", lambda e, i, f, h=h, b=b: e.matmul(bk[b][:, (h % 2) * 256:(h % 2) * 256 + 256].rearrange("p (a n) -> p a n", a=2), kq[:, h, 0, t * P:(t + 1) * P], kq[:, h, :, t * P:(t + 1) * P], start=True, stop=True),
                 [f"n_k{h}", f"n_q{h}", sl.free(f"bank{b}")], f"KQ{t}{h}")
        for h in range(H):
            b = B[1] + h // 2
            c0 = (h % 2) * 256
            s.op("v", lambda e, i, f, h=h, b=b, c0=c0: e.scalar_tensor_tensor(M[p][:, h, :], bk[b][:, c0:c0 + P], kd[:, 2, t, h:h + 1], E[p][:, h, :], ALU.mult, ALU.mult),
                 [f"KQ{t}{h | 1}", f"E{t}{h}", sl.free(f"M{p}")], f"M{t}{h}")
        for q in range(2):
            s.op("v", lambda e, i, f, q=q: e.tensor_tensor(Dm[t][:, 2 * q:2 * q + 2, :], bk[B[1] + q][:].rearrange("p (h a n) -> p h a n", h=2, a=2)[:, :, 1, :], E[p][:, 2 * q:2 * q + 2, :], ALU.mult),
                 [f"KQ{t}{2*q+1}", f"E{t}3", (f"O1{t}", 1)], f"D{t}{q}")
            sl.read(f"bank{B[1]+q}", f"D{t}{q}")
        sl.read(f"E{p}", f"D{t}1")
        s.op("g", lambda e, i, f: e.tensor_copy(X[p][:], g.ident[:, None, :].broadcast_to((P, H, P))), [sl.free(f"X{p}")], f"X{t}init", alone=True)
        s.op("g", lambda e, i, f: e.tensor_copy(Pf[t][:], g.ident[:, None, :].broadcast_to((P, H, P))), [(f"Uh{t}", 1)], f"P{t}init", alone=True)
        s.op("v", lambda e, i, f: e.copy_predicated(Pf[t][:], g.mask[:, 0, 0, None, :].broadcast_to((P, H, P)), M[p][:]), [f"P{t}init", f"M{t}3"], f"P{t}0", alone=True)
        for h in range(H):
            s.op("t", lambda e, i, f, h=h: e.transpose(bk[B[0]][:, h * P:(h + 1) * P], M[p][:, h, :], g.ident[:]), [f"M{t}3", sl.free(f"bank{B[0]}")], f"MT{t}{h}")
        s.op("v", lambda e, i, f: e.copy_predicated(X[p][:], g.mask[:, 0, 1, None, :].broadcast_to((P, H, P)), bk[B[0]][:].rearrange("p (h n) -> p h n", h=H)), [f"X{t}init", f"MT{t}3"], f"X{t}0", alone=True)
        sl.read(f"bank{B[0]}", f"X{t}0")

    def level(t, p, l):
        B = [p * 4 + j for j in range(3)]
        last = l == 6
        for h in range(H):
            s.op("t", lambda e, i, f, h=h: e.matmul(bk[B[0]][:, h * P:(h + 1) * P], M[p][:, h, :], X[p][:, h, :], start=True, stop=True),
                 [f"X{t}{l-1}", sl.free(f"bank{B[0]}")], f"W{t}{l}{h}")
        s.op("s", lambda e, i, f: e.activation(W[p][:], bk[B[0]][:].rearrange("p (h n) -> p h n", h=H), ACT.Copy), [f"W{t}{l}3", sl.free(f"W{p}")], f"We{t}{l}")
        sl.read(f"bank{B[0]}", f"We{t}{l}")
        if last:
            sl.read(f"M{p}", f"W{t}{l}3")
            sl.read(f"X{p}", f"W{t}{l}3")
        if not last:
            for h in range(H):
                s.op("t", lambda e, i, f, h=h: e.matmul(bk[B[1]][:, h * P:(h + 1) * P], Pf[t][:, h, :], W[p][:, h, :], start=True, stop=True),
                     [f"We{t}{l}", f"P{t}{l-1}", sl.free(f"bank{B[1]}")], f"XW{t}{l}{h}")
            s.op("v", lambda e, i, f: e.copy_predicated(X[p][:], g.mask[:, l, 1, None, :].broadcast_to((P, H, P)), bk[B[1]][:].rearrange("p (h n) -> p h n", h=H)), [f"XW{t}{l}3", f"W{t}{l}3"], f"X{t}{l}", alone=True)
            sl.read(f"bank{B[1]}", f"X{t}{l}")
        for h in range(H):
            s.op("t", lambda e, i, f, h=h: e.matmul(bk[B[2]][:, h * P:(h + 1) * P], W[p][:, h, :], Pf[t][:, h, :], start=True, stop=True),
                 [f"We{t}{l}", f"P{t}{l-1}", sl.free(f"bank{B[2]}")], f"WP{t}{l}{h}")
        s.op("v", lambda e, i, f: e.copy_predicated(Pf[t][:], g.mask[:, l, 0, None, :].broadcast_to((P, H, P)), bk[B[2]][:].rearrange("p (h n) -> p h n", h=H)), [f"WP{t}{l}3"], f"P{t}{l}", alone=True)
        sl.read(f"bank{B[2]}", f"P{t}{l}")
        sl.read(f"W{p}", f"WP{t}{l}3")

    def state(t):
        first = t == 0
        bR, bO = 3, 7
        hb = lambda k: kd[:, k, t, :, None].broadcast_to((P, H, 64))
        ps = lambda b, o: bk[b][:, o:o + 256].rearrange("p (h n) -> p h n", h=H)
        if first:
            s.op("g", lambda e, i, f: e.memset(S[:], 0.0), [("S3", 1)], "Sinit", alone=True)
        prev = "Sinit" if first else f"S{t-1}"
        for h in range(H):
            s.op("t", lambda e, i, f, h=h: e.matmul(bk[bR][:, h * 64:h * 64 + 64], kq[:, h, 0, t * P:(t + 1) * P], S[:, h, :], start=True, stop=True),
                 [prev, f"n_k{h}", sl.free("bank3")], f"KS{t}{h}")
        for h in range(H):
            s.op("t", lambda e, i, f, h=h: e.matmul(bk[bO][:, h * 64:h * 64 + 64], kq[:, h, 1, t * P:(t + 1) * P], S[:, h, :], start=True, stop=True),
                 [prev, f"n_q{h}", sl.free("bank7")], f"QS{t}{h}")
        s.op("v", lambda e, i, f: e.tensor_tensor(R[:], ps(bR, 0), hb(4), ALU.mult), [f"KS{t}3", "kd", (f"Uh{(t-1)%4}", 1 if first else 0)], f"gks{t}")
        s.op("v", lambda e, i, f: e.tensor_tensor(T1[:], ps(bO, 0), hb(4), ALU.mult), [f"QS{t}3"], f"orr{t}")
        s.op("v", lambda e, i, f: e.tensor_tensor(R[:], v[:, t], R[:], ALU.subtract), [f"gks{t}", f"v{t}"], f"R{t}")
        for h in range(H):
            s.op("t", lambda e, i, f, h=h: e.matmul(bk[bR][:, 256 + h * 64:256 + h * 64 + 64], Pf[t][:, h, :], R[:, h, :], start=True, stop=True),
                 [f"R{t}", f"P{t}6"], f"Uh{t}{h}")
        s.producers[f"Uh{t}"] = s.producers[f"Uh{t}3"]
        s.op("v", lambda e, i, f: e.tensor_tensor(U[:], ps(bR, 256), hb(3), ALU.mult), [f"Uh{t}3", (f"dS{(t-1)%4}", 1 if first else 0)], f"U{t}")
        for h in range(H):
            s.op("t", lambda e, i, f, h=h: e.matmul(bk[bR][:, h * 64:h * 64 + 64], kdec[:, t, h, :], U[:, h, :], start=True, stop=True),
                 [f"U{t}", f"kdec{t}"], f"dS{t}{h}")
        s.producers[f"dS{t}"] = s.producers[f"dS{t}3"]
        for h in range(H):
            s.op("t", lambda e, i, f, h=h: e.matmul(bk[bO][:, 256 + h * 64:256 + h * 64 + 64], Dm[t][:, h, :], U[:, h, :], start=True, stop=True),
                 [f"U{t}", f"D{t}1", f"orr{t}"], f"O1{t}{h}")
        s.producers[f"O1{t}"] = s.producers[f"O1{t}3"]
        s.op("v", lambda e, i, f: e.tensor_tensor(S[:], S[:], hb(6), ALU.mult), [prev, f"QS{t}3"], f"sdec{t}")
        s.op("v", lambda e, i, f: e.tensor_tensor(S[:], ps(bR, 0), S[:], ALU.add), [f"dS{t}3", f"sdec{t}"], f"S{t}")
        sl.read("bank3", f"S{t}")
        s.op("v", lambda e, i, f: e.tensor_tensor(o[:, t], ps(bO, 256), T1[:], ALU.add), [f"O1{t}3", f"orr{t}", ("og", 1)], f"orh{t}")
        s.producers[f"org{t}"] = s.producers[f"orh{t}"]
        sl.read("bank7", f"orh{t}")

    for pair in range(2):
        for p in range(2):
            setup(2 * pair + p, p)
        for l in range(1, 7):
            for p in range(2):
                level(2 * pair + p, p, l)
        for p in range(2):
            state(2 * pair + p)
    for n in "kq":
        s.producers[f"done_{n}"] = s.producers["QS33"]
    flat = lambda t: t[:].rearrange("p t h v -> p (t h) v")
    s.op("g", lambda e, i, f: e.tensor_tensor(o2[:], o[:], o[:], ALU.mult), ["orh3", ("store_og", 1)], "osq")
    s.op("v", lambda e, i, f: e.tensor_reduce(ss[:], flat(o2), AX.X, ALU.add), ["osq"], "oss")
    s.op("s", lambda e, i, f: e.activation(ss[:], ss[:], ACT.Sqrt, bias=g.eps5[:, 0:1], scale=1.0 / 64), ["oss"], "orms")
    s.op("v", lambda e, i, f: e.reciprocal(ss[:], ss[:]), ["orms"], "orrms")
    s.op("v", lambda e, i, f: e.tensor_tensor(flat(o2), flat(o), ss[:, :, None].broadcast_to((P, 16, 64)), ALU.mult), ["orrms"], "on")
    s.op("g", lambda e, i, f: e.tensor_tensor(flat(o2), flat(o2), sgw[:].rearrange("p t (h v) -> p (t h) v", v=64), ALU.mult), ["on", "sgw"], "og")
    s.dma("y", lambda e, i, f: e.dma_start(rows(D["og"], i)[:, :, ds(f * 256, 256)], o2[:].rearrange("p t h v -> p t (h v)")), ["og"], "store_og")
    sl.close()

LEAVES, NODES, LW, GROUPS, GL = 256, 255, 16, 32, 8
SEGS = TILES + GROUPS - 1
ROW = DIM + 1


def fff(g, tag, times, first, rows_in, cols_in, act, out):
    nc, pg, sb, D = g.nc, g.pg, g.scoped(), g.dram
    bk = g.bank
    pg.group(times)
    nw = sb(tag + "nw", [P, KC, LEAVES])
    nb = sb(tag + "nb", [P, LEAVES])
    xT = sb(tag + "xT", [P, KC, SEQ])
    bits, N, Pr = (sb(tag + n, [P, TPB, LEAVES]) for n in ("bits", "N", "Pr"))
    leaf = sb(tag + "leaf", [P, TPB])
    ohb = sb(tag + "ohb", [P, TPB, GROUPS], BF16)

    s = pg.stage("tree parameters", 1)
    s.dma("y", lambda e, i, f: e.dma_start(nw[:].rearrange("p c n -> p (c n)"), D["nwT"][ds(first + f, 1)].rearrange("a p c n -> p (a c n)")), [], "nw")
    s.dma("y", lambda e, i, f: e.dma_start(nb[:], D["nb"][ds(first + f, 1)].broadcast_to((P, LEAVES))), [], "nb")
    s.op("v", lambda e, i, f: e.memset(N[:], 1.0))

    s = pg.stage("routing", N_BATCH)
    s.dma("y", lambda e, i, f: e.dma_start(xT[:], cols(D[cols_in], i)), [("lg3", 1)], "xT")
    for t in range(TPB):
        for c in range(KC):
            s.op("t", lambda e, i, f, c=c, t=t: e.matmul(bk[t // 2][:, (t % 2) * 256:(t % 2) * 256 + 256], xT[:, c, t * P:(t + 1) * P], nw[:, c, :], start=(c == 0), stop=(c == 1)),
                 ["xT", (f"bits{t//2}", 1)], f"lg{t}" if c else None)
    for q in range(2):
        s.op("v", lambda e, i, f, q=q: e.scalar_tensor_tensor(bits[:, 2 * q:2 * q + 2, :], bk[q][:].rearrange("p (t n) -> p t n", t=2), -1.0, nb[:, None, :].broadcast_to((P, 2, LEAVES)), ALU.mult, ALU.is_lt),
             [f"lg{2*q+1}"], f"bits{q}")
    for l in range(8):
        a, b = (1 << l) - 1, (2 << l) - 1
        s.op("v", lambda e, i, f, a=a, b=b: e.tensor_tensor(Pr[:, :, a:b], N[:, :, a:b], bits[:, :, a:b], ALU.mult), ["bits0", "bits1"] + ([f"NL{l-1}", f"NR{l-1}"] if l else []), f"Pr{l}")
        if l < 7:
            kids = N[:, :, b:2 * b + 1].rearrange("p t (j k) -> p t j k", k=2)
            s.op("v", lambda e, i, f, a=a, b=b, kids=kids: e.tensor_tensor(kids[:, :, :, 0], N[:, :, a:b], Pr[:, :, a:b], ALU.subtract), [f"Pr{l}"], f"NL{l}")
            s.op("v", lambda e, i, f, a=a, b=b, kids=kids: e.tensor_copy(kids[:, :, :, 1], Pr[:, :, a:b]), [f"Pr{l}"], f"NR{l}", alone=True)
    s.op("v", lambda e, i, f: e.tensor_copy(ohb[:], N[:, :, 31:63]), ["NL4", "NR4", ("st_oh", 1)], "ohb", alone=True)
    s.op("v", lambda e, i, f: e.tensor_tensor(bits[:, :, 0:NODES], Pr[:, :, 0:NODES], g.lvw[:, None, 0:NODES].broadcast_to((P, TPB, NODES)), ALU.mult), ["Pr7"], "lw")
    s.op("v", lambda e, i, f: e.tensor_reduce(leaf[:], bits[:, :, 0:NODES], AX.X, ALU.add), ["lw", ("st_leaf", 1)], "leaf")
    s.dma("y", lambda e, i, f: e.dma_start(D["leaf"][:, ds(i * TPB, TPB)], leaf[:]), ["leaf"], "st_leaf")
    s.dma("y", lambda e, i, f: e.dma_start(D["ohb"][:, ds(i * TPB * GROUPS, TPB * GROUPS)], ohb[:].rearrange("p t n -> p (t n)")), ["ohb"], "st_oh")

    sb = g.scoped()
    pos = sb(tag + "pos", [P, TILES])
    posi = sb(tag + "posi", [P, TILES], I32)
    seg = sb(tag + "seg", [P, 3, 64], I32)
    xsT = sb(tag + "xsT", [P, KC, TOKENS])
    lrow = sb(tag + "lrow", [P, TOKENS])
    xr = sb(tag + "xr", [P, TILES, ROW])
    acc = sb(tag + "acc", [P, TILES * DIM])
    TG = TILES * GROUPS
    def part(n, w=TG):
        o = part.at
        part.at += w
        return acc[:, o:o + w]
    part.at = 0
    cnt, A0, A1, c2 = (part(n) for n in range(4))
    cmp = part(4, 2048)
    tot, st, t0, t1, ra, rg = (part(5, 64)[:, 0:32] for _ in range(6))
    sgf = part(6, 128)
    oh = sb(tag + "oh", [P, TG], BF16)
    lf = sb(tag + "lf", [P, TILES])
    tg = lambda a: a.rearrange("p (t n) -> p t n", n=GROUPS)
    s = pg.stage("sort", 1)
    s.dma("y", lambda e, i, f: e.dma_start(oh[:], D["ohb"]), [], "oh")
    s.dma("y", lambda e, i, f: e.dma_start(lf[:], D["leaf"]), [], "lf")
    s.dma("y", lambda e, i, f: e.dma_start(xr[:, :, 0:DIM], D[rows_in].rearrange("(t p) d -> p t d", p=P)), [], "xr")
    for q in range(2):
        s.op("t", lambda e, i, f, q=q: e.matmul(bk[q][:], g.onesb[:], oh[:, q * 512:(q + 1) * 512], start=True, stop=True), ["oh"], f"cnt{q}")
        s.op("t", lambda e, i, f, q=q: e.matmul(bk[2 + q][:], g.upperb[:], oh[:, q * 512:(q + 1) * 512], start=True, stop=True), ["oh"], f"cum{q}")
    for q in range(2):
        s.op("v", lambda e, i, f, q=q: e.tensor_copy(cnt[:, q * 512:(q + 1) * 512], bk[q][:]), [f"cnt{q}"], f"cn{q}")
    cur, last = cnt, ["cn0", "cn1"]
    for k in range(5):
        d, new = GROUPS << k, (A0, A1)[k % 2]
        s.op("v", lambda e, i, f, d=d, cur=cur, new=new: e.tensor_tensor(new[:, d:], cur[:, d:], cur[:, :TG - d], ALU.add), last, f"pa{k}")
        s.op("v", lambda e, i, f, d=d, cur=cur, new=new: e.tensor_copy(new[:, :d], cur[:, :d]), last, f"pb{k}")
        cur, last = new, [f"pa{k}", f"pb{k}"]
    pref = cur
    s.op("v", lambda e, i, f: e.tensor_copy(tot, pref[:, TG - GROUPS:]), last, "tot")
    cur, lastg = tot, ["tot"]
    for k in range(5):
        d, new = 1 << k, (t0, t1)[k % 2]
        s.op("v", lambda e, i, f, d=d, cur=cur, new=new: e.tensor_tensor(new[:, d:], cur[:, d:], cur[:, :GROUPS - d], ALU.add), lastg, f"ga{k}")
        s.op("v", lambda e, i, f, d=d, cur=cur, new=new: e.tensor_copy(new[:, :d], cur[:, :d]), lastg, f"gb{k}")
        cur, lastg = new, [f"ga{k}", f"gb{k}"]
    s.op("v", lambda e, i, f, cur=cur: e.tensor_tensor(st, cur, tot, ALU.subtract), lastg, "start")
    s.op("v", lambda e, i, f: e.tensor_tensor(c2, pref, cnt, ALU.subtract), last, "q0")
    s.op("v", lambda e, i, f: e.tensor_tensor(tg(c2), tg(c2), st[:, None, :].broadcast_to((P, TILES, GROUPS)), ALU.add), ["q0", "start"], "q1")
    for q in range(2):
        s.op("v", lambda e, i, f, q=q: e.tensor_tensor(c2[:, q * 512:(q + 1) * 512], bk[2 + q][:], c2[:, q * 512:(q + 1) * 512], ALU.add), ["q1", f"cum{q}"], f"q2{q}")
    s.op("v", lambda e, i, f: e.tensor_tensor(c2, c2, oh[:], ALU.mult), ["q20", "q21"], "q3")
    s.op("v", lambda e, i, f: e.tensor_reduce(pos[:], tg(c2), AX.X, ALU.add), ["q3"], "pos")
    s.op("v", lambda e, i, f: e.tensor_scalar(posi[:], pos[:], -1.0, None, ALU.add), ["pos"], "posi")
    s.op("v", lambda e, i, f: e.tensor_copy(xr[:, :, DIM:ROW], lf[:, :, None]), ["xr", "lf"], "xrl")
    for t in range(TILES):
        s.dma("g", lambda e, i, f, t=t: e.indirect_dma_start(D["xs"], bass.IndirectOffsetOnAxis(posi[:, t:t + 1].bitcast(U32), 0), xr[:, t, :], None), ["posi", "xrl"], f"sc{t}")
    c3 = lambda n, a, b: cmp[:, 0:a * b].rearrange("p (a b) -> p a b", b=b)
    ir = g.iota
    s.op("v", lambda e, i, f: e.tensor_tensor(c3(0, 32, 32), st[:, None, :].broadcast_to((P, 32, 32)), g.iota128[:, 0:32, None].broadcast_to((P, 32, 32)), ALU.is_lt), ["start"], "m0")
    s.op("v", lambda e, i, f: e.tensor_reduce(ra, c3(0, 32, 32), AX.X, ALU.add), ["m0"], "m1")
    s.op("v", lambda e, i, f: e.tensor_tensor(ra, ra, ir[:, 0:32], ALU.add), ["m1"], "ra")
    s.op("v", lambda e, i, f: e.tensor_tensor(c3(0, 32, 32), g.iota128[:, None, 0:32].broadcast_to((P, 32, 32)), st[:, :, None].broadcast_to((P, 32, 32)), ALU.is_le), ["m1"], "m2")
    s.op("v", lambda e, i, f: e.tensor_reduce(rg, c3(0, 32, 32), AX.X, ALU.add), ["m2"], "m3")
    s.op("v", lambda e, i, f: e.tensor_tensor(rg, rg, ir[:, 0:32], ALU.add), ["m3"], "rg")
    for n, (r, wait) in enumerate(((ra, "ra"), (rg, "rg"))):
        s.op("v", lambda e, i, f, r=r: e.tensor_tensor(c3(0, 63, 32), r[:, None, :].broadcast_to((P, 63, 32)), ir[:, 1:64, None].broadcast_to((P, 63, 32)), ALU.is_le), [wait, "m3"] + (["n1"] if n else []), "n0" if n == 0 else "n2")
        s.op("v", lambda e, i, f, n=n: e.tensor_reduce(sgf[:, n * 64:n * 64 + 63], c3(0, 63, 32), AX.X, ALU.add), ["n0" if n == 0 else "n2"], "n1" if n == 0 else "n3")
    s.op("v", lambda e, i, f: e.tensor_scalar(seg[:, 0, 0:63], sgf[:, 0:63], -1.0, float(P), ALU.add, ALU.mult), ["n1"], "sg0")
    s.op("v", lambda e, i, f: e.tensor_scalar(seg[:, 1, 0:63], sgf[:, 0:63], -1.0, float(DIM), ALU.add, ALU.mult), ["n1"], "sg1")
    s.op("v", lambda e, i, f: e.tensor_scalar(seg[:, 2, 0:63], sgf[:, 64:127], -1.0, None, ALU.add), ["n3"], "sg2")

    xs = sb(tag + "xs", [P, TPB, ROW])
    s = pg.stage("sorted", N_BATCH)
    s.dma("y", lambda e, i, f: e.dma_start(xs[:], rows(D["xs"], i)), [("lr3", 1), ("t13", 1)], "xs")
    for c in range(KC):
        for t in range(TPB):
            s.op("t", lambda e, i, f, c=c, t=t: e.transpose(bk[c][:, t * P:(t + 1) * P], xs[:, t, c * P:(c + 1) * P], g.ident[:]), ["xs", (f"e{c}", 1)], f"t{c}{t}")
    for t in range(TPB):
        s.op("t", lambda e, i, f, t=t: e.matmul(bk[2][:, t * P:(t + 1) * P], xs[:, t, DIM:ROW].broadcast_to((P, P)), g.ident[:], start=True, stop=True), ["xs", ("e2", 1)], f"lr{t}")
    s.op("s", lambda e, i, f: e.activation(xsT[:, 0, ds(i * SEQ, SEQ)], bk[0][:], ACT.Copy), ["t03"], "e0", alone=True)
    s.op("v", lambda e, i, f: e.tensor_copy(xsT[:, 1, ds(i * SEQ, SEQ)], bk[1][:]), ["t13"], "e1", alone=True)
    s.op("s", lambda e, i, f: e.activation(lrow[:, ds(i * SEQ, SEQ)], bk[2][:], ACT.Copy), ["lr3"], "e2", alone=True)

    w1 = [sb(f"{tag}w1_{j}", [P, 258]) for j in range(3)]
    w2 = [sb(f"{tag}w2_{j}", [P, DIM]) for j in range(3)]
    b2 = [sb(f"{tag}b2_{j}", [GL, ROW]) for j in range(3)]
    hT = [sb(f"{tag}hT_{j}", [P, P]) for j in range(3)]
    hm = [sb(f"{tag}hm_{j}", [P, P]) for j in range(3)]
    m8 = [sb(f"{tag}m8_{j}", [GL, P]) for j in range(3)]
    s = pg.stage("clear", 1)
    s.op("g", lambda e, i, f: e.memset(acc[:], 0.0))
    s = pg.stage("segments", SEGS // 3)
    at = {}
    def load(e, i, j, what, key):
        at[key] = e.value_load(seg[0:1, what, ds(i * 3 + j, 1)], min_val=0, max_val=[TOKENS - P, TILES * DIM - DIM, GROUPS - 1][what])
    for j in range(3):
        def group_loads(e, i, f, j=j):
            load(e, i, j, 2, ("y", j))
            k = at["y", j] + (first + f) * GROUPS
            return e.dma_start(w1[j][:], D["w1p"][ds(k, 1)].rearrange("a p n -> p (a n)"))
        s.dma("y", group_loads, [(f"o{j}", 1), (f"hmd{j}", 1), (f"h{j}", 1)], f"w1{j}")
        s.dma("y", lambda e, i, f, j=j: e.dma_start(w2[j][:], D["w2p"][ds((at["y", j] + (first + f) * GROUPS) * P, P), :]), [(f"o{j}", 1)], f"w2{j}")
        s.dma("y", lambda e, i, f, j=j: e.dma_start(b2[j][:], D["b2p"][ds((at["y", j] + (first + f) * GROUPS) * GL, GL), :]), [(f"o{j}", 1), (f"m8d{j}", 1)], f"b2{j}")
    for j in range(3):
        def hidden(e, i, f, j=j):
            load(e, i, j, 0, ("t", j))
            return e.matmul(bk[j][:, 0:P], w1[j][:, 0:P], xsT[:, 0, ds(at["t", j], P)], start=True, stop=False)
        s.op("t", hidden, [f"w1{j}", (f"h{j}", 1)])
        s.op("t", lambda e, i, f, j=j: e.matmul(bk[j][:, 0:P], w1[j][:, P:2 * P], xsT[:, 1, ds(at["t", j], P)], start=False, stop=True), [], f"hp{j}")
        s.op("s", lambda e, i, f, j=j: e.activation(hT[j][:], bk[j][:, 0:P], act, bias=w1[j][:, 256:257]), [f"hp{j}", (f"hmd{j}", 1)], f"h{j}")
    for j in range(3):
        def masks(e, i, f, j=j):
            load(e, i, j, 0, ("v", j))
            return e.scalar_tensor_tensor(hm[j][:], lrow[:, ds(at["v", j], P)], w1[j][:, 257:258], hT[j][:], ALU.is_equal, ALU.mult)
        s.op("v", masks, [f"h{j}", (f"o{j}", 1)], f"hmd{j}")
        s.op("v", lambda e, i, f, j=j: e.tensor_scalar(m8[j][:], lrow[0:GL, ds(at["v", j], P)], b2[j][:, DIM:ROW], None, ALU.is_equal), [f"b2{j}", (f"o{j}", 1)], f"m8d{j}")
    for j in range(3):
        s.op("t", lambda e, i, f, j=j: e.matmul(bk[3 + j][:, 0:DIM], hm[j][:], w2[j][:], start=True, stop=False), [f"hmd{j}", f"w2{j}", (f"acc{j}", 1)])
        s.op("t", lambda e, i, f, j=j: e.matmul(bk[3 + j][:, 0:DIM], m8[j][:], b2[j][:, 0:DIM], start=False, stop=True), [f"m8d{j}"], f"o{j}")
        def gather(e, i, f, j=j):
            load(e, i, j, 1, ("w", j))
            row = acc[:, ds(at["w", j], DIM)]
            return e.tensor_tensor(row, bk[3 + j][:, 0:DIM], row, ALU.add)
        s.op("v", gather, [f"o{j}", f"acc{j-1}" if j else ("acc2", 1)], f"acc{j}")

    s = pg.stage("unsort", 1)
    yr = xr[:].rearrange("p t d -> p (t d)")[:, 0:TILES * DIM].rearrange("p (t d) -> p t d", d=DIM)
    s.dma("y", lambda e, i, f: e.dma_start(D["ys"].rearrange("(t p) d -> p t d", p=P), acc[:].rearrange("p (t d) -> p t d", d=DIM)), [], "ys")
    for t in range(TILES):
        s.dma("g", lambda e, i, f, t=t: e.indirect_dma_start(yr[:, t, :], None, D["ys"], bass.IndirectOffsetOnAxis(posi[:, t:t + 1].bitcast(U32), 0)), ["ys"], f"ga{t}")
    s.dma("y", lambda e, i, f: e.dma_start(D[out][ds(f, 1)].rearrange("a (t p) d -> p (a t) d", p=P), yr), [f"ga{t}" for t in range(TILES)], "out")

def turn(g, s, src, dst, banks, id_, wait, free, by, n_chunks=KC, dst_wait=()):
    bk = g.bank
    for c in range(n_chunks):
        b = banks[c % len(banks)]
        for t in range(TPB):
            s.op("t", lambda e, i, f, c=c, t=t, b=b: e.transpose(bk[b][:, t * P:(t + 1) * P], src[:, t, c * P:(c + 1) * P], g.ident[:]),
                 list(wait) + [free.free(f"bank{b}")], f"{id_}t{c}{t}")
        who = by[c % len(by)]
        if who == "s":
            s.op("s", lambda e, i, f, c=c, b=b: e.activation(dst[:, c, :], bk[b][:], ACT.Copy), [f"{id_}t{c}3"] + list(dst_wait), f"{id_}{c}")
        else:
            s.op("v", lambda e, i, f, c=c, b=b: e.tensor_copy(dst[:, c, :], bk[b][:]), [f"{id_}t{c}3"] + list(dst_wait), f"{id_}{c}", alone=True)
        free.read(f"bank{b}", f"{id_}{c}")


def attention(g):
    nc, pg, sb, D = g.nc, g.pg, g.scoped(), g.dram
    bk = g.bank
    pg.group()
    s = pg.stage("attention", N_BATCH)
    sl = Slots(s)
    q, k, v, xf, y = (sb("a_" + n, [P, TPB, DIM]) for n in ("q", "k", "v", "xf", "y"))
    qT, kT, yT = (sb("a_" + n, [P, KC, SEQ]) for n in ("qT", "kT", "yT"))
    pr = [sb(f"a_pr{j}", [P, SEQ]) for j in range(TPB)]
    pT = [sb(f"a_pT{j}", [P, TPB, P]) for j in range(TPB)]
    st = sb("a_st", [P, TPB, 4])
    for n, (t, w) in enumerate(((q, "qT"), (k, "kT"))):
        s.dma("y", lambda e, i, f, n=n, t=t: e.dma_start(t[:], rows(D["qkv"][n], i)), [(w + "t13", 1)], "qk"[n])
    s.dma("y", lambda e, i, f: e.dma_start(v[:], rows(D["qkv"][2], i)), [("av3", 1)], "v")
    s.dma("y", lambda e, i, f: e.dma_start(xf[:], rows(D["xf"], i)), [("y3", 1)], "xf")
    turn(g, s, q, qT, (0, 1), "qT", ["q"], sl, "sv", dst_wait=[("sc3", 1)])
    turn(g, s, k, kT, (2, 3), "kT", ["k"], sl, "sv", dst_wait=[("sc3", 1)])
    for t in range(TPB):
        for c in range(KC):
            s.op("t", lambda e, i, f, t=t, c=c: e.matmul(bk[4 + t][:], qT[:, c, t * P:(t + 1) * P], kT[:, c, :], start=(c == 0), stop=(c == 1)),
                 ["qT0", "qT1", "kT0", "kT1", sl.free(f"bank{4+t}")], f"sc{t}" if c else None)
        s.op("v", lambda e, i, f, t=t: e.tensor_reduce(st[:, t, 0:1], bk[4 + t][:], AX.X, ALU.max), [f"sc{t}", (f"ex{t}", 1)], f"mx{t}")
        s.op("v", lambda e, i, f, t=t: e.tensor_scalar(st[:, t, 1:2], st[:, t, 0:1], -1.0 / 16, None, ALU.mult), [f"mx{t}"], f"nm{t}")
        s.op("s", lambda e, i, f, t=t: e.activation(pr[t][:], bk[4 + t][:], ACT.Exp, bias=st[:, t, 1:2], scale=1.0 / 16, accum_out=st[:, t, 2:3]), [f"nm{t}", (f"pt{t}3", 1), (f"rs{t}", 1)], f"ex{t}")
        sl.read(f"bank{4+t}", f"ex{t}")
    for t in range(TPB):
        for k_ in range(TPB):
            s.op("t", lambda e, i, f, t=t, k_=k_: e.transpose(bk[t][:, k_ * P:(k_ + 1) * P], pr[t][:, k_ * P:(k_ + 1) * P], g.ident[:]), [f"ex{t}", sl.free(f"bank{t}")], f"pt{t}{k_}")
        s.op("v", lambda e, i, f, t=t: e.tensor_copy(pT[t][:], bk[t][:].rearrange("p (k n) -> p k n", k=TPB)), [f"pt{t}3", (f"av{t}", 1)], f"pT{t}", alone=True)
        sl.read(f"bank{t}", f"pT{t}")
        s.op("v", lambda e, i, f, t=t: e.reciprocal(st[:, t, 3:4], st[:, t, 2:3]), [f"ex{t}"], f"rs{t}")
    for t in range(TPB):
        b = 4 + t
        for k_ in range(TPB):
            s.op("t", lambda e, i, f, t=t, k_=k_, b=b: e.matmul(bk[b][:, 0:DIM], pT[t][:, k_, :], v[:, k_, :], start=(k_ == 0), stop=(k_ == 3)), [f"pT{t}", "v", sl.free(f"bank{b}")], f"av{t}" if k_ == 3 else None)
        s.op("v", lambda e, i, f, t=t, b=b: e.scalar_tensor_tensor(y[:, t, :], bk[b][:, 0:DIM], st[:, t, 3:4], xf[:, t, :], ALU.mult, ALU.add), [f"av{t}", f"rs{t}", "xf", ("st_y", 1), ("yTt13", 1)], f"y{t}")
        sl.read(f"bank{b}", f"y{t}")
    s.dma("y", lambda e, i, f: e.dma_start(rows(D["y"], i), y[:]), ["y3"], "st_y")
    turn(g, s, y, yT, (0, 1), "yT", ["y3"], sl, "sv", dst_wait=[("st_yT", 1)])
    s.dma("y", lambda e, i, f: e.dma_start(cols(D["yT"], i), yT[:]), ["yT0", "yT1"], "st_yT")
    sl.close()


def combine(g):
    nc, pg, sb, D = g.nc, g.pg, g.scoped(), g.dram
    bk = g.bank
    pg.group()
    wo = sb("b_wo", [P, 4, DIM])
    w = sb("b_w", [P, DIM])
    s = pg.stage("combine weights", 1)
    s.dma("y", lambda e, i, f: e.dma_start(wo[:], D["wo0"]), [], "wo")
    s.dma("y", lambda e, i, f: e.dma_start(w[:], D["L1_ffn_attn_norm_w"][None, :].broadcast_to((P, DIM))), [], "w")
    s = pg.stage("combine", N_BATCH)
    sl = Slots(s)
    og = sb("b_og", [P, TPB, 512])
    ogT = sb("b_ogT", [P, 4, SEQ])
    x, y, ff, xn, a, a2 = (sb("b_" + n, [P, TPB, DIM]) for n in ("x", "y", "ff", "xn", "a", "a2"))
    xnT, aT = (sb("b_" + n, [P, KC, SEQ]) for n in ("xnT", "aT"))
    stat, mv, rs = sb("b_stat", [P, TPB, 6]), sb("b_mv", [P, TPB, 2]), sb("b_rs", [P, TPB, 4])
    s.dma("y", lambda e, i, f: e.dma_start(og[:], rows(D["og"], i)), [("ogTt33", 1)], "og")
    s.dma("y", lambda e, i, f: e.dma_start(x[:], rows(D["x"], i)), [("st_x1", 1), ("xn3", 1)], "x")
    s.dma("y", lambda e, i, f: e.dma_start(y[:], rows(D["y"], i)), [("sum1", 1)], "y")
    s.dma("y", lambda e, i, f: e.dma_start(ff[:], rows(D["ff"][0], i)), [("sum2", 1)], "ff")
    turn(g, s, og, ogT, (0, 1, 2, 3), "ogT", ["og"], sl, "s", n_chunks=4, dst_wait=[("ow3", 1)])
    s.op("g", lambda e, i, f: e.tensor_tensor(y[:], x[:], y[:], ALU.add), ["x", "y"], "sum1")
    s.op("g", lambda e, i, f: e.tensor_tensor(x[:], y[:], ff[:], ALU.add), ["sum1", "ff"], "sum2")
    for t in range(TPB):
        b = 4 + t // 2
        for c in range(4):
            s.op("t", lambda e, i, f, t=t, c=c, b=b: e.matmul(bk[b][:, (t % 2) * 256:(t % 2) * 256 + 256], ogT[:, c, t * P:(t + 1) * P], wo[:, c, :], start=(c == 0), stop=(c == 3)),
                 [f"ogT{c}", sl.free(f"bank{b}")], f"ow{t}" if c == 3 else None)
    for q in range(2):
        s.op("v", lambda e, i, f, q=q: e.tensor_tensor(x[:, 2 * q:2 * q + 2, :], bk[4 + q][:].rearrange("p (t n) -> p t n", t=2), x[:, 2 * q:2 * q + 2, :], ALU.add), [f"ow{2*q+1}", "sum2"], f"x1{q}")
        sl.read(f"bank{4+q}", f"x1{q}")
    s.dma("y", lambda e, i, f: e.dma_start(rows(D["x1"], i), x[:]), ["x11", "x10"], "st_x1")
    for t in range(TPB):
        s.op("v", lambda e, i, f, t=t: e.bn_stats(stat[:, t, :], x[:, t, :]), [f"x1{t//2}"], f"st{t}", alone=True)
    for t in range(TPB):
        s.op("v", lambda e, i, f, t=t: e.bn_aggr(mv[:, t, :], stat[:, t, :]), [f"st{t}"], f"ag{t}", alone=True)
    s.op("s", lambda e, i, f: e.activation(rs[:, :, 0:1], mv[:, :, 1:2], ACT.Sqrt, bias=g.eps5[:, 0:1]), ["ag3"], "sd")
    s.op("v", lambda e, i, f: e.reciprocal(rs[:, :, 1:2], rs[:, :, 0:1]), ["sd"], "rstd")
    for t in range(TPB):
        s.op("v", lambda e, i, f, t=t: e.tensor_scalar(xn[:, t, :], x[:, t, :], mv[:, t, 0:1], rs[:, t, 1:2], ALU.subtract, ALU.mult), ["rstd", ("xnTt13", 1), ("st_xn", 1), ("am3", 1)], f"xn{t}")
    s.dma("y", lambda e, i, f: e.dma_start(rows(D["xn2"], i), xn[:]), ["xn3"], "st_xn")
    turn(g, s, xn, xnT, (6, 7), "xnT", ["xn3"], sl, "sv", dst_wait=[("st_xnT", 1)])
    s.dma("y", lambda e, i, f: e.dma_start(cols(D["xn2T"], i), xnT[:]), ["xnT0", "xnT1"], "st_xnT")
    rms(s, xn, a, a2, rs, w, g, ["xn3"], [("aTt13", 1)], "a")
    turn(g, s, a, aT, (0, 1), "aT", ["am3"], sl, "sv", dst_wait=[("st_aT", 1)])
    s.dma("y", lambda e, i, f: e.dma_start(cols(D["aT"], i), aT[:]), ["aT0", "aT1"], "st_aT")
    sl.close()


def rms(s, x, a, sq, rs, w, g, wait, free, n):
    s.op("g", lambda e, i, f: e.tensor_tensor(sq[:], x[:], x[:], ALU.mult), wait, n + "sq")
    s.op("v", lambda e, i, f: e.tensor_reduce(rs[:, :, 2], sq[:], AX.X, ALU.add), [n + "sq"], n + "ss")
    s.op("s", lambda e, i, f: e.activation(rs[:, :, 2], rs[:, :, 2], ACT.Sqrt, bias=g.eps6[:, 0:1], scale=1.0 / DIM), [n + "ss"], n + "rt")
    s.op("v", lambda e, i, f: e.reciprocal(rs[:, :, 3], rs[:, :, 2]), [n + "rt"], n + "rr")
    for t in range(TPB):
        s.op("v", lambda e, i, f, t=t: e.scalar_tensor_tensor(a[:, t, :], x[:, t, :], rs[:, t, 3:4], w[:], ALU.mult, ALU.mult), [n + "rr"] + list(free), f"{n}m{t}")


def linear(g):
    nc, pg, sb, D = g.nc, g.pg, g.scoped(), g.dram
    bk = g.bank
    NH, HD = 4, 64
    pg.group()
    w = sb("l_w", [P, KC, 768])
    wo = sb("l_wo", [P, KC, DIM])
    va = sb("l_va", [P, TPB, NH, HD + 1])
    s = pg.stage("linear weights", 1)
    s.dma("y", lambda e, i, f: e.dma_start(w[:], D["lin_w"]), [], "w")
    s.dma("y", lambda e, i, f: e.dma_start(wo[:], D["lin_wo"]), [], "wo")
    s.op("v", lambda e, i, f: e.memset(va[:], 1.0))
    s = pg.stage("linear", N_BATCH)
    sl = Slots(s)
    xT = sb("l_xT", [P, KC, SEQ])
    qk, ex, sq = (sb("l_" + n, [P, TPB, 512]) for n in ("qk", "ex", "sq"))
    ss = sb("l_ss", [P, TPB * 8])
    qkT = sb("l_qkT", [P, TPB, 4, P])
    sT = sb("l_sT", [P, TPB, 2, 2, P])
    kv = sb("l_kv", [P, 2, HD + 1])
    den = sb("l_den", [P, 2, 2])
    y = sb("l_y", [P, TPB, DIM])
    yT = sb("l_yT", [P, KC, SEQ])
    lo = sb("l_lo", [P, TPB, DIM])
    s.dma("y", lambda e, i, f: e.dma_start(xT[:], cols(D["xn2T"], i)), [("pv3", 1)], "xT")
    for t in range(TPB):
        b, b2 = t % 2, 2 + t % 2
        for c in range(KC):
            s.op("t", lambda e, i, f, t=t, c=c, b=b: e.matmul(bk[b][:], xT[:, c, t * P:(t + 1) * P], w[:, c, 0:512], start=(c == 0), stop=(c == 1)), ["xT", sl.free(f"bank{b}")], f"pq{t}" if c else None)
        for c in range(KC):
            s.op("t", lambda e, i, f, t=t, c=c, b2=b2: e.matmul(bk[b2][:, 0:256], xT[:, c, t * P:(t + 1) * P], w[:, c, 512:768], start=(c == 0), stop=(c == 1)), ["xT", sl.free(f"bank{b2}")], f"pv{t}" if c else None)
        s.op("v", lambda e, i, f, t=t, b=b: e.tensor_scalar(ex[:, t, :], bk[b][:], 0.0, None, ALU.min), [f"pq{t}", (f"feat{t}", 1)], f"mn{t}")
        s.op("s", lambda e, i, f, t=t: e.activation(ex[:, t, :], ex[:, t, :], ACT.Exp), [f"mn{t}"], f"ex{t}")
        s.op("v", lambda e, i, f, t=t, b=b: e.scalar_tensor_tensor(qk[:, t, :], bk[b][:], 0.0, ex[:, t, :], ALU.max, ALU.add), [f"ex{t}", (f"kvu{t}", 1), (f"tq{t}3", 1)], f"feat{t}")
        sl.read(f"bank{b}", f"feat{t}")
        s.op("v", lambda e, i, f, t=t, b2=b2: e.tensor_copy(va[:, t, :, 0:HD], bk[b2][:, 0:256].rearrange("p (h d) -> p h d", h=NH)), [f"pv{t}", (f"kvu{t}", 1), (f"o{t}3", 1)], f"va{t}", alone=True)
        sl.read(f"bank{b2}", f"va{t}")
        s.op("g", lambda e, i, f, t=t: e.tensor_tensor(sq[:, t, :], qk[:, t, :], qk[:, t, :], ALU.mult), [f"feat{t}", ("ssum", 1)], f"sq{t}")
    h8 = lambda a: a[:].rearrange("p t (h d) -> p (t h) d", d=HD)
    s.op("v", lambda e, i, f: e.tensor_reduce(ss[:], h8(sq), AX.X, ALU.add), ["sq3", ("un", 1)], "ssum")
    s.op("s", lambda e, i, f: e.activation(ss[:], ss[:], ACT.Sqrt), ["ssum"], "nrm")
    s.op("v", lambda e, i, f: e.tensor_scalar(ss[:], ss[:], 1e-6, None, ALU.add), ["nrm"], "nrm2")
    s.op("v", lambda e, i, f: e.reciprocal(ss[:], ss[:]), ["nrm2"], "rn")
    s.op("v", lambda e, i, f: e.tensor_tensor(h8(qk), h8(qk), ss[:, :, None].broadcast_to((P, TPB * 8, HD)), ALU.mult), ["rn", "sq3"], "un")
    s.op("g", lambda e, i, f: e.memset(kv[:], 0.0), [("kvn3", 1), ("o33", 1)], "kvn", alone=True)
    for t in range(TPB):
        b = 4 + t % 2
        for j in range(4):
            s.op("t", lambda e, i, f, t=t, j=j, b=b: e.transpose(bk[b][:, j * P:(j + 1) * P], qk[:, t, j * P:(j + 1) * P], g.ident[:]), ["un", sl.free(f"bank{b}")], f"tq{t}{j}")
        s.op("s", lambda e, i, f, t=t, b=b: e.activation(qkT[:, t], bk[b][:].rearrange("p (j n) -> p j n", j=4), ACT.Copy), [f"tq{t}3", (f"o{t}3", 1)], f"qT{t}")
        sl.read(f"bank{b}", f"qT{t}")
        for q in range(2):
            for h in (q, q + 2):
                a = q * HD
                s.op("t", lambda e, i, f, t=t, h=h, a=a, q=q: e.matmul(bk[6 + q][:, (h // 2) * P:(h // 2 + 1) * P], qkT[a:a + HD, t, 2 + h // 2, :], qkT[a:a + HD, t, h // 2, :], start=True, stop=True), [f"qT{t}", sl.free(f"bank{6+q}")], f"s{t}{h}")
            s.op("v", lambda e, i, f, t=t, q=q: e.tensor_tensor(sT[:, t, q], bk[6 + q][:, 0:256].rearrange("p (h n) -> p h n", h=2), g.upper[:, None, :].broadcast_to((P, 2, P)), ALU.mult), [f"s{t}{q+2}", (f"o{t}3", 1)], f"sT{t}{q}")
            sl.read(f"bank{6+q}", f"sT{t}{q}")
    for t in range(TPB):
        prev = "kvn" if t == 0 else f"kvn{t-1}"
        b2 = 2 + t % 2
        for q in range(2):
            b, a = q + 4 * (t % 2), q * HD
            for h in (q, q + 2):
                o = (h // 2) * 65
                s.op("t", lambda e, i, f, t=t, h=h, o=o, b=b, q=q: e.matmul(bk[b][:, o:o + 65], sT[:, t, q, h // 2, :], va[:, t, h, :], start=True, stop=False), [f"sT{t}{q}", f"va{t}", sl.free(f"bank{b}")])
                s.op("t", lambda e, i, f, t=t, h=h, o=o, b=b, a=a: e.matmul(bk[b][:, o:o + 65], qkT[a:a + HD, t, h // 2, :], kv[a:a + HD, h // 2, :], start=False, stop=True), [prev], f"o{t}{h}")
        for h in range(NH):
            a = (h % 2) * HD
            s.op("t", lambda e, i, f, t=t, h=h, a=a, b2=b2: e.matmul(bk[b2][a:a + HD, (h // 2) * 65:(h // 2) * 65 + 65], qk[:, t, 256 + h * HD:256 + (h + 1) * HD], va[:, t, h, :], start=True, stop=True), [sl.free(f"bank{b2}")], f"kv{t}{h}")
        s.producers[f"kvu{t}"] = s.producers[f"kv{t}3"]
        s.op("v", lambda e, i, f, b2=b2: e.tensor_tensor(kv[:], bk[b2][:, 0:130].rearrange("p (j n) -> p j n", j=2), kv[:], ALU.add), [f"kv{t}3", f"o{t}3", prev], f"kvn{t}")
        sl.read(f"bank{b2}", f"kvn{t}")
        for q in range(2):
            b = q + 4 * (t % 2)
            ov = bk[b][:, 0:130].rearrange("p (j n) -> p j n", j=2)
            s.op("v", lambda e, i, f, ov=ov, q=q: e.tensor_scalar(den[:, q, :, None], ov[:, :, HD:HD + 1], 1e-6, None, ALU.add), [f"o{t}{q+2}"] + ([f"y{t-1}{q}"] if t else [(f"y3{q}", 1)]), f"d{t}{q}")
            s.op("v", lambda e, i, f, q=q: e.reciprocal(den[:, q, :], den[:, q, :]), [f"d{t}{q}"], f"rd{t}{q}")
            s.op("v", lambda e, i, f, t=t, ov=ov, q=q: e.tensor_tensor(y[:, t, :].rearrange("p (j q d) -> p j q d", q=2, d=HD)[:, :, q, :], ov[:, :, 0:HD], den[:, q, :, None].broadcast_to((P, 2, HD)), ALU.mult), [f"rd{t}{q}", ("yTt13", 1)], f"y{t}{q}")
            sl.read(f"bank{b}", f"y{t}{q}")
    turn(g, s, y, yT, (2, 3), "yT", ["y30", "y31"], sl, "sv", dst_wait=[("lo3", 1)])
    for t in range(TPB):
        b = 6 + t // 2
        for c in range(KC):
            s.op("t", lambda e, i, f, t=t, c=c, b=b: e.matmul(bk[b][:, (t % 2) * 256:(t % 2) * 256 + 256], yT[:, c, t * P:(t + 1) * P], wo[:, c, :], start=(c == 0), stop=(c == 1)), ["yT0", "yT1", sl.free(f"bank{b}")], f"lo{t}" if c else None)
    for q in range(2):
        s.op("s", lambda e, i, f, q=q: e.activation(lo[:, 2 * q:2 * q + 2, :], bk[6 + q][:].rearrange("p (t n) -> p t n", t=2), ACT.Copy), [f"lo{2*q+1}", ("st_lo", 1)], f"loe{q}")
        sl.read(f"bank{6+q}", f"loe{q}")
    s.dma("y", lambda e, i, f: e.dma_start(rows(D["lin"], i), lo[:]), ["loe1", "loe0"], "st_lo")
    sl.close()


def grouped(g):
    nc, pg, sb, D = g.nc, g.pg, g.scoped(), g.dram
    bk = g.bank
    pg.group()
    w = sb("g_w", [P, KC, 5 * P])
    wv = sb("g_wv", [P, KC, 64])
    wo = sb("g_wo", [P, KC, DIM])
    s = pg.stage("grouped weights", 1)
    s.dma("y", lambda e, i, f: e.dma_start(w[:], D["gqa_w"]), [], "w")
    s.dma("y", lambda e, i, f: e.dma_start(wv[:], D["gqa_wv"]), [], "wv")
    s.dma("y", lambda e, i, f: e.dma_start(wo[:], D["gqa_wo"]), [], "wo")
    s = pg.stage("grouped", N_BATCH)
    sl = Slots(s)
    aT = sb("g_aT", [P, KC, SEQ])
    qkT = sb("g_qkT", [P, 5, SEQ])
    v = sb("g_v", [P, TPB, 64])
    xn = sb("g_xn", [P, TPB, DIM])
    st = sb("g_st", [P, TPB, 4, 4, 4])
    pr = [sb(f"g_pr{j}", [P, 4, SEQ]) for j in range(2)]
    pT = [sb(f"g_pT{j}", [P, 4, TPB, P]) for j in range(2)]
    o = sb("g_o", [P, TPB, DIM])
    oT = sb("g_oT", [P, KC, SEQ])
    s.dma("y", lambda e, i, f: e.dma_start(aT[:], cols(D["aT"], i)), [("pv", 1)], "aT")
    s.dma("y", lambda e, i, f: e.dma_start(xn[:], rows(D["xn2"], i)), [("st_h", 1)], "xn")
    for j in range(5):
        b = j % 4
        for c in range(KC):
            s.op("t", lambda e, i, f, j=j, c=c, b=b: e.matmul(bk[b][:], w[:, c, j * P:(j + 1) * P], aT[:, c, :], start=(c == 0), stop=(c == 1)), ["aT", sl.free(f"bank{b}")], f"p{j}" if c else None)
        s.op("s", lambda e, i, f, j=j, b=b: e.activation(qkT[:, j, :], bk[b][:], ACT.Copy), [f"p{j}", ("last_scores", 1)], f"qk{j}")
        sl.read(f"bank{b}", f"qk{j}")
    for t in range(TPB):
        for c in range(KC):
            s.op("t", lambda e, i, f, t=t, c=c: e.matmul(bk[4][:, t * 64:(t + 1) * 64], aT[:, c, t * P:(t + 1) * P], wv[:, c, :], start=(c == 0), stop=(c == 1)), ["aT", sl.free("bank4")], f"pv{t}" if c else None)
    s.producers["pv"] = s.producers["pv3"]
    s.op("s", lambda e, i, f: e.activation(v[:], bk[4][:, 0:256].rearrange("p (t n) -> p t n", t=TPB), ACT.Copy), ["pv3", ("last_av", 1)], "v")
    sl.read("bank4", "v")
    step = 0
    units = [(t, j) for t in range(TPB) for j in range(4)]

    def scores(t, j):
        W, p = (t + 1) * P, (4 * t + j) % 2
        for k in range(4):
            s.op("t", lambda e, i, f, t=t, j=j, k=k, W=W: e.matmul(bk[k][:, 0:W], qkT[32 * k:32 * k + 16, j, t * P:(t + 1) * P], qkT[32 * k:32 * k + 16, 4, 0:W], start=True, stop=False, skip_group_check=True),
                 [f"qk{j}", "qk4", sl.free(f"bank{k}")])
        for k in range(4):
            s.op("t", lambda e, i, f, t=t, k=k, W=W: e.matmul(bk[k][:, W - P:W], g.identb[:], g.negl[:], start=False, stop=True, skip_group_check=True), [], f"sc{t}{j}{k}")
        for k in range(4):
            s.op("v", lambda e, i, f, t=t, j=j, k=k, W=W: e.tensor_reduce(st[:, t, j, 0, k:k + 1], bk[k][:, 0:W], AX.X, ALU.max), [f"sc{t}{j}{k}"], f"mx{t}{j}{k}")
        s.op("v", lambda e, i, f, t=t, j=j: e.tensor_scalar(st[:, t, j, 1, :], st[:, t, j, 0, :], -0.25, None, ALU.mult), [f"mx{t}{j}3", (f"ex{t}{j}3", 1)], f"nm{t}{j}")
        for k in range(4):
            s.op("s", lambda e, i, f, t=t, j=j, k=k, W=W, p=p: e.activation(pr[p][:, k, 0:W], bk[k][:, 0:W], ACT.Exp, bias=st[:, t, j, 1, k:k + 1], scale=0.25, accum_out=st[:, t, j, 2, k:k + 1]),
                 [f"nm{t}{j}", sl.free(f"pr{p}")], f"ex{t}{j}{k}")
            sl.read(f"bank{k}", f"ex{t}{j}{k}")

    def values(t, j):
        W, p = (t + 1) * P, (4 * t + j) % 2
        for k in range(4):
            b = 4 + k % 2
            for u in range(t + 1):
                s.op("t", lambda e, i, f, k=k, u=u, b=b, p=p: e.transpose(bk[b][:, u * P:(u + 1) * P], pr[p][:, k, u * P:(u + 1) * P], g.ident[:]), [f"ex{t}{j}{k}", sl.free(f"bank{b}")], f"tr{t}{j}{k}{u}")
            if k % 2:
                s.op("s", lambda e, i, f, t=t, k=k, b=b, p=p, W=W: e.activation(pT[p][:, k, 0:t + 1, :], bk[b][:, 0:W].rearrange("p (u n) -> p u n", n=P), ACT.Copy), [f"tr{t}{j}{k}{t}", sl.free(f"pT{p}")], f"pT{t}{j}{k}")
            else:
                s.op("v", lambda e, i, f, t=t, k=k, b=b, p=p, W=W: e.tensor_copy(pT[p][:, k, 0:t + 1, :], bk[b][:, 0:W].rearrange("p (u n) -> p u n", n=P)), [f"tr{t}{j}{k}{t}", sl.free(f"pT{p}")], f"pT{t}{j}{k}", alone=True)
            sl.read(f"bank{b}", f"pT{t}{j}{k}")
        sl.read(f"pr{p}", f"tr{t}{j}3{t}")
        b = 6 + j % 2
        for k in range(4):
            for u in range(t + 1):
                s.op("t", lambda e, i, f, t=t, k=k, u=u, b=b, p=p: e.matmul(bk[b][:, k * 16:(k + 1) * 16], pT[p][:, k, u, :], v[:, u, k * 16:(k + 1) * 16], start=(u == 0), stop=(u == t)), [f"pT{t}{j}{k}", "v", sl.free(f"bank{b}")], f"av{t}{j}{k}" if u == t else None)
        sl.read(f"pT{p}", f"av{t}{j}3")
        s.op("v", lambda e, i, f, t=t, j=j: e.reciprocal(st[:, t, j, 3, :], st[:, t, j, 2, :]), [f"ex{t}{j}3"], f"rs{t}{j}")
        s.op("v", lambda e, i, f, t=t, j=j, b=b: e.tensor_tensor(o[:, t, :].rearrange("p (k j d) -> p k j d", j=4, d=16)[:, :, j, :], bk[b][:, 0:64].rearrange("p (k d) -> p k d", d=16), st[:, t, j, 3, :, None].broadcast_to((P, 4, 16)), ALU.mult), [f"av{t}{j}3", f"rs{t}{j}", ("oTt13", 1)], f"o{t}{j}")
        sl.read(f"bank{b}", f"o{t}{j}")

    for n, (t, j) in enumerate(units):
        scores(t, j)
        if n:
            values(*units[n - 1])
    values(*units[-1])
    s.producers["last_scores"] = s.producers["sc333"]
    s.producers["last_av"] = s.producers["av333"]
    turn(g, s, o, oT, (0, 1), "oT", ["o33"], sl, "sv", dst_wait=[("ho3", 1)])
    for t in range(TPB):
        b = 2 + t // 2
        for c in range(KC):
            s.op("t", lambda e, i, f, t=t, c=c, b=b: e.matmul(bk[b][:, (t % 2) * 256:(t % 2) * 256 + 256], oT[:, c, t * P:(t + 1) * P], wo[:, c, :], start=(c == 0), stop=(c == 1)), ["oT0", "oT1", sl.free(f"bank{b}")], f"ho{t}" if c else None)
    for q in range(2):
        s.op("v", lambda e, i, f, q=q: e.tensor_tensor(xn[:, 2 * q:2 * q + 2, :], bk[2 + q][:].rearrange("p (t n) -> p t n", t=2), xn[:, 2 * q:2 * q + 2, :], ALU.add), [f"ho{2*q+1}", "xn"], f"h{q}")
        sl.read(f"bank{2+q}", f"h{q}")
    s.dma("y", lambda e, i, f: e.dma_start(rows(D["h"], i), xn[:]), ["h0", "h1"], "st_h")
    sl.close()


def experts(g):
    nc, pg, sb, D = g.nc, g.pg, g.scoped(), g.dram
    bk = g.bank
    NE = 8
    pg.group()
    we = sb("m_we", [P, KC, NE * DIM])
    wg = sb("m_wg", [P, KC, NE])
    w = sb("m_w", [P, DIM])
    s = pg.stage("expert weights", 1)
    s.dma("y", lambda e, i, f: e.dma_start(we[:], D["moe_w"]), [], "we")
    s.dma("y", lambda e, i, f: e.dma_start(wg[:], D["moe_gate"]), [], "wg")
    s.dma("y", lambda e, i, f: e.dma_start(w[:], D["L1_ffn_ffn_norm_w"][None, :].broadcast_to((P, DIM))), [], "w")
    s = pg.stage("experts", N_BATCH)
    sl = Slots(s)
    h, x1, lin, tt, t2 = (sb("m_" + n, [P, TPB, DIM]) for n in ("h", "x1", "lin", "t", "t2"))
    tT = sb("m_tT", [P, KC, SEQ])
    rs = sb("m_rs", [P, TPB, 4])
    lg = sb("m_lg", [P, TPB, NE])
    m8 = sb("m_m8", [P, TPB, 8])
    ix = sb("m_ix", [P, TPB, 8], U32)
    ixf = sb("m_ixf", [P, TPB, 8])
    cw = sb("m_cw", [P, TPB, 4])
    c1, comb = sb("m_c1", [P, TPB, NE]), sb("m_comb", [P, TPB, NE])
    s.dma("y", lambda e, i, f: e.dma_start(h[:], rows(D["h"], i)), [("s1", 1), ("tm3", 1)], "h")
    s.dma("y", lambda e, i, f: e.dma_start(x1[:], rows(D["x1"], i)), [("st_out", 1)], "x1")
    s.dma("y", lambda e, i, f: e.dma_start(lin[:], rows(D["lin"], i)), [("s2", 1)], "lin")
    rms(s, h, tt, t2, rs, w, g, ["h"], [("tTt13", 1)], "t")
    s.op("g", lambda e, i, f: e.tensor_tensor(x1[:], x1[:], h[:], ALU.add), ["x1", "h"], "s1")
    s.op("g", lambda e, i, f: e.tensor_tensor(x1[:], x1[:], lin[:], ALU.add), ["s1", "lin"], "s2")
    turn(g, s, tt, tT, (0, 1), "tT", ["tm3"], sl, "sv", dst_wait=[("last_exp", 1)])
    for t in range(TPB):
        for c in range(KC):
            s.op("t", lambda e, i, f, t=t, c=c: e.matmul(bk[0][:, t * NE:(t + 1) * NE], tT[:, c, t * P:(t + 1) * P], wg[:, c, :], start=(c == 0), stop=(c == 1)), ["tT0", "tT1", sl.free("bank0")], f"lg{t}" if c else None)
    s.op("v", lambda e, i, f: e.tensor_copy(lg[:], bk[0][:, 0:TPB * NE].rearrange("p (t n) -> p t n", t=TPB)), ["lg3"], "lg", alone=True)
    sl.read("bank0", "lg")
    for t in range(TPB):
        s.op("v", lambda e, i, f, t=t: e.max(m8[:, t, :], lg[:, t, :]), ["lg"], f"m8{t}", alone=True)
    for t in range(TPB):
        s.op("v", lambda e, i, f, t=t: e.max_index(ix[:, t, :], m8[:, t, :], lg[:, t, :]), [f"m8{t}"], f"ix{t}", alone=True)
    s.op("v", lambda e, i, f: e.tensor_copy(ixf[:], ix[:]), ["ix3"], "ixf", alone=True)
    s.op("v", lambda e, i, f: e.tensor_tensor(cw[:, :, 0:1], m8[:, :, 1:2], m8[:, :, 0:1], ALU.subtract), ["m83"], "dm")
    s.op("s", lambda e, i, f: e.activation(cw[:, :, 1:2], cw[:, :, 0:1], ACT.Exp), ["dm"], "e2")
    s.op("v", lambda e, i, f: e.tensor_scalar(cw[:, :, 2:3], cw[:, :, 1:2], 1.0, None, ALU.add), ["e2"], "w0")
    s.op("v", lambda e, i, f: e.reciprocal(cw[:, :, 2:3], cw[:, :, 2:3]), ["w0"], "w1")
    s.op("v", lambda e, i, f: e.tensor_tensor(cw[:, :, 3:4], cw[:, :, 2:3], cw[:, :, 1:2], ALU.mult), ["w1"], "w2")
    io = g.iota[:, None, 0:NE].broadcast_to((P, TPB, NE))
    for k, (dst, nm) in enumerate(((c1, "c1"), (comb, "c2"))):
        s.op("v", lambda e, i, f, k=k, dst=dst: e.tensor_tensor(dst[:], ixf[:, :, k:k + 1].broadcast_to((P, TPB, NE)), io, ALU.is_equal), ["ixf", ("last_acc", 1)], nm + "a")
        s.op("v", lambda e, i, f, k=k, dst=dst: e.tensor_tensor(dst[:], dst[:], cw[:, :, 2 + k:3 + k].broadcast_to((P, TPB, NE)), ALU.mult), [nm + "a", "w2"], nm)
    s.op("v", lambda e, i, f: e.tensor_tensor(comb[:], comb[:], c1[:], ALU.add), ["c1", "c2"], "comb")
    for t in range(TPB):
        for q in range(4):
            b = (t % 2) * 4 + q
            for c in range(KC):
                s.op("t", lambda e, i, f, t=t, q=q, c=c, b=b: e.matmul(bk[b][:], tT[:, c, t * P:(t + 1) * P], we[:, c, q * 512:(q + 1) * 512], start=(c == 0), stop=(c == 1)), ["tT0", "tT1", sl.free(f"bank{b}")], f"x{t}{q}" if c else None)
            for n in range(2):
                k = 2 * q + n
                prev = f"a{t}{k-1}" if k else "s2"
                s.op("v", lambda e, i, f, t=t, n=n, k=k, b=b: e.scalar_tensor_tensor(x1[:, t, :], bk[b][:, n * 256:(n + 1) * 256], comb[:, t, k:k + 1], x1[:, t, :], ALU.mult, ALU.add), [f"x{t}{q}", "comb", prev], f"a{t}{k}")
            sl.read(f"bank{b}", f"a{t}{2*q+1}")
    s.producers["last_exp"] = s.producers["x33"]
    s.producers["last_acc"] = s.producers["a37"]
    s.dma("y", lambda e, i, f: e.dma_start(rows(D["out"], i), x1[:]), ["a37"], "st_out")
    sl.close()


SCRATCH = {"xf": ((TOKENS, DIM), F32), "xnT": ((KC, P, TOKENS), F32), "xfT": ((KC, P, TOKENS), F32), "ab": ((N_BATCH, P, 64), F32), "kinds": ((2, P, KINDS, TILES, 4), F32), "og": ((TOKENS, 512), F32),
 "leaf": ((P, TILES), F32), "ohb": ((P, TILES * GROUPS), BF16), "xs": ((TOKENS, ROW), F32), "ys": ((TOKENS, DIM), F32), "qkv": ((3, TOKENS, DIM), F32), "ff": ((1, TOKENS, DIM), F32),
 "y": ((TOKENS, DIM), F32), "yT": ((KC, P, TOKENS), F32), "x1": ((TOKENS, DIM), F32), "xn2": ((TOKENS, DIM), F32), "xn2T": ((KC, P, TOKENS), F32), "aT": ((KC, P, TOKENS), F32), "lin": ((TOKENS, DIM), F32), "h": ((TOKENS, DIM), F32)}
def all_stages(g):
    norms(g, None)
    decays(g)
    delta(g)
    fff(g, "t3", 3, 0, "xf", "xfT", ACT.Relu, "qkv")
    attention(g)
    fff(g, "t1", 1, 3, "y", "yT", ACT.Gelu, "ff")
    combine(g)
    linear(g)
    grouped(g)
    experts(g)


def build(nc, shapes, out_shapes):
    with ExitStack() as ctx:
        dram = {n: nc.dram_tensor(n, s, dt, kind="ExternalInput").ap() for n, (s, dt) in shapes.items()}
        for n, s in out_shapes.items():
            dram[n] = nc.dram_tensor(n, s, F32, kind="ExternalOutput").ap()

        def scratch(n, s, dt=F32):
            dram[n] = nc.dram_tensor(n, s, dt, kind="Internal").ap()

        for n, (s, dt) in SCRATCH.items():
            scratch(n, s, dt)
        pg = Program(nc, ctx)
        g = Kernel(nc, pg, ctx, dram)
        g.load_constants()
        all_stages(g)
        if g.open is not None:
            g.open.close()
        pg.number()
        block = ctx.enter_context(nc.Block())
        for e, on in (("y", block.sync), ("t", block.tensor), ("v", block.vector), ("s", block.scalar), ("g", block.gpsimd)):
            def body(eng, e=e):
                pg.emit(eng, e)
            on(body)


def constants():
    r = np.arange(P)
    c = {"ident": np.eye(P, dtype=np.float32), "ones": np.ones((P, P), np.float32)}
    c["upper"] = (r[:, None] <= r[None, :]).astype(np.float32)
    c["negm"] = np.where(r[:, None] <= r[None, :], 0.0, -1e30).astype(np.float32)
    c["negl"] = np.ascontiguousarray(c["negm"].T)
    c["lvw"] = np.array([2.0 ** (7 - int(np.log2(n + 1))) for n in range(255)] + [0.0], np.float32)
    c["iota"] = np.arange(64).astype(np.float32)
    c["iota128"] = (128 * np.arange(64)).astype(np.float32)
    mask = np.zeros((P, 7, 2, P), np.uint32)
    for l in range(7):
        m = 1 << l
        low = (r // m) % 2 == 0
        same = (r[:, None] // (2 * m)) == (r[None, :] // (2 * m))
        mask[:, l, 0] = same & low[:, None] & ~low[None, :]
        mask[:, l, 1] = mask[:, l, 0].T
    c["mask"] = mask
    return c


def lay_out(a):
    z = constants()
    z["x"] = a["L0_attn_x"].reshape(TOKENS, DIM)
    kp = lambda w: w.reshape(KC, P, -1).transpose(1, 0, 2)
    z["wab"] = kp(np.concatenate([a["L0_attn_Wa"], a["L0_attn_Wb"]], 1))
    q, k, v, gt = (a[f"L0_attn_W{n}"] for n in "qkvg")
    z["w_qkvg"] = np.stack([kp(np.concatenate([q[:, j * 512:][:, :512], k[:, j * 512:][:, :512], v[:, j * 256:][:, :256], gt[:, j * 256:][:, :256]], 1)) for j in range(2)])
    taps = lambda w, j, n: w[j * n * P:(j + 1) * n * P].reshape(n, P, 4).transpose(1, 0, 2).reshape(P, n * 4)
    z["conv_w"] = np.stack([np.concatenate([taps(a["L0_attn_conv_q"], j, 4), taps(a["L0_attn_conv_k"], j, 4), taps(a["L0_attn_conv_v"], j, 2)], 1) for j in range(2)])
    for n in ("L0_attn_dt_bias", "L0_attn_A_log", "L0_attn_o_norm_w"):
        z[n] = a[n]
    tree = lambda n: [a[f"L0_ffn_{t}_{n}"] for t in "qkvf"]
    z["nwT"] = np.stack([np.concatenate([kp(w.T), np.zeros((P, KC, 1), np.float32)], 2) for w in tree("nw")])
    z["nb"] = np.stack([np.concatenate([w, np.zeros(1, np.float32)]) for w in tree("nb")])
    leaf = np.arange(LEAVES, dtype=np.float32)
    z["w1p"] = np.concatenate([np.concatenate([
        w.reshape(GROUPS, GL, KC, P, LW).transpose(0, 3, 2, 1, 4).reshape(GROUPS, P, 256),
        b.reshape(GROUPS, P, 1), np.repeat(leaf, LW).reshape(GROUPS, P, 1)], 2) for w, b in zip(tree("w1"), tree("b1"))])
    z["w2p"] = np.concatenate([w.reshape(LEAVES * LW, DIM) for w in tree("w2")])
    z["b2p"] = np.concatenate([np.concatenate([b, leaf[:, None]], 1) for b in tree("b2")])
    z["wo0"] = a["L0_attn_Wo"].reshape(4, P, DIM).transpose(1, 0, 2)
    z["lin_w"] = kp(np.concatenate([a[f"L1_attn_W{n}"].T for n in "qkv"], 1))
    z["lin_wo"] = kp(a["L1_attn_Wo"].T)
    wq = a["L1_ffn_wq"].T.reshape(DIM, 4, 4, 16).transpose(0, 2, 1, 3)
    wk = a["L1_ffn_wk"].T.reshape(DIM, 1, 4, 16)
    qk = np.concatenate([wq, wk], 1)
    z["gqa_w"] = kp(np.concatenate([qk, np.zeros_like(qk)], 3).reshape(DIM, 5 * P))
    z["gqa_wv"] = kp(a["L1_ffn_wv"].T)
    z["gqa_wo"] = kp(a["L1_ffn_wo"].T)
    z["moe_w"] = kp(a["L1_ffn_expert_w"].transpose(2, 0, 1).reshape(DIM, 8 * DIM))
    z["moe_gate"] = kp(a["L1_ffn_gate_w"].T)
    for n in ("L1_ffn_attn_norm_w", "L1_ffn_ffn_norm_w"):
        z[n] = a[n]
    return {n: np.ascontiguousarray(v) for n, v in z.items()}


def kernel(**inputs):
    import concourse.bacc as bacc
    from concourse.bass_utils import run_bass_kernel_spmd

    arrays = lay_out({n: np.asarray(v) for n, v in inputs.items()})
    nc = bacc.Bacc("TRN2", target_bir_lowering=False, num_devices=1)
    build(nc, {n: (v.shape, mybir.dt.from_np(v.dtype)) for n, v in arrays.items()}, {"out": (TOKENS, DIM)})
    r = run_bass_kernel_spmd(nc, [arrays], core_ids=[0])
    return r.results[0]["out"].reshape(N_BATCH, SEQ, DIM)
```

```python
import numpy as np
import concourse.bass as bass
from concourse import mybir
from concourse.alu_op_type import AluOpType as ALU
from contextlib import ExitStack

F32 = mybir.dt.float32
BF16 = mybir.dt.bfloat16
I32 = mybir.dt.int32
U32 = mybir.dt.uint32
ACT = mybir.ActivationFunctionType
AX = mybir.AxisListType
ds = bass.ds

P = 128
N_BATCH, SEQ, DIM = 8, 512, 256
TOKENS = N_BATCH * SEQ
TILES = TOKENS // P
TPB = SEQ // P
KC = DIM // P
START = 8192
LATE = 32


def start(key):
    return 0 if key[0] == "g" and len(key) > 1 else START


class Stage:

    def __init__(self, name, count, late=False):
        self.name, self.count, self.late = name, count, late
        self.queue = {e: [] for e in "tvsgy"}
        self.producers = {}
        self.stores = []

    def op(self, engine, fn, after=(), name=None, alone=False):
        entry = dict(fn=fn, after=after, name=name, alone=alone, dma=None)
        self.queue[engine].append(entry)
        if name:
            assert name not in self.producers, name
            self.producers[name] = (engine, entry)
        return entry

    def alias(self, name, of):
        self.producers[name] = self.producers[of]

    def dma(self, engine, fn, after=(), name=None):
        entry = self.op(engine, fn, after, name, alone=True)
        entry["dma"] = (engine, len(self.stores) + (LATE if self.late and engine == "y" else 0))
        self.stores.append(entry)
        return entry


class Slots:

    def __init__(self, stage):
        self.stage, self.reader = stage, {}

    def free(self, slot):
        return self.reader.get(slot, (f"last reader of {slot}", 1))

    def read(self, slot, by):
        self.reader[slot] = by

    def close(self):
        for slot, by in self.reader.items():
            self.stage.alias(f"last reader of {slot}", by)


class Side:

    def __init__(self, stage, k, number):
        self.stage, self.k, self.number = stage, k, number

    def own(self, p):
        if not isinstance(p, str):
            return self.own(p[0]), p[1]
        return p[1:] if p[0] == "=" else f"{p}_{self.k}"

    def op(self, engine, fn, after=(), name=None, alone=False):
        number = self.number
        self.stage.op(engine, lambda e, i, f: fn(e, number(i), f), [self.own(p) for p in after], name and self.own(name), alone)

    def dma(self, engine, fn, after=(), name=None):
        number = self.number
        self.stage.dma(engine, lambda e, i, f: fn(e, number(i), f), [self.own(p) for p in after], name and self.own(name))

    def alias(self, name, of):
        self.stage.alias(self.own(name), self.own(of))


def side_by_side(main, *others):
    due = [0.0] * len(others)
    for _ in main:
        for j, (steps, rate) in enumerate(others):
            due[j] += rate
            while due[j] >= 1:
                next(steps, None)
                due[j] -= 1


def finish(*steps):
    left = list(steps)
    while left:
        left = [x for x in left if next(x, left) is not left]


class Program:

    def __init__(self, nc, ctx):
        self.nc, self.ctx, self.groups = nc, ctx, []

    def group(self, times=1):
        self.groups.append((times, []))

    def stage(self, name, count=1, late=False):
        s = Stage(name, count, late)
        self.groups[-1][1].append(s)
        return s

    def number(self):
        self.sems = {}
        self.idle = self.ctx.enter_context(self.nc.semaphore("idle"))
        level = {}
        for times, stages in self.groups:
            first = dict(level)
            for s in stages:
                names = {p if isinstance(p, str) else p[0] for e in "tvsgy" for o in s.queue[e] for p in o["after"] if isinstance(p, str) or s.count > 1}
                assert names <= set(s.producers), (s.name, names - set(s.producers))
                wanted = {id(s.producers[p][1]) for p in names}
                s.step, s.base = {}, {}
                for e in "tvsg":
                    mine = [o for o in s.queue[e] if o["dma"] is None]
                    n = 0
                    for o in mine:
                        o["rank"] = None
                        if id(o) in wanted or o is mine[-1]:
                            n += 1
                            o["rank"] = n
                    s.step[e] = n
                for o in s.stores:
                    s.step[o["dma"]] = 16
                    o["rank"] = 16
                for key, n in s.step.items():
                    s.base[key] = level.setdefault(key, start(key))
                    level[key] += n * s.count
            for s in stages:
                s.per_time = {k: level[k] - first.get(k, start(k)) for k in level}
            for k in level:
                level[k] = first.get(k, start(k)) + times * (level[k] - first.get(k, start(k)))
        for key in level:
            self.sems[key] = self.ctx.enter_context(self.nc.semaphore("progress_" + "".join(map(str, key))))

    def ends(self, s, f):
        for key, n in s.step.items():
            if n:
                yield key, s.base[key] + s.count * n + f * s.per_time[key]

    def emit(self, eng, e):
        previous = None
        for key in self.sems:
            if start(key) and key[0] == e:
                eng.sem_inc(self.sems[key], START)
        for times, stages in self.groups:
            def body(f, previous):
                for n, s in enumerate(stages):
                    waits = []
                    if n == 0:
                        if previous is not None:
                            waits += self.ends(*previous)
                        if times > 1:
                            waits += self.ends(stages[-2 if stages[-1].late else -1], f - 1)
                    else:
                        waits += self.ends(stages[n - 1], f)
                        if n == 2 and times > 1 and stages[-1].late:
                            waits += self.ends(stages[-1], f - 1)
                    for key, value in waits:
                        eng.wait_ge(self.sems[key], value)
                        if times > 1:
                            eng.sem_inc(self.idle, 1)
                    if s.queue[e]:
                        if s.count > 1:
                            with eng.Fori(0, s.count) as i:
                                self.run(eng, e, s, i, f)
                        else:
                            self.run(eng, e, s, 0, f)
            if times > 1:
                with eng.Fori(0, times) as f:
                    body(f, previous)
            else:
                body(0, previous)
            previous = (stages[-1], times - 1)
        if e == "y":
            for key, value in self.ends(*previous):
                eng.wait_ge(self.sems[key], value)

    def run(self, eng, e, s, i, f):
        waited = {}
        for o in s.queue[e]:
            need = {}
            for p in o["after"]:
                p, lag = p if isinstance(p, tuple) else (p, 0)
                if lag and s.count == 1:
                    continue
                pe, po = s.producers[p]
                key = po["dma"] if po["dma"] is not None else pe
                value = s.base[key] + po["rank"] - lag * s.step[key]
                if value > need.get(key, 0):
                    need[key] = value
            some = False
            for key, value in need.items():
                if value > waited.get(key, 0):
                    waited[key] = value
                    v = value + i * s.step[key]
                    if not isinstance(f, int):
                        v = v + f * s.per_time[key]
                    eng.wait_ge(self.sems[key], v)
                    if e == "y":
                        eng.sem_inc(self.idle, 1)
                    some = True
            if some and o["alone"] and e != "y":
                eng.sem_inc(self.idle, 1)
            ins = o["fn"](eng, i, f)
            if o["dma"] is not None:
                ins.then_inc(self.sems[o["dma"]], 16)
            elif o["rank"] is not None:
                ins.then_inc(self.sems[e], 1)

HEADS = 8
KINDS = 7


def rows(ap, b):
    return ap[ds(b * SEQ, SEQ), :].rearrange("(t p) d -> p t d", p=P)


def cols(ap, b):
    return ap[:, :, ds(b * SEQ, SEQ)].rearrange("c p n -> p c n")


class Kernel:

    def __init__(self, nc, pg, ctx, dram):
        self.nc, self.pg, self.ctx, self.dram = nc, pg, ctx, dram
        self.open = None
        self.bank = [ctx.enter_context(nc.psum_tensor(f"bank{b}", [P, 512], F32)) for b in range(8)]

    def keep(self, name, shape, dt=F32):
        return self.ctx.enter_context(self.nc.sbuf_tensor(name, shape, dt))

    def scoped(self):
        if self.open is not None:
            self.open.close()
        self.open = ExitStack()
        return lambda name, shape, dt=F32: self.open.enter_context(self.nc.sbuf_tensor("s_" + name, shape, dt))

    def load_constants(self):
        self.pg.group()
        s = self.pg.stage("constants", 1)

        def const(name, shape, dt=F32, view=None):
            t = self.keep("c_" + name, shape, dt)
            src = self.dram[name]
            if view == "row":
                src = src[None, :].broadcast_to((P, shape[1]))
            s.dma("y", lambda e, i, f: e.dma_start(t[:], src), [], name)
            return t

        self.ident = const("ident", [P, P])
        self.upper = const("upper", [P, P])
        self.ones = const("ones", [P, P])
        self.pick = const("pick", [P, 15])
        self.slot = const("slot", [16, 4, P])
        self.mask = const("mask", [P, 7, 2, P], U32)
        self.lvw = const("lvw", [P, 256], view="row")
        self.iota = const("iota", [P, 64], view="row")
        self.iota128 = const("iota128", [P, 64], view="row")
        self.wab = const("wab", [P, KC, 16])
        self.dtb = const("L0_attn_dt_bias", [P, 8], view="row")
        self.alog = const("L0_attn_A_log", [P, 8], view="row")
        self.onw = const("L0_attn_o_norm_w", [P, 64], view="row")

        def rounded(name, source):
            t = self.keep("c_" + name, [P, P], BF16)
            s.op("v", lambda e, i, f: e.tensor_copy(t[:], source[:]), [source_name[id(source)]])
            return t

        negm, negl = const("negm", [P, P]), const("negl", [P, P])
        source_name = {id(self.ident): "ident", id(self.ones): "ones", id(self.upper): "upper", id(negm): "negm", id(negl): "negl"}
        self.identb, self.onesb, self.upperb = rounded("identb", self.ident), rounded("onesb", self.ones), rounded("upperb", self.upper)
        self.negm, self.negl = rounded("negmb", negm), rounded("neglb", negl)
        self.ea = self.keep("ea", [P, 8])
        self.eps5 = self.keep("eps5", [P, 1])
        self.eps6 = self.keep("eps6", [P, 1])
        self.one = self.keep("one", [P, 1])
        s.op("v", lambda e, i, f: e.memset(self.eps5[:], 1e-5))
        s.op("v", lambda e, i, f: e.memset(self.eps6[:], 1e-6))
        s.op("v", lambda e, i, f: e.memset(self.one[:], 1.0))

def norms(g):
    nc, pg, own, D = g.nc, g.pg, g.scoped(), g.dram
    pg.group()
    batches = pg.stage("norms", N_BATCH // 2)

    def one(side):
        s = Side(batches, side, lambda i: 2 * i + side)
        bk = g.bank[4 * side:4 * side + 4]
        sb = lambda name, shape: own(f"{name}_{side}", shape)
        x = sb("x_in", [P, TPB, DIM])
        xn = sb("xn_rows", [P, TPB, DIM])
        xf = sb("xf_rows", [P, TPB, DIM])
        xnT = sb("xn_cols", [P, KC, SEQ])
        xfT = sb("xf_cols", [P, KC, SEQ])
        stat = sb("stat", [P, TPB, 6])
        mv = sb("mv", [P, TPB, 2])
        stat2 = sb("stat2", [P, TPB, 6])
        mv2 = sb("mv2", [P, TPB, 2])
        rs = sb("rs", [P, TPB, 4])
        ab = sb("ab", [P, TPB, 2 * HEADS])
        s.dma("y", lambda e, i, f: e.dma_start(x[:], rows(D["x"], i)), [("sub", 1)], "x")
        yield
        for t in range(TPB):
            s.op("v", lambda e, i, f, t=t: e.bn_stats(stat[:, t, :], x[:, t, :]), ["x"], f"st{t}", alone=True)
        yield
        for t in range(TPB):
            s.op("v", lambda e, i, f, t=t: e.bn_aggr(mv[:, t, :], stat[:, t, :]), [f"st{t}"], f"ag{t}", alone=True)
        s.op("s", lambda e, i, f: e.activation(rs[:, :, 0:1], mv[:, :, 1:2], ACT.Sqrt, bias=g.eps5[:, 0:1]), [f"ag{TPB-1}"], "sd")
        s.op("v", lambda e, i, f: e.reciprocal(rs[:, :, 1:2], rs[:, :, 0:1]), ["sd"], "rstd")
        yield
        for t in range(TPB):
            s.op("v", lambda e, i, f, t=t: e.tensor_scalar(xn[:, t, :], x[:, t, :], mv[:, t, 0:1], rs[:, t, 1:2], ALU.subtract, ALU.mult),
                 ["rstd", ("tn7", 1)], f"xn{t}" if t < 3 else "sub")
        yield
        for t in range(TPB):
            s.op("v", lambda e, i, f, t=t: e.bn_stats(stat2[:, t, :], xn[:, t, :]), [f"xn{t}" if t < 3 else "sub"], f"st2{t}", alone=True)
        yield
        for t in range(TPB):
            s.op("v", lambda e, i, f, t=t: e.bn_aggr(mv2[:, t, :], stat2[:, t, :]), [f"st2{t}"], f"ag2{t}", alone=True)
        s.op("s", lambda e, i, f: e.activation(rs[:, :, 2:3], mv2[:, :, 1:2], ACT.Sqrt, scale=DIM / (DIM - 1.0)), [f"ag2{TPB-1}"], "sd2")
        s.op("s", lambda e, i, f: e.activation(rs[:, :, 2:3], rs[:, :, 2:3], ACT.Sqrt, bias=g.eps5[:, 0:1]), ["sd2"], "rsd2")
        s.op("v", lambda e, i, f: e.reciprocal(rs[:, :, 3:4], rs[:, :, 2:3]), ["rsd2"], "rstd2")
        yield
        for t in range(TPB):
            s.op("v", lambda e, i, f, t=t: e.tensor_scalar(xf[:, t, :], xn[:, t, :], mv2[:, t, 0:1], rs[:, t, 3:4], ALU.subtract, ALU.mult),
                 ["rstd2", ("tf7", 1), ("store_xf", 1)], f"xf{t}")
        s.dma("y", lambda e, i, f: e.dma_start(rows(D["xf"], i), xf[:]), [f"xf{TPB-1}"], "store_xf")
        yield
        for c in range(KC):
            for t in range(TPB):
                s.op("t", lambda e, i, f, c=c, t=t: e.transpose(bk[c][:, t * P:(t + 1) * P], xn[:, t, c * P:(c + 1) * P], g.ident[:]),
                     ["sub", (f"exn{c}", 1), ("eab", 1)], f"tn{c * TPB + t}")
        yield
        for c in range(KC):
            s.op("s", lambda e, i, f, c=c: e.activation(xnT[:, c, :], bk[c][:], ACT.Copy), [f"tn{c * TPB + 3}", ("store_xnT", 1), ("ab3", 1)], f"exn{c}")
        yield
        for c in range(KC):
            for t in range(TPB):
                s.op("t", lambda e, i, f, c=c, t=t: e.transpose(bk[2 + c][:, t * P:(t + 1) * P], xf[:, t, c * P:(c + 1) * P], g.ident[:]),
                     [f"xf{TPB-1}", (f"exf{c}", 1)], f"tf{c * TPB + t}")
        yield
        for c in range(KC):
            s.op("v", lambda e, i, f, c=c: e.tensor_copy(xfT[:, c, :], bk[2 + c][:]), [f"tf{c * TPB + 3}", ("store_xfT", 1)], f"exf{c}")
        s.dma("y", lambda e, i, f: e.dma_start(cols(D["xnT"], i), xnT[:]), ["exn1"], "store_xnT")
        s.dma("y", lambda e, i, f: e.dma_start(cols(D["xfT"], i), xfT[:]), ["exf1"], "store_xfT")
        yield
        for t in range(TPB):
            for c in range(KC):
                s.op("t", lambda e, i, f, c=c, t=t: e.matmul(bk[0][:, t * 16:(t + 1) * 16], xnT[:, c, t * P:(t + 1) * P], g.wab[:, c, :], start=(c == 0), stop=(c == KC - 1)),
                     ["exn1", ("eab", 1)], f"ab{t}" if c else None)
        s.op("v", lambda e, i, f: e.tensor_copy(ab[:], bk[0][:, 0:64].rearrange("p (t n) -> p t n", n=16)), ["ab3", ("store_ab", 1)], "eab")
        s.dma("y", lambda e, i, f: e.dma_start(D["ab"][ds(i, 1)].rearrange("a p n -> p (a n)"), ab[:].rearrange("p t n -> p (t n)")), ["eab"], "store_ab")
        yield

    finish(one(0), one(1))


def decays(g):
    nc, pg, sb, D = g.nc, g.pg, g.scoped(), g.dram
    pg.group()
    s = pg.stage("decays", 1)
    N = N_BATCH * TPB * HEADS
    ab = sb("ab_all", [P, N_BATCH, TPB, 2, HEADS])
    z, m, az, sp, gg = (sb(n, [P, N]) for n in ("z", "m", "az", "sp", "gg"))
    out = sb("kinds", [P, 2, KINDS, TILES, 4])
    bk = g.bank
    a_in = ab[:, :, :, 0, :].rearrange("p b t h -> p (b t) h")
    b_in = ab[:, :, :, 1, :].rearrange("p b t h -> p (b t) h")
    v3 = lambda t: t[:].rearrange("p (n h) -> p n h", h=HEADS)
    bc = lambda t: t[:, None, :].broadcast_to((P, N // HEADS, HEADS))
    s.dma("y", lambda e, i, f: e.dma_start(ab[:].rearrange("p b t k h -> p b (t k h)"), D["ab"].rearrange("b p n -> p b n")), [], "ab")
    s.op("v", lambda e, i, f: e.tensor_tensor(v3(z), a_in, bc(g.dtb), ALU.add), ["ab"], "z")
    s.op("v", lambda e, i, f: e.tensor_scalar(m[:], z[:], -1.0, None, ALU.mult), ["z"], "m0")
    s.op("v", lambda e, i, f: e.tensor_tensor(az[:], z[:], m[:], ALU.min), ["m0"], "az")
    s.op("s", lambda e, i, f: e.activation(az[:], az[:], ACT.Exp), ["az"], "e1")
    s.op("s", lambda e, i, f: e.activation(sp[:], az[:], ACT.Ln, bias=g.one[:, 0:1]), ["e1"], "l1")
    s.op("v", lambda e, i, f: e.scalar_tensor_tensor(sp[:], z[:], 0.0, sp[:], ALU.max, ALU.add), ["l1"], "sp")
    s.op("s", lambda e, i, f: e.activation(g.ea[:], g.alog[:], ACT.Exp), [], "ea")
    s.op("v", lambda e, i, f: e.tensor_tensor(v3(gg), v3(sp), bc(g.ea), ALU.mult), ["sp", "ea"], "g0")
    s.op("v", lambda e, i, f: e.tensor_scalar(gg[:], gg[:], -1.0, None, ALU.mult), ["g0"], "g")
    s.op("t", lambda e, i, f: e.matmul(bk[0][:, 0:N], g.upper[:], gg[:], start=True, stop=True), ["g"], None)
    s.op("t", lambda e, i, f: e.matmul(bk[1][:, 0:N], g.ones[:], gg[:], start=True, stop=True), ["g"], "cum")
    def kind(k):
        return out[:, :, k]
    def src(t):
        return t.rearrange("p (n q h) -> p q n h", q=2, h=4)
    s.op("s", lambda e, i, f: e.activation(m[:].rearrange("p (n h) -> p n h", h=HEADS), b_in, ACT.Sigmoid), ["az"], "sig")
    s.op("v", lambda e, i, f: e.tensor_copy(az[:], bk[0][:, 0:N]), ["cum", "l1"], "G")
    s.op("v", lambda e, i, f: e.tensor_copy(z[:], bk[1][:, 0:N]), ["cum", "sp"], "GC")
    s.op("v", lambda e, i, f: e.tensor_tensor(sp[:], z[:], az[:], ALU.subtract), ["G", "g0", "GC"], "GC-G")
    for q in range(2):
        v = lambda k, q=q: kind(k)[:, q]
        w = lambda t, q=q: src(t)[:, q]
        s.op("v", lambda e, i, f, v=v, w=w: e.tensor_copy(v(0), w(gg[:])), ["g"])
        s.op("v", lambda e, i, f, v=v, w=w: e.tensor_scalar(v(1), w(az[:]), -1.0, None, ALU.mult), ["G"])
        s.op("v", lambda e, i, f, v=v, w=w: e.tensor_scalar(v(2), w(m[:]), -2.0, None, ALU.mult), ["sig"])
        s.op("v", lambda e, i, f, v=v, w=w: e.tensor_scalar(v(3), w(m[:]), 2.0, None, ALU.mult), ["sig"], f"k3{q}")
        s.op("s", lambda e, i, f, v=v, w=w: e.activation(v(4), w(az[:]), ACT.Exp), ["G"])
        s.op("s", lambda e, i, f, v=v, w=w: e.activation(v(5), w(sp[:]), ACT.Exp), ["GC-G"])
        s.op("s", lambda e, i, f, v=v, w=w: e.activation(v(6), w(z[:]), ACT.Exp), ["GC"], f"k6{q}")
        s.dma("y", lambda e, i, f, q=q: e.dma_start(D["kinds"][q].rearrange("p k t h -> p (k t h)"), out[:, q].rearrange("p k t h -> p (k t h)")), [f"k3{q}", f"k6{q}"], f"store{q}")


def delta(g):
    nc, pg, sb, D = g.nc, g.pg, g.scoped(), g.dram
    pg.group()
    bk = g.bank
    H = 4
    w = sb("w_qkvg", [P, 2, KC, 1536])
    cw = sb("conv_w", [P, 2, 40])
    xT = sb("d_xT", [P, KC, SEQ])
    kd, kq, sgw, kdec, v = ([sb(f"d_{n}{j}", shape) for j in range(2)] for n, shape in (
        ("kinds", [P, KINDS, TPB, H]), ("kq", [P, H, 2, SEQ]), ("gate", [P, TPB, 256]),
        ("kdec", [P, TPB, H, P]), ("v", [P, TPB, H, 64])))
    vT = sb("d_vT", [P, 2, SEQ])
    sq = [sb(f"d_sq{j}", [P, SEQ]) for j in range(2)]
    nr = sb("d_nr", [8, SEQ])
    E, M, X, W = ([sb(f"d_{n}{j}", [P, H, P]) for j in range(2)] for n in ("E", "M", "X", "W"))
    Dm = [sb(f"d_DD{j}", [P, H, P]) for j in range(4)]
    Pf = [sb(f"d_Pf{j}", [P, H, P]) for j in range(4)]
    S, R, U, T1 = (sb(n, [P, H, 64]) for n in ("d_S", "d_R", "d_U", "d_T1"))
    o = sb("d_o", [P, TPB, H, 64])
    o2 = sb("d_o2", [P, TPB, H, 64])
    ss = sb("d_ss", [P, TPB * H])

    s = pg.stage("delta weights", 1)
    s.dma("y", lambda e, i, f: e.dma_start(w[:].rearrange("p a c n -> p a (c n)"), D["w_qkvg"].rearrange("a p c n -> p a (c n)")), [], "w")
    s.dma("y", lambda e, i, f: e.dma_start(cw[:], D["conv_w"].rearrange("a p n -> p a n")), [], "cw")

    tiles = [("v", 0), ("v", 1)] + [(n, h) for h in range(H) for n in "kq"]
    col = {"q": 0, "k": 512, "v": 1024}
    ccol = {"q": 0, "k": 16, "v": 32}

    def project(s, sl, par, ahead):
        z = f"_{par}"
        if par == 0:
            s.dma("y", lambda e, i, f: e.dma_start(xT[:], cols(D["xnT"], i + ahead)), [sl.free("xT")], "xT")
        x_there = "xT" if par == 0 else ("xT", 1)
        dest = lambda n, h: vT[:, h, :] if n == "v" else kq[par][:, h, 0 if n == "k" else 1, :]
        yield
        item = sl.free(f"item{par}")
        for j, (n, h) in enumerate(tiles):
            b, id_ = 6 + j % 2, f"{n}{h}{z}"
            for c in range(KC):
                s.op("t", lambda e, i, f, b=b, n=n, h=h, c=c: e.matmul(bk[b][:], w[:, par, c, col[n] + h * P:col[n] + (h + 1) * P], xT[:, c, :], start=(c == 0), stop=(c == 1)),
                     [x_there, sl.free(f"bank{b}")], f"proj_{id_}" if c else None)
            d, k0 = dest(n, h), ccol[n] + 4 * h
            s.op("s", lambda e, i, f, b=b, d=d, k0=k0: e.activation(d, bk[b][:], ACT.Copy, scale=cw[:, par, k0 + 3:k0 + 4]),
                 [f"proj_{id_}", sl.free("vT") if n == "v" else item], f"c0_{id_}")
            for a in (1, 2, 3):
                s.op("v", lambda e, i, f, b=b, d=d, k0=k0, a=a: e.scalar_tensor_tensor(d[:, a:], bk[b][:, 0:SEQ - a], cw[:, par, k0 + 3 - a:k0 + 4 - a], d[:, a:], ALU.mult, ALU.add),
                     [f"c{a-1}_{id_}"], f"c{a}_{id_}")
            sl.read(f"bank{b}", f"c3_{id_}")
            if j == 4:
                s.dma("y", lambda e, i, f: e.dma_start(kd[par][:].rearrange("p k t h -> p k (t h)"), D["kinds"][par, :, :, ds((i + ahead) * TPB, TPB)].rearrange("p k t h -> p k (t h)")),
                      [sl.free(f"kd{par}")], "kd" + z)
            if j % 2:
                for n_, h_ in tiles[j - 1:j + 1]:
                    s.op("s", lambda e, i, f, d=dest(n_, h_): e.activation(d, d, ACT.Silu), [f"c3_{n_}{h_}{z}"], f"silu_{n_}{h_}{z}")
            yield
        for q in range(2):
            for t in (2 * q, 2 * q + 1):
                for c in range(KC):
                    s.op("t", lambda e, i, f, t=t, c=c: e.matmul(bk[6][:, (t % 2) * 256:(t % 2) * 256 + 256], xT[:, c, t * P:(t + 1) * P], w[:, par, c, 1280:1536], start=(c == 0), stop=(c == 1)),
                         [sl.free("bank6")], f"gate{t}{z}" if c else None)
            s.op("s", lambda e, i, f, q=q: e.activation(sgw[par][:, 2 * q:2 * q + 2, :], bk[6][:].rearrange("p (t n) -> p t n", t=2), ACT.Silu), [f"gate{2*q+1}{z}", item], f"sg{q}{z}")
            sl.read("bank6", f"sg{q}{z}")
            yield
        sl.read("xT", f"gate3{z}")
        for j, (n, h) in enumerate(tiles[2:]):
            id_, d, k = f"{n}{h}{z}", dest(n, h), j % 2
            s.op("g", lambda e, i, f, d=d, k=k: e.tensor_tensor(sq[k][:], d, d, ALU.mult), [f"silu_{id_}", sl.free(f"sq{k}")], f"sq_{id_}")
            s.op("t", lambda e, i, f, j=j, k=k: e.matmul(bk[7][0:8, :], g.pick[:, 7 - j:15 - j], sq[k][:], start=(j == 0), stop=(j == 7)), [f"sq_{id_}", sl.free("bank7")], f"ss_{id_}")
            sl.read(f"sq{k}", f"ss_{id_}")
            if j % 2:
                t = j // 2
                for h in range(2):
                    s.op("t", lambda e, i, f, t=t, h=h: e.transpose(bk[6][:, h * P:(h + 1) * P], vT[:, h, t * P:(t + 1) * P], g.ident[:]),
                         [f"silu_v{h}{z}", sl.free("bank6")], f"tv{t}{h}{z}")
                s.op("s", lambda e, i, f, t=t: e.activation(v[par][:, t], bk[6][:, 0:256].rearrange("p (h n) -> p h n", h=H), ACT.Copy), [f"tv{t}1{z}", item], f"v{t}{z}")
                sl.read("bank6", f"v{t}{z}")
            yield
        sl.read("vT", f"tv31{z}")
        s.op("g", lambda e, i, f: e.tensor_tensor(sgw[par][:].rearrange("p t (h v) -> p (t h) v", v=64), sgw[par][:].rearrange("p t (h v) -> p (t h) v", v=64), g.onw[:, None, :].broadcast_to((P, 16, 64)), ALU.mult),
             [f"sg0{z}", f"sg1{z}"], f"sgw{z}")
        s.op("s", lambda e, i, f: e.activation(nr[:], bk[7][0:8, :], ACT.Sqrt), [f"ss_q3{z}", sl.free("nr")], f"nrm{z}")
        sl.read("bank7", f"nrm{z}")
        s.op("v", lambda e, i, f: e.reciprocal(nr[:], nr[:]), [f"nrm{z}"], f"rn{z}")
        yield
        yield
        yield
        for j, (n, h) in enumerate(tiles[2:]):
            id_, b, d = f"{n}{h}{z}", 6 + j % 2, dest(n, h)
            s.op("t", lambda e, i, f, b=b, j=j: e.matmul(bk[b][:], g.ident[0:8, j:j + 1].broadcast_to((8, P)), nr[:], start=True, stop=True), [f"rn{z}", sl.free(f"bank{b}")], f"rb_{id_}")
            s.op("v", lambda e, i, f, d=d, b=b: e.scalar_tensor_tensor(d, bk[b][:], 1e6, d, ALU.min, ALU.mult), [f"rb_{id_}", f"sq_{id_}"], f"n_{id_}")
            sl.read(f"bank{b}", f"n_{id_}")
            yield
        sl.read("nr", f"rb_q3{z}")
        for t in range(TPB):
            b = 6 + t % 2
            for h in range(H):
                s.op("t", lambda e, i, f, b=b, t=t, h=h: e.transpose(bk[b][:, h * P:(h + 1) * P], kq[par][:, h, 0, t * P:(t + 1) * P], g.ident[:]),
                     [f"n_k{h}{z}", sl.free(f"bank{b}")], f"tk{t}{h}{z}")
            s.op("v", lambda e, i, f, b=b, t=t: e.tensor_tensor(kdec[par][:, t], bk[b][:].rearrange("p (h n) -> p h n", h=H), kd[par][:, 5, t, :, None].broadcast_to((P, H, P)), ALU.mult),
                 [f"tk{t}3{z}", "kd" + z, item], f"kdec{t}{z}")
            sl.read(f"bank{b}", f"kdec{t}{z}")
            yield

    def made(par, name):
        return (f"{name}_0", 1) if par == 0 else f"{name}_1"

    def setup(s, sl, par, t, p):
        z, kd_, kq_ = f"_{par}", kd[par], kq[par]
        T = f"{t}{z}"
        B = [2 * p, 2 * p + 1]
        s.op("t", lambda e, i, f: e.matmul(bk[B[0]][:].rearrange("p (h n) -> p h n", h=H), g.identb[:], g.negm[:, None, :].broadcast_to((P, H, P)), start=True, stop=False, skip_group_check=True),
             [sl.free(f"bank{B[0]}")])
        for h in range(H):
            s.op("t", lambda e, i, f, h=h: e.matmul(bk[B[0]][:, h * P:(h + 1) * P], kd_[:, 0, t, h:h + 1].broadcast_to((P, P)), g.upper[:], start=False, stop=True, skip_group_check=True),
                 [made(par, "kd")], f"G{T}{h}")
        for h in range(H):
            s.op("s", lambda e, i, f, h=h: e.activation(E[p][:, h, :], bk[B[0]][:, h * P:(h + 1) * P], ACT.Exp, bias=kd_[:, 1, t, h:h + 1]),
                 [f"G{T}3", sl.free(f"E{p}")], f"E{T}{h}")
        sl.read(f"bank{B[0]}", f"E{T}3")
        for q in (1, 0):
            b = B[q]
            for h in (2 * (1 - q), 2 * (1 - q) + 1):
                s.op("t", lambda e, i, f, h=h, b=b: e.matmul(bk[b][:, (h % 2) * 256:(h % 2) * 256 + 256].rearrange("p (a n) -> p a n", a=2), kq_[:, h, 0, t * P:(t + 1) * P], kq_[:, h, :, t * P:(t + 1) * P], start=True, stop=True),
                     [made(par, f"n_k{h}"), made(par, f"n_q{h}"), sl.free(f"bank{b}")], f"KQ{T}{h}")
            for h in (2 * (1 - q), 2 * (1 - q) + 1):
                c0 = (h % 2) * 256
                s.op("v", lambda e, i, f, h=h, b=b, c0=c0: e.scalar_tensor_tensor(M[p][:, h, :], bk[b][:, c0:c0 + P], kd_[:, 2, t, h:h + 1], E[p][:, h, :], ALU.mult, ALU.mult),
                     [f"KQ{T}{h | 1}", f"E{T}{h}", sl.free(f"M{p}")], f"M{T}{h}")
            h = 2 * (1 - q)
            s.op("v", lambda e, i, f, h=h, b=b: e.tensor_tensor(Dm[t][:, h:h + 2, :], bk[b][:].rearrange("p (h a n) -> p h a n", h=2, a=2)[:, :, 1, :], E[p][:, h:h + 2, :], ALU.mult),
                 [f"KQ{T}{h+1}", f"E{T}3", sl.free(f"D{t}")], f"D{T}{h}")
            sl.read(f"bank{b}", f"D{T}{h}")
            if q:
                yield
        sl.read(f"E{p}", f"D{T}2")
        s.op("g", lambda e, i, f: e.tensor_copy(X[p][:], g.ident[:, None, :].broadcast_to((P, H, P))), [sl.free(f"X{p}")], f"X{T}init", alone=True)
        s.op("g", lambda e, i, f: e.tensor_copy(Pf[t][:], g.ident[:, None, :].broadcast_to((P, H, P))), [sl.free(f"P{t}")], f"P{T}init", alone=True)
        s.op("v", lambda e, i, f: e.copy_predicated(Pf[t][:], g.mask[:, 0, 0, None, :].broadcast_to((P, H, P)), M[p][:]), [f"P{T}init", f"M{T}3"], f"P{T}0", alone=True)
        yield
        for h in range(H):
            s.op("t", lambda e, i, f, h=h: e.transpose(bk[B[1]][:, h * P:(h + 1) * P], M[p][:, h, :], g.ident[:]), [f"M{T}3", sl.free(f"bank{B[1]}")], f"MT{T}{h}")
        s.op("v", lambda e, i, f: e.copy_predicated(X[p][:], g.mask[:, 0, 1, None, :].broadcast_to((P, H, P)), bk[B[1]][:].rearrange("p (h n) -> p h n", h=H)), [f"X{T}init", f"MT{T}3"], f"X{T}0", alone=True)
        sl.read(f"bank{B[1]}", f"X{T}0")
        yield

    def invert(s, sl, par, pair):
        z = f"_{par}"
        both = [setup(s, sl, par, 2 * pair + p, p) for p in range(2)]
        for _ in range(3):
            for p in range(2):
                next(both[p])
                yield
        for l in range(1, 7):
            last = l == 6
            nW = 64 if last else P
            for p in range(2):
                a, T = 2 * p, f"{2 * pair + p}{z}"
                for h in range(H):
                    s.op("t", lambda e, i, f, h=h, a=a, p=p, nW=nW: e.matmul(bk[a][:, h * P:h * P + nW], M[p][:, h, :], X[p][:, h, 0:nW], start=True, stop=True),
                         [f"X{T}{l-1}", sl.free(f"bank{a}")], f"W{T}{l}{h}")
                s.op("s", lambda e, i, f, a=a, p=p, nW=nW: e.activation(W[p][:, :, 0:nW], bk[a][:].rearrange("p (h n) -> p h n", h=H)[:, :, 0:nW], ACT.Copy), [f"W{T}{l}3", sl.free(f"W{p}")], f"We{T}{l}")
                sl.read(f"bank{a}", f"We{T}{l}")
                if last:
                    sl.read(f"M{p}", f"W{T}{l}3")
                    sl.read(f"X{p}", f"W{T}{l}3")
            yield
            for p in range(2):
                a, b, t = 2 * p, 2 * p + 1, 2 * pair + p
                T = f"{t}{z}"
                if not last:
                    for h in range(H):
                        s.op("t", lambda e, i, f, h=h, a=a, p=p, t=t: e.matmul(bk[a][:, h * P:(h + 1) * P], Pf[t][:, h, :], W[p][:, h, :], start=True, stop=True),
                             [f"We{T}{l}", f"P{T}{l-1}", sl.free(f"bank{a}")], f"XW{T}{l}{h}")
                    s.op("v", lambda e, i, f, a=a, p=p, l=l: e.copy_predicated(X[p][:], g.mask[:, l, 1, None, :].broadcast_to((P, H, P)), bk[a][:].rearrange("p (h n) -> p h n", h=H)), [f"XW{T}{l}3", f"W{T}{l}3"], f"X{T}{l}", alone=True)
                    sl.read(f"bank{a}", f"X{T}{l}")
                    for h in range(H):
                        s.op("t", lambda e, i, f, h=h, b=b, p=p, t=t: e.matmul(bk[b][:, h * P:(h + 1) * P], W[p][:, h, :], Pf[t][:, h, :], start=True, stop=True),
                             [f"We{T}{l}", f"P{T}{l-1}", sl.free(f"bank{b}")], f"WP{T}{l}{h}")
                    s.op("v", lambda e, i, f, b=b, t=t, l=l: e.copy_predicated(Pf[t][:], g.mask[:, l, 0, None, :].broadcast_to((P, H, P)), bk[b][:].rearrange("p (h n) -> p h n", h=H)), [f"WP{T}{l}3"], f"P{T}{l}", alone=True)
                else:
                    for h in range(H):
                        s.op("t", lambda e, i, f, h=h, b=b, p=p, t=t: e.matmul(bk[b][0:64, h * 64:(h + 1) * 64], W[p][:, h, 0:64], Pf[t][:, h, 64:P], start=True, stop=True),
                             [f"We{T}{l}", f"P{T}{l-1}", sl.free(f"bank{b}")], f"WP{T}{l}{h}")
                    s.op("v", lambda e, i, f, b=b, t=t: e.tensor_copy(Pf[t][0:64, :, 64:P], bk[b][0:64, 0:256].rearrange("p (h n) -> p h n", h=H)), [f"WP{T}{l}3"], f"P{T}{l}")
                sl.read(f"bank{b}", f"P{T}{l}")
                sl.read(f"W{p}", f"WP{T}{l}3")
                yield

    def state(s, sl, par, pair, batch):
        z, kd_, kq_ = f"_{par}", kd[par], kq[par]
        bR, bO = 4, 5
        ps = lambda b, o: bk[b][:, o:o + 256].rearrange("p (h n) -> p h n", h=H)
        for t in (2 * pair, 2 * pair + 1):
            T = f"{t}{z}"
            hb = lambda k, t=t: kd_[:, k, t, :, None].broadcast_to((P, H, 64))
            if t == 0:
                s.op("g", lambda e, i, f: e.memset(S[:], 0.0), [sl.free("S")], f"Sinit{z}", alone=True)
            prev = f"Sinit{z}" if t == 0 else f"S{t-1}{z}"
            for h in range(H):
                s.op("t", lambda e, i, f, h=h, t=t: e.matmul(bk[bR][:, h * 64:h * 64 + 64], kq_[:, h, 0, t * P:(t + 1) * P], S[:, h, :], start=True, stop=True),
                     [prev, made(par, f"n_k{h}"), sl.free("bank4")], f"KS{T}{h}")
            for h in range(H):
                s.op("t", lambda e, i, f, h=h, t=t: e.matmul(bk[bO][:, h * 64:h * 64 + 64], kq_[:, h, 1, t * P:(t + 1) * P], S[:, h, :], start=True, stop=True),
                     [prev, made(par, f"n_q{h}"), sl.free("bank5")], f"QS{T}{h}")
            s.op("v", lambda e, i, f, hb=hb: e.tensor_tensor(R[:], ps(bR, 0), hb(4), ALU.mult), [f"KS{T}3", made(par, "kd"), sl.free("R")], f"gks{T}")
            s.op("v", lambda e, i, f, t=t: e.tensor_tensor(R[:], v[par][:, t], R[:], ALU.subtract), [f"gks{T}", made(par, f"v{t}")], f"R{T}")
            s.op("v", lambda e, i, f, hb=hb: e.tensor_tensor(T1[:], ps(bO, 0), hb(4), ALU.mult), [f"QS{T}3"], f"orr{T}")
            s.op("v", lambda e, i, f, hb=hb: e.tensor_tensor(S[:], S[:], hb(6), ALU.mult), [prev, f"QS{T}3"], f"sdec{T}")
            yield
            for h in range(H):
                s.op("t", lambda e, i, f, h=h, t=t: e.matmul(bk[bR][:, 256 + h * 64:256 + h * 64 + 64], Pf[t][:, h, :], R[:, h, :], start=True, stop=True),
                     [f"R{T}", f"P{T}6"], f"Uh{T}{h}")
            sl.read("R", f"Uh{T}3")
            sl.read(f"P{t}", f"Uh{T}3")
            s.op("v", lambda e, i, f, hb=hb: e.tensor_tensor(U[:], ps(bR, 256), hb(3), ALU.mult), [f"Uh{T}3", sl.free("U")], f"U{T}")
            yield
            for h in range(H):
                s.op("t", lambda e, i, f, h=h, t=t: e.matmul(bk[bR][:, h * 64:h * 64 + 64], kdec[par][:, t, h, :], U[:, h, :], start=True, stop=True),
                     [f"U{T}", made(par, f"kdec{t}")], f"dS{T}{h}")
            for h in range(H):
                s.op("t", lambda e, i, f, h=h, t=t: e.matmul(bk[bO][:, 256 + h * 64:256 + h * 64 + 64], Dm[t][:, h, :], U[:, h, :], start=True, stop=True),
                     [f"U{T}", f"D{T}2", f"orr{T}"], f"O1{T}{h}")
            sl.read("U", f"O1{T}3")
            sl.read(f"D{t}", f"O1{T}3")
            s.op("v", lambda e, i, f: e.tensor_tensor(S[:], ps(bR, 0), S[:], ALU.add), [f"dS{T}3", f"sdec{T}"], f"S{T}")
            sl.read("bank4", f"S{T}")
            s.op("v", lambda e, i, f, t=t: e.tensor_tensor(o[:, t], ps(bO, 256), T1[:], ALU.add), [f"O1{T}3", f"orr{T}", sl.free("o")], f"orh{T}")
            sl.read("bank5", f"orh{T}")
            yield
        if pair == 0:
            return
        sl.read("S", f"S3{z}")
        sl.read(f"kd{par}", f"orh3{z}")
        flat = lambda t: t[:].rearrange("p t h v -> p (t h) v")
        s.op("g", lambda e, i, f: e.tensor_tensor(o2[:], o[:], o[:], ALU.mult), [f"orh3{z}", sl.free("o2")], f"osq{z}")
        s.op("v", lambda e, i, f: e.tensor_reduce(ss[:], flat(o2), AX.X, ALU.add), [f"osq{z}"], f"oss{z}")
        s.op("s", lambda e, i, f: e.activation(ss[:], ss[:], ACT.Sqrt, bias=g.eps5[:, 0:1], scale=1.0 / 64), [f"oss{z}"], f"orms{z}")
        yield
        s.op("v", lambda e, i, f: e.reciprocal(ss[:], ss[:]), [f"orms{z}"], f"orrms{z}")
        s.op("v", lambda e, i, f: e.tensor_tensor(flat(o2), flat(o), ss[:, :, None].broadcast_to((P, 16, 64)), ALU.mult), [f"orrms{z}"], f"on{z}")
        sl.read("o", f"on{z}")
        s.op("g", lambda e, i, f: e.tensor_tensor(flat(o2), flat(o2), sgw[par][:].rearrange("p t (h v) -> p (t h) v", v=64), ALU.mult), [f"on{z}", made(par, "sgw")], f"og{z}")
        sl.read(f"item{par}", f"og{z}")
        s.dma("y", lambda e, i, f: e.dma_start(rows(D["og"], i + batch)[:, :, par * 256:par * 256 + 256], o2[:].rearrange("p t h v -> p t (h v)")), [f"og{z}"], f"store_og{z}")
        sl.read("o2", f"store_og{z}")
        yield

    for name, count, batch in (("delta first", 1, 0), ("delta", N_BATCH - 1, 0), ("delta last", 1, N_BATCH - 1)):
        s = pg.stage(name, count)
        sl = Slots(s)
        if name == "delta first":
            finish(project(s, sl, 0, 0))
        else:
            ahead = project(s, sl, 1, batch)
            side_by_side(invert(s, sl, 0, 0), (ahead, 0.7))
            side_by_side(invert(s, sl, 0, 1), (state(s, sl, 0, 0, batch), 0.7), (ahead, 1.0))
            finish(ahead)
            ahead = project(s, sl, 0, 1) if name == "delta" else iter(())
            next(ahead, None)
            tail = state(s, sl, 0, 1, batch)
            main = invert(s, sl, 1, 0)
            side_by_side((next(main, None) for _ in range(8)), (tail, 1.2))
            finish(tail)
            side_by_side(main, (ahead, 1.0))
            side_by_side(invert(s, sl, 1, 1), (state(s, sl, 1, 0, batch), 0.7), (ahead, 1.0))
            finish(state(s, sl, 1, 1, batch), ahead)
        sl.close()

LEAVES, NODES, LW, GROUPS, GL = 256, 255, 16, 32, 8
SEGS = TILES + GROUPS - 1
ROW = DIM + 1


def fff(g, tag, times, first, rows_in, cols_in, act, out):
    nc, pg, sb, D = g.nc, g.pg, g.scoped(), g.dram
    bk = g.bank
    pg.group(times)
    U = 9
    nw = sb(tag + "nw", [P, KC, LEAVES])
    nb = sb(tag + "nb", [P, LEAVES])
    pos = sb(tag + "pos", [P, TILES])
    posi = sb(tag + "posi", [P, TILES], I32)
    seg = sb(tag + "seg", [P, 2, 64], I32)
    sorted_ = sb(tag + "xsT", [P, (KC + 1) * TOKENS])
    xsT = sorted_[:, 0:KC * TOKENS].rearrange("p (c n) -> p c n", c=KC)
    lrow = sorted_[:, KC * TOKENS:]
    xr = sb(tag + "xr", [P, TILES, ROW])
    W12 = 258 + DIM
    w12s = sb(tag + "w12", [P, U * W12])
    RT = 8
    xT = [w12s[:, j * KC * RT * P:(j + 1) * KC * RT * P].rearrange("p (c n) -> p c n", c=KC) for j in range(2)]
    bits, N, Pr = ([sorted_[:, (3 * j + n) * RT * LEAVES:(3 * j + n + 1) * RT * LEAVES].rearrange("p (t n) -> p t n", n=LEAVES) for j in range(2)] for n in range(3))
    leaf = [sb(f"{tag}leaf{j}", [P, RT]) for j in range(2)]
    ohb = [sb(f"{tag}ohb{j}", [P, RT, GROUPS], BF16) for j in range(2)]

    s = pg.stage("tree parameters", 1)
    s.dma("y", lambda e, i, f: e.dma_start(nw[:].rearrange("p c n -> p (c n)"), D["nwT"][ds(first + f, 1)].rearrange("a p c n -> p (a c n)")), [], "nw")
    s.dma("y", lambda e, i, f: e.dma_start(nb[:], D["nb"][ds(first + f, 1)].broadcast_to((P, LEAVES))), [], "nb")
    for k in range(2):
        s.op("v", lambda e, i, f, k=k: e.memset(N[k], 1.0))

    def route(s, k):
        x, bit, n, pr, z = xT[k], bits[k], N[k], Pr[k], f"_{k}"
        at = lambda i: (2 * i + k) * RT
        s.dma("y", lambda e, i, f: e.dma_start(x, D[cols_in][:, :, ds(at(i) * P, RT * P)].rearrange("c p n -> p c n")), [(f"lg{RT-1}{z}", 1)], "xT" + z)
        for t in range(RT):
            b = 4 * k + t // 2
            for c in range(KC):
                s.op("t", lambda e, i, f, c=c, t=t, b=b: e.matmul(bk[b][:, (t % 2) * 256:(t % 2) * 256 + 256], x[:, c, t * P:(t + 1) * P], nw[:, c, :], start=(c == 0), stop=(c == 1)),
                     ["xT" + z, (f"bits{t//2}{z}", 1)], f"lg{t}{z}" if c else None)
        for q in range(RT // 2):
            s.op("v", lambda e, i, f, q=q: e.scalar_tensor_tensor(bit[:, 2 * q:2 * q + 2, :], bk[4 * k + q][:].rearrange("p (t n) -> p t n", t=2), -1.0, nb[:, None, :].broadcast_to((P, 2, LEAVES)), ALU.mult, ALU.is_lt),
                 [f"lg{2*q+1}{z}"], f"bits{q}{z}")
        yield
        for l in range(8):
            a, b = (1 << l) - 1, (2 << l) - 1
            s.op("v", lambda e, i, f, a=a, b=b: e.tensor_tensor(pr[:, :, a:b], n[:, :, a:b], bit[:, :, a:b], ALU.mult), [f"bits{RT//2-1}{z}"] + ([f"NL{l-1}{z}", f"NR{l-1}{z}"] if l else []), f"Pr{l}{z}")
            yield
            if l < 7:
                kids = n[:, :, b:2 * b + 1].rearrange("p t (j k) -> p t j k", k=2)
                s.op("v", lambda e, i, f, a=a, b=b, kids=kids: e.tensor_tensor(kids[:, :, :, 0], n[:, :, a:b], pr[:, :, a:b], ALU.subtract), [f"Pr{l}{z}"], f"NL{l}{z}")
                s.op("v", lambda e, i, f, a=a, b=b, kids=kids: e.tensor_copy(kids[:, :, :, 1], pr[:, :, a:b]), [f"Pr{l}{z}"], f"NR{l}{z}", alone=True)
                yield
        s.op("v", lambda e, i, f: e.tensor_copy(ohb[k][:], n[:, :, GROUPS - 1:2 * GROUPS - 1]), [f"NL4{z}", f"NR4{z}", ("st_oh" + z, 1)], "ohb" + z, alone=True)
        s.op("v", lambda e, i, f: e.tensor_tensor(bit[:, :, 0:NODES], pr[:, :, 0:NODES], g.lvw[:, None, 0:NODES].broadcast_to((P, RT, NODES)), ALU.mult), [f"Pr7{z}"], "lw" + z)
        yield
        s.op("v", lambda e, i, f: e.tensor_reduce(leaf[k][:], bit[:, :, 0:NODES], AX.X, ALU.add), ["lw" + z, ("st_leaf" + z, 1)], "leaf" + z)
        s.dma("y", lambda e, i, f: e.dma_start(D["leaf"][:, ds(at(i), RT)], leaf[k][:]), ["leaf" + z], "st_leaf" + z)
        s.dma("y", lambda e, i, f: e.dma_start(D["ohb"][:, ds(at(i) * GROUPS, RT * GROUPS)], ohb[k][:].rearrange("p t n -> p (t n)")), ["ohb" + z], "st_oh" + z)
        yield

    s = pg.stage("routing", TILES // (2 * RT))
    finish(route(s, 0), route(s, 1))

    acc = sb(tag + "acc", [P, TILES * DIM])
    TG = TILES * GROUPS
    def part(n, w=TG):
        o = part.at
        part.at += w
        return acc[:, o:o + w]
    part.at = 0
    cnt, A0, A1, c2 = (part(n) for n in range(4))
    cmp = part(4, 2048)
    tot, st, t0, t1, ra, rg = (part(5, 64)[:, 0:32] for _ in range(6))
    sgf = part(6, 128)
    oh = sb(tag + "oh", [P, TG], BF16)
    lf = sb(tag + "lf", [P, TILES])
    tg = lambda a: a.rearrange("p (t n) -> p t n", n=GROUPS)
    s = pg.stage("sort", 1)
    s.dma("y", lambda e, i, f: e.dma_start(oh[:], D["ohb"]), [], "oh")
    s.dma("y", lambda e, i, f: e.dma_start(lf[:], D["leaf"]), [], "lf")
    s.dma("y", lambda e, i, f: e.dma_start(xr[:, :, 0:DIM], D[rows_in].rearrange("(t p) d -> p t d", p=P)), [], "xr")
    for q in range(2):
        s.op("t", lambda e, i, f, q=q: e.matmul(bk[q][:], g.onesb[:], oh[:, q * 512:(q + 1) * 512], start=True, stop=True), ["oh"], f"cnt{q}")
        s.op("t", lambda e, i, f, q=q: e.matmul(bk[2 + q][:], g.upperb[:], oh[:, q * 512:(q + 1) * 512], start=True, stop=True), ["oh"], f"cum{q}")
    for q in range(2):
        s.op("v", lambda e, i, f, q=q: e.tensor_copy(cnt[:, q * 512:(q + 1) * 512], bk[q][:]), [f"cnt{q}"], f"cn{q}")
    cur, last = cnt, ["cn0", "cn1"]
    for k in range(5):
        d, new = GROUPS << k, (A0, A1)[k % 2]
        s.op("v", lambda e, i, f, d=d, cur=cur, new=new: e.tensor_tensor(new[:, d:], cur[:, d:], cur[:, :TG - d], ALU.add), last, f"pa{k}")
        s.op("v", lambda e, i, f, d=d, cur=cur, new=new: e.tensor_copy(new[:, :d], cur[:, :d]), last, f"pb{k}")
        cur, last = new, [f"pa{k}", f"pb{k}"]
    pref = cur
    s.op("v", lambda e, i, f: e.tensor_copy(tot, pref[:, TG - GROUPS:]), last, "tot")
    cur, lastg = tot, ["tot"]
    for k in range(5):
        d, new = 1 << k, (t0, t1)[k % 2]
        s.op("v", lambda e, i, f, d=d, cur=cur, new=new: e.tensor_tensor(new[:, d:], cur[:, d:], cur[:, :GROUPS - d], ALU.add), lastg, f"ga{k}")
        s.op("v", lambda e, i, f, d=d, cur=cur, new=new: e.tensor_copy(new[:, :d], cur[:, :d]), lastg, f"gb{k}")
        cur, lastg = new, [f"ga{k}", f"gb{k}"]
    s.op("v", lambda e, i, f, cur=cur: e.tensor_tensor(st, cur, tot, ALU.subtract), lastg, "start")
    s.op("v", lambda e, i, f: e.tensor_tensor(c2, pref, cnt, ALU.subtract), last, "q0")
    s.op("v", lambda e, i, f: e.tensor_tensor(tg(c2), tg(c2), st[:, None, :].broadcast_to((P, TILES, GROUPS)), ALU.add), ["q0", "start"], "q1")
    for q in range(2):
        s.op("v", lambda e, i, f, q=q: e.tensor_tensor(c2[:, q * 512:(q + 1) * 512], bk[2 + q][:], c2[:, q * 512:(q + 1) * 512], ALU.add), ["q1", f"cum{q}"], f"q2{q}")
    s.op("v", lambda e, i, f: e.tensor_tensor(c2, c2, oh[:], ALU.mult), ["q20", "q21"], "q3")
    s.op("v", lambda e, i, f: e.tensor_reduce(pos[:], tg(c2), AX.X, ALU.add), ["q3"], "pos")
    s.op("v", lambda e, i, f: e.tensor_scalar(posi[:], pos[:], -1.0, None, ALU.add), ["pos"], "posi")
    s.op("v", lambda e, i, f: e.tensor_copy(xr[:, :, DIM:ROW], lf[:, :, None]), ["xr", "lf"], "xrl")
    for t in range(TILES):
        s.dma("g", lambda e, i, f, t=t: e.indirect_dma_start(D["xs"], bass.IndirectOffsetOnAxis(posi[:, t:t + 1].bitcast(U32), 0), xr[:, t, :], None), ["posi", "xrl"], f"sc{t}")
    c3 = lambda n, a, b: cmp[:, 0:a * b].rearrange("p (a b) -> p a b", b=b)
    ir = g.iota
    s.op("v", lambda e, i, f: e.tensor_tensor(c3(0, 32, 32), st[:, None, :].broadcast_to((P, 32, 32)), g.iota128[:, 0:32, None].broadcast_to((P, 32, 32)), ALU.is_lt), ["start"], "m0")
    s.op("v", lambda e, i, f: e.tensor_reduce(ra, c3(0, 32, 32), AX.X, ALU.add), ["m0"], "m1")
    s.op("v", lambda e, i, f: e.tensor_tensor(ra, ra, ir[:, 0:32], ALU.add), ["m1"], "ra")
    s.op("v", lambda e, i, f: e.tensor_tensor(c3(0, 32, 32), g.iota128[:, None, 0:32].broadcast_to((P, 32, 32)), st[:, :, None].broadcast_to((P, 32, 32)), ALU.is_le), ["m1"], "m2")
    s.op("v", lambda e, i, f: e.tensor_reduce(rg, c3(0, 32, 32), AX.X, ALU.add), ["m2"], "m3")
    s.op("v", lambda e, i, f: e.tensor_tensor(rg, rg, ir[:, 0:32], ALU.add), ["m3"], "rg")
    for n, (r, wait) in enumerate(((ra, "ra"), (rg, "rg"))):
        s.op("v", lambda e, i, f, r=r: e.tensor_tensor(c3(0, 63, 32), r[:, None, :].broadcast_to((P, 63, 32)), ir[:, 1:64, None].broadcast_to((P, 63, 32)), ALU.is_le), [wait, "m3"] + (["n1"] if n else []), "n0" if n == 0 else "n2")
        s.op("v", lambda e, i, f, n=n: e.tensor_reduce(sgf[:, n * 64:n * 64 + 63], c3(0, 63, 32), AX.X, ALU.add), ["n0" if n == 0 else "n2"], "n1" if n == 0 else "n3")
    s.op("v", lambda e, i, f: e.tensor_scalar(seg[:, 0, 0:63], sgf[:, 0:63], -1.0, float(P), ALU.add, ALU.mult), ["n1"], "sg0")
    s.op("v", lambda e, i, f: e.tensor_scalar(seg[:, 1, 0:63], sgf[:, 64:127], -1.0, None, ALU.add), ["n3"], "sg2")
    s.op("v", lambda e, i, f: e.memset(acc[:], 0.0), ["sg0", "sg2"])

    xss = [sb(f"{tag}xs{j}", [P, TPB, ROW]) for j in range(2)]
    batches = pg.stage("sorted", N_BATCH // 2)

    def columns(k):
        s, xs, bk = Side(batches, k, lambda i: 2 * i + k), xss[k], g.bank[3 * k:3 * k + 3]
        s.dma("y", lambda e, i, f: e.dma_start(xs[:], rows(D["xs"], i)), [("lr3", 1), ("t13", 1)], "xs")
        for c in range(KC):
            for t in range(TPB):
                s.op("t", lambda e, i, f, c=c, t=t: e.transpose(bk[c][:, t * P:(t + 1) * P], xs[:, t, c * P:(c + 1) * P], g.ident[:]), ["xs", (f"e{c}", 1)], f"t{c}{t}")
        for t in range(TPB):
            s.op("t", lambda e, i, f, t=t: e.matmul(bk[2][:, t * P:(t + 1) * P], xs[:, t, DIM:ROW].broadcast_to((P, P)), g.ident[:], start=True, stop=True), ["xs", ("e2", 1)], f"lr{t}")
        s.op("s", lambda e, i, f: e.activation(xsT[:, 0, ds(i * SEQ, SEQ)], bk[0][:], ACT.Copy), ["t03"], "e0", alone=True)
        s.op("v", lambda e, i, f: e.tensor_copy(xsT[:, 1, ds(i * SEQ, SEQ)], bk[1][:]), ["t13"], "e1", alone=True)
        s.op("s", lambda e, i, f: e.activation(lrow[:, ds(i * SEQ, SEQ)], bk[2][:], ACT.Copy), ["lr3"], "e2", alone=True)

    columns(0)
    columns(1)

    w12 = [w12s[:, j * W12:(j + 1) * W12] for j in range(U)]
    w1, w2 = [t[:, 0:258] for t in w12], [t[:, 258:] for t in w12]
    b2 = [sb(f"{tag}b2_{j}", [GL, ROW]) for j in range(U)]
    hT = [sb(f"{tag}hT_{j}", [P, P]) for j in range(4)]
    hm = [sb(f"{tag}hm_{j}", [P, P]) for j in range(4)]
    m8 = [sb(f"{tag}m8_{j}", [GL, P]) for j in range(4)]
    s = pg.stage("segments", SEGS // U)
    sl = Slots(s)
    at = {}

    def load(e, i, j, what, key):
        at[key] = e.value_load(seg[0:1, what, ds(i * U + j, 1)], min_val=0, max_val=[TOKENS - P, GROUPS - 1][what])

    def loads(j):
        def group_loads(e, i, f, j=j):
            load(e, i, j, 1, ("y", j))
            return e.dma_start(w12[j], D["w12p"][ds(at["y", j] + (first + f) * GROUPS, 1)].rearrange("a p n -> p (a n)"))

        def bias_loads(e, i, f, j=j):
            load(e, i, j, 1, ("s", j))
            return e.dma_start(b2[j][:], D["b2p"][ds((at["s", j] + (first + f) * GROUPS) * GL, GL), :])
        s.dma("y", group_loads, [(f"hmd{j}", 1), (f"h{j}", 1), (f"o{j}", 1)], f"w1{j}")
        s.dma("s", bias_loads, [(f"o{j}", 1), (f"m8d{j}", 1)], f"b2{j}")

    def hidden(j):
        b, r = j % 4, j % 4

        def first_half(e, i, f):
            if j == 0:
                for n in range(U):
                    load(e, i, n, 0, ("t", n))
            return e.matmul(bk[b][:, 0:P], w1[j][:, 0:P], xsT[:, 0, ds(at["t", j], P)], start=True, stop=False)
        s.op("t", first_half, [f"w1{j}", sl.free(f"bank{b}")])
        s.op("t", lambda e, i, f: e.matmul(bk[b][:, 0:P], w1[j][:, P:2 * P], xsT[:, 1, ds(at["t", j], P)], start=False, stop=True), [], f"hp{j}")
        s.op("s", lambda e, i, f: e.activation(hT[r][:], bk[b][:, 0:P], act, bias=w1[j][:, 256:257]), [f"hp{j}", sl.free(f"hT{r}")], f"h{j}")
        sl.read(f"bank{b}", f"h{j}")

        def masks(e, i, f):
            load(e, i, j, 0, ("v", j))
            return e.scalar_tensor_tensor(hm[r][:], lrow[:, ds(at["v", j], P)], w1[j][:, 257:258], hT[r][:], ALU.is_equal, ALU.mult)
        s.op("v", masks, [f"h{j}", sl.free(f"hm{r}")], f"hmd{j}")
        s.op("v", lambda e, i, f: e.tensor_scalar(m8[r][:], lrow[0:GL, ds(at["v", j], P)], b2[j][:, DIM:ROW], None, ALU.is_equal), [f"b2{j}", sl.free(f"m8{r}")], f"m8d{j}")
        sl.read(f"hT{r}", f"hmd{j}")

    def output(j):
        b, r = 4 + j % 4, j % 4
        s.op("t", lambda e, i, f: e.matmul(bk[b][:, 0:DIM], hm[r][:], w2[j], start=True, stop=False), [f"hmd{j}", sl.free(f"bank{b}")])
        s.op("t", lambda e, i, f: e.matmul(bk[b][:, 0:DIM], m8[r][:], b2[j][:, 0:DIM], start=False, stop=True), [f"m8d{j}"], f"o{j}")
        sl.read(f"hm{r}", f"o{j}")
        sl.read(f"m8{r}", f"o{j}")

        def gather(e, i, f):
            row = acc[:, ds(at["v", j] * (DIM // P), DIM)]
            return e.tensor_tensor(row, bk[b][:, 0:DIM], row, ALU.add)
        s.op("v", gather, [f"o{j}", f"acc{j-1}" if j else (f"acc{U-1}", 1)], f"acc{j}")
        sl.read(f"bank{b}", f"acc{j}")

    for j in range(4):
        loads(j)
    for n in range(U + 3):
        if n + 4 < U:
            loads(n + 4)
        if n < U:
            hidden(n)
        if n >= 3:
            output(n - 3)
    sl.close()

    s = pg.stage("unsort", 1, late=True)
    yr = xr[:].rearrange("p t d -> p (t d)")[:, 0:TILES * DIM].rearrange("p (t d) -> p t d", d=DIM)
    s.dma("y", lambda e, i, f: e.dma_start(D["ys"].rearrange("(t p) d -> p t d", p=P), acc[:].rearrange("p (t d) -> p t d", d=DIM)), [], "ys")
    for t in range(TILES):
        s.dma("g", lambda e, i, f, t=t: e.indirect_dma_start(yr[:, t, :], None, D["ys"], bass.IndirectOffsetOnAxis(posi[:, t:t + 1].bitcast(U32), 0)), ["ys"], f"ga{t}")
    s.dma("g", lambda e, i, f: e.dma_start(D[out][ds(f, 1)].rearrange("a (t p) d -> p (a t) d", p=P), yr), [f"ga{t}" for t in range(TILES)], "out")

def turn(g, bk, s, src, dst, banks, id_, wait, free, by, n_chunks=KC, dst_wait=()):
    for c in range(n_chunks):
        b = banks[c % len(banks)]
        for t in range(TPB):
            s.op("t", lambda e, i, f, c=c, t=t, b=b: e.transpose(bk[b][:, t * P:(t + 1) * P], src[:, t, c * P:(c + 1) * P], g.ident[:]),
                 list(wait) + [free.free(f"bank{b}")], f"{id_}t{c}{t}")
        who = by[c % len(by)]
        if who == "s":
            s.op("s", lambda e, i, f, c=c, b=b: e.activation(dst[:, c, :], bk[b][:], ACT.Copy), [f"{id_}t{c}3"] + list(dst_wait), f"{id_}{c}")
        else:
            s.op("v", lambda e, i, f, c=c, b=b: e.tensor_copy(dst[:, c, :], bk[b][:]), [f"{id_}t{c}3"] + list(dst_wait), f"{id_}{c}", alone=True)
        free.read(f"bank{b}", f"{id_}{c}")


def attention(g):
    nc, pg, own, D = g.nc, g.pg, g.scoped(), g.dram
    pg.group()
    batches = pg.stage("attention", N_BATCH // 2)

    def one(side):
        s = Side(batches, side, lambda i: 2 * i + side)
        sl = Slots(s)
        bk = g.bank[4 * side:4 * side + 4]
        sb = lambda name, shape, dt=F32: own(f"{name}_{side}", shape, dt)
        q, k, v, xf, y = (sb("a_" + n, [P, TPB, DIM]) for n in ("q", "k", "v", "xf", "y"))
        qT, kT, yT = (sb("a_" + n, [P, KC, SEQ]) for n in ("qT", "kT", "yT"))
        pr = [sb(f"a_pr{j}", [P, SEQ]) for j in range(TPB)]
        pT = [sb(f"a_pT{j}", [P, TPB, P]) for j in range(TPB)]
        st = sb("a_st", [P, TPB, 4])
        for n, (t, w) in enumerate(((q, "qT"), (k, "kT"))):
            s.dma("y", lambda e, i, f, n=n, t=t: e.dma_start(t[:], rows(D["qkv"][n], i)), [(w + "t13", 1)], "qk"[n])
        s.dma("y", lambda e, i, f: e.dma_start(v[:], rows(D["qkv"][2], i)), [("av3", 1)], "v")
        s.dma("y", lambda e, i, f: e.dma_start(xf[:], rows(D["xf"], i)), [("y3", 1)], "xf")
        yield
        turn(g, bk, s, q, qT, (0, 1), "qT", ["q"], sl, "sv", dst_wait=[("sc3", 1)])
        yield
        turn(g, bk, s, k, kT, (2, 3), "kT", ["k"], sl, "sv", dst_wait=[("sc3", 1)])
        for t in range(TPB):
            yield
            for c in range(KC):
                s.op("t", lambda e, i, f, t=t, c=c: e.matmul(bk[t][:], qT[:, c, t * P:(t + 1) * P], kT[:, c, :], start=(c == 0), stop=(c == 1)),
                     ["qT0", "qT1", "kT0", "kT1", sl.free(f"bank{t}")], f"sc{t}" if c else None)
            s.op("v", lambda e, i, f, t=t: e.tensor_reduce(st[:, t, 0:1], bk[t][:], AX.X, ALU.max), [f"sc{t}", (f"ex{t}", 1)], f"mx{t}")
            s.op("v", lambda e, i, f, t=t: e.tensor_scalar(st[:, t, 1:2], st[:, t, 0:1], -1.0 / 16, None, ALU.mult), [f"mx{t}"], f"nm{t}")
            s.op("s", lambda e, i, f, t=t: e.activation(pr[t][:], bk[t][:], ACT.Exp, bias=st[:, t, 1:2], scale=1.0 / 16, accum_out=st[:, t, 2:3]), [f"nm{t}", (f"pt{t}3", 1), (f"rs{t}", 1)], f"ex{t}")
            sl.read(f"bank{t}", f"ex{t}")
        for t in range(TPB):
            yield
            for k_ in range(TPB):
                s.op("t", lambda e, i, f, t=t, k_=k_: e.transpose(bk[t][:, k_ * P:(k_ + 1) * P], pr[t][:, k_ * P:(k_ + 1) * P], g.ident[:]), [f"ex{t}", sl.free(f"bank{t}")], f"pt{t}{k_}")
            s.op("v", lambda e, i, f, t=t: e.tensor_copy(pT[t][:], bk[t][:].rearrange("p (k n) -> p k n", k=TPB)), [f"pt{t}3", (f"av{t}", 1)], f"pT{t}", alone=True)
            sl.read(f"bank{t}", f"pT{t}")
            s.op("v", lambda e, i, f, t=t: e.reciprocal(st[:, t, 3:4], st[:, t, 2:3]), [f"ex{t}"], f"rs{t}")
        for t in range(TPB):
            yield
            b = t
            for k_ in range(TPB):
                s.op("t", lambda e, i, f, t=t, k_=k_, b=b: e.matmul(bk[b][:, 0:DIM], pT[t][:, k_, :], v[:, k_, :], start=(k_ == 0), stop=(k_ == 3)), [f"pT{t}", "v", sl.free(f"bank{b}")], f"av{t}" if k_ == 3 else None)
            s.op("v", lambda e, i, f, t=t, b=b: e.scalar_tensor_tensor(y[:, t, :], bk[b][:, 0:DIM], st[:, t, 3:4], xf[:, t, :], ALU.mult, ALU.add), [f"av{t}", f"rs{t}", "xf", ("st_y", 1), ("yTt13", 1)], f"y{t}")
            sl.read(f"bank{b}", f"y{t}")
        s.dma("s", lambda e, i, f: e.dma_start(rows(D["y"], i), y[:]), ["y3"], "st_y")
        yield
        turn(g, bk, s, y, yT, (0, 1), "yT", ["y3"], sl, "sv", dst_wait=[("st_yT", 1)])
        s.dma("s", lambda e, i, f: e.dma_start(cols(D["yT"], i), yT[:]), ["yT0", "yT1"], "st_yT")
        sl.close()
        yield

    finish(one(0), one(1))


def combine(g):
    nc, pg, own, D = g.nc, g.pg, g.scoped(), g.dram
    pg.group()
    wo = own("b_wo", [P, 4, DIM])
    w = own("b_w", [P, DIM])
    s = pg.stage("combine weights", 1)
    s.dma("y", lambda e, i, f: e.dma_start(wo[:], D["wo0"]), [], "wo")
    s.dma("y", lambda e, i, f: e.dma_start(w[:], D["L1_ffn_attn_norm_w"][None, :].broadcast_to((P, DIM))), [], "w")
    batches = pg.stage("combine", N_BATCH // 2)

    def one(side):
        s = Side(batches, side, lambda i: 2 * i + side)
        sl = Slots(s)
        bk = g.bank[4 * side:4 * side + 4]
        sb = lambda name, shape, dt=F32: own(f"{name}_{side}", shape, dt)
        og = sb("b_og", [P, TPB, 512])
        ogT = sb("b_ogT", [P, 4, SEQ])
        x, y, ff, xn, a, a2 = (sb("b_" + n, [P, TPB, DIM]) for n in ("x", "y", "ff", "xn", "a", "a2"))
        xnT, aT = (sb("b_" + n, [P, KC, SEQ]) for n in ("xnT", "aT"))
        stat, mv, rs = sb("b_stat", [P, TPB, 6]), sb("b_mv", [P, TPB, 2]), sb("b_rs", [P, TPB, 4])
        s.dma("y", lambda e, i, f: e.dma_start(og[:], rows(D["og"], i)), [("ogTt33", 1)], "og")
        s.dma("y", lambda e, i, f: e.dma_start(y[:], rows(D["y"], i)), [("sum2", 1)], "y")
        s.dma("y", lambda e, i, f: e.dma_start(ff[:], rows(D["ff"][0], i)), [("sum2", 1)], "ff")
        s.dma("y", lambda e, i, f: e.dma_start(x[:], rows(D["x"], i)), [("st_x1", 1), ("xn3", 1)], "x")
        yield
        turn(g, bk, s, og, ogT, (0, 1, 2, 3), "ogT", ["og"], sl, "s", n_chunks=4, dst_wait=[("ow3", 1)])
        s.op("g", lambda e, i, f: e.tensor_tensor(y[:], x[:], y[:], ALU.add), ["x", "y"], "sum1")
        s.op("g", lambda e, i, f: e.tensor_tensor(x[:], y[:], ff[:], ALU.add), ["sum1", "ff"], "sum2")
        for t in range(TPB):
            yield
            b = t // 2
            for c in range(4):
                s.op("t", lambda e, i, f, t=t, c=c, b=b: e.matmul(bk[b][:, (t % 2) * 256:(t % 2) * 256 + 256], ogT[:, c, t * P:(t + 1) * P], wo[:, c, :], start=(c == 0), stop=(c == 3)),
                     [f"ogT{c}", sl.free(f"bank{b}")], f"ow{t}" if c == 3 else None)
        for q in range(2):
            s.op("v", lambda e, i, f, q=q: e.tensor_tensor(x[:, 2 * q:2 * q + 2, :], bk[q][:].rearrange("p (t n) -> p t n", t=2), x[:, 2 * q:2 * q + 2, :], ALU.add), [f"ow{2*q+1}", "sum2"], f"x1{q}")
            sl.read(f"bank{q}", f"x1{q}")
        s.dma("s", lambda e, i, f: e.dma_start(rows(D["x1"], i), x[:]), ["x11", "x10"], "st_x1")
        for t in range(TPB):
            yield
            s.op("v", lambda e, i, f, t=t: e.bn_stats(stat[:, t, :], x[:, t, :]), [f"x1{t//2}"], f"st{t}", alone=True)
        for t in range(TPB):
            yield
            s.op("v", lambda e, i, f, t=t: e.bn_aggr(mv[:, t, :], stat[:, t, :]), [f"st{t}"], f"ag{t}", alone=True)
        s.op("s", lambda e, i, f: e.activation(rs[:, :, 0:1], mv[:, :, 1:2], ACT.Sqrt, bias=g.eps5[:, 0:1]), ["ag3"], "sd")
        s.op("v", lambda e, i, f: e.reciprocal(rs[:, :, 1:2], rs[:, :, 0:1]), ["sd"], "rstd")
        for t in range(TPB):
            yield
            s.op("v", lambda e, i, f, t=t: e.tensor_scalar(xn[:, t, :], x[:, t, :], mv[:, t, 0:1], rs[:, t, 1:2], ALU.subtract, ALU.mult), ["rstd", ("xnTt13", 1), ("st_xn", 1), ("am3", 1)], f"xn{t}")
        s.dma("s", lambda e, i, f: e.dma_start(rows(D["xn2"], i), xn[:]), ["xn3"], "st_xn")
        yield
        turn(g, bk, s, xn, xnT, (2, 3), "xnT", ["xn3"], sl, "sv", dst_wait=[("st_xnT", 1)])
        s.dma("s", lambda e, i, f: e.dma_start(cols(D["xn2T"], i), xnT[:]), ["xnT0", "xnT1"], "st_xnT")
        rms(s, xn, a, a2, rs, w, g, ["xn3"], [("aTt13", 1)], "a")
        yield
        turn(g, bk, s, a, aT, (0, 1), "aT", ["am3"], sl, "sv", dst_wait=[("st_aT", 1)])
        s.dma("s", lambda e, i, f: e.dma_start(cols(D["aT"], i), aT[:]), ["aT0", "aT1"], "st_aT")
        sl.close()
        yield

    finish(one(0), one(1))


def rms(s, x, a, sq, rs, w, g, wait, free, n):
    s.op("g", lambda e, i, f: e.tensor_tensor(sq[:], x[:], x[:], ALU.mult), wait, n + "sq")
    s.op("v", lambda e, i, f: e.tensor_reduce(rs[:, :, 2], sq[:], AX.X, ALU.add), [n + "sq"], n + "ss")
    s.op("s", lambda e, i, f: e.activation(rs[:, :, 2], rs[:, :, 2], ACT.Sqrt, bias=g.eps6[:, 0:1], scale=1.0 / DIM), [n + "ss"], n + "rt")
    s.op("v", lambda e, i, f: e.reciprocal(rs[:, :, 3], rs[:, :, 2]), [n + "rt"], n + "rr")
    for t in range(TPB):
        s.op("v", lambda e, i, f, t=t: e.scalar_tensor_tensor(a[:, t, :], x[:, t, :], rs[:, t, 3:4], w[:], ALU.mult, ALU.mult), [n + "rr"] + list(free), f"{n}m{t}")


def second_layer(g):
    nc, pg, sb, D = g.nc, g.pg, g.scoped(), g.dram
    NH, HD, NE = 4, 64, 8
    pg.group()
    s = pg.stage("second layer's weights", 1)

    def weights(name, source, shape):
        t = sb(name, shape)
        s.dma("y", lambda e, i, f: e.dma_start(t[:], source), [], name)
        return t

    w = weights("g_w", D["gqa_w"], [P, KC, 5 * P])
    wv = weights("g_wv", D["gqa_wv"], [P, KC, P])
    wo = weights("g_wo", D["gqa_wo"], [P, 4, DIM])
    w_l = weights("l_w", D["lin_w"], [P, KC, 768])
    wo_l = weights("l_wo", D["lin_wo"], [P, KC, DIM])
    we = weights("m_we", D["moe_w"], [P, KC, NE * DIM])
    wg = weights("m_wg", D["moe_gate"], [P, KC, NE])
    w_e = weights("m_w", D["L1_ffn_ffn_norm_w"][None, :].broadcast_to((P, DIM)), [P, DIM])
    va = sb("l_va", [P, TPB, NH, HD + 1])
    s.op("v", lambda e, i, f: e.memset(va[:], 1.0))
    aT = sb("g_aT", [P, KC, SEQ])
    qkT = sb("g_qkT", [P, 5, SEQ])
    v = sb("g_v", [P, TPB, P])
    rsum, rrow = sb("g_rsum", [P, TPB, 16]), sb("g_rrow", [16, SEQ])
    xn = sb("g_xn", [P, TPB, DIM])
    st = sb("g_st", [P, TPB, 4, 4, 4])
    pr = [sb(f"g_pr{j}", [P, SEQ]) for j in range(5)]
    pT = [sb(f"g_pT{j}", [P, SEQ]) for j in range(3)]
    oT = sb("g_oT", [P, 4, SEQ])
    xT = sb("l_xT", [P, KC, SEQ])
    qk, ex, sq = (sb("l_" + n, [P, TPB, 512]) for n in ("qk", "ex", "sq"))
    ss = sb("l_ss", [P, TPB * 8])
    fT = sb("l_qkT", [P, TPB, 4, P])
    sT = sb("l_sT", [P, TPB, 2, 2, P])
    kv = sb("l_kv", [P, 2, HD + 1])
    den = sb("l_den", [P, 2, 2])
    y_l = sb("l_y", [P, TPB, DIM])
    yT = sb("l_yT", [P, KC, SEQ])
    lo = sb("l_lo", [P, TPB, DIM])
    h, x1, lin, tt, t2 = (sb("m_" + n, [P, TPB, DIM]) for n in ("h", "x1", "lin", "t", "t2"))
    tT = sb("m_tT", [P, KC, SEQ])
    rs_e = sb("m_rs", [P, TPB, 4])
    lg = sb("m_lg", [P, TPB, NE])
    m8 = sb("m_m8", [P, TPB, 8])
    ix = sb("m_ix", [P, TPB, 8], U32)
    ixf = sb("m_ixf", [P, TPB, 8])
    cw = sb("m_cw", [P, TPB, 4])
    c1, comb = sb("m_c1", [P, TPB, NE]), sb("m_comb", [P, TPB, NE])

    def grouped(s, sl, batch):
        bk = g.bank
        s.dma("y", lambda e, i, f: e.dma_start(aT[:], cols(D["aT"], i + batch)), [("pv", 1)], "aT")
        for j in range(5):
            b = j % 3
            yield
            for c in range(KC):
                s.op("t", lambda e, i, f, j=j, c=c, b=b: e.matmul(bk[b][:], w[:, c, j * P:(j + 1) * P], aT[:, c, :], start=(c == 0), stop=(c == 1)), ["aT", sl.free(f"bank{b}")], f"p{j}" if c else None)
            s.op("s", lambda e, i, f, j=j, b=b: e.activation(qkT[:, j, :], bk[b][:], ACT.Copy, scale=0.25 if j < 4 else 1.0), [f"p{j}", ("last_scores", 1)], f"qk{j}")
            sl.read(f"bank{b}", f"qk{j}")
        for t in range(TPB):
            for c in range(KC):
                s.op("t", lambda e, i, f, t=t, c=c: e.matmul(bk[3][:, t * P:(t + 1) * P], aT[:, c, t * P:(t + 1) * P], wv[:, c, :], start=(c == 0), stop=(c == 1)), ["aT", sl.free("bank3")], f"pv{t}" if c else None)
        s.alias("pv", "pv3")
        s.op("s", lambda e, i, f: e.activation(v[:], bk[3][:].rearrange("p (t n) -> p t n", t=TPB), ACT.Copy), ["pv3", ("last_av", 1)], "v")
        sl.read("bank3", "v")
        units = [(t, j, k) for t in range(TPB) for j in range(4) for k in range(4)]

        def scores(n):
            (t, j, k), b = units[n], n % 3
            W, u = (t + 1) * P, f"{t}{j}{k}"
            s.op("t", lambda e, i, f: e.matmul(bk[b][:, 0:W], qkT[32 * k:32 * k + 16, j, t * P:(t + 1) * P], qkT[32 * k:32 * k + 16, 4, 0:W], start=True, stop=False, skip_group_check=True),
                 [f"qk{j}", "qk4", sl.free(f"bank{b}")])
            s.op("t", lambda e, i, f: e.matmul(bk[b][:, W - P:W], g.identb[:], g.negl[:], start=False, stop=True, skip_group_check=True), [], "sc" + u)
            s.op("v", lambda e, i, f: e.tensor_reduce(st[:, t, j, 0, k:k + 1], bk[b][:, 0:W], AX.X, ALU.max, negate=True), ["sc" + u, ("ex" + u, 1)], "mx" + u)
            s.op("s", lambda e, i, f: e.activation(pr[n % 5][:, 0:W], bk[b][:, 0:W], ACT.Exp, bias=st[:, t, j, 0, k:k + 1], accum_out=st[:, t, j, 2, k:k + 1]),
                 ["mx" + u, sl.free(f"pr{n % 5}"), ("rs", 1)], "ex" + u)
            sl.read(f"bank{b}", "ex" + u)

        def transposes(n):
            (t, j, k), b = units[n], 3 + n % 2
            W, u = (t + 1) * P, f"{t}{j}{k}"
            for c in range(t + 1):
                s.op("t", lambda e, i, f, c=c: e.transpose(bk[b][:, c * P:(c + 1) * P], pr[n % 5][:, c * P:(c + 1) * P], g.ident[:]), ["ex" + u, sl.free(f"bank{b}")], f"tr{u}{c}")
            sl.read(f"pr{n % 5}", f"tr{u}{t}")
            if n % 3 == 0:
                s.op("s", lambda e, i, f: e.activation(pT[n % 3][:, 0:W], bk[b][:, 0:W], ACT.Copy), [f"tr{u}{t}", sl.free(f"pT{n % 3}")], "pT" + u)
            else:
                s.op("v", lambda e, i, f: e.tensor_copy(pT[n % 3][:, 0:W], bk[b][:, 0:W]), [f"tr{u}{t}", sl.free(f"pT{n % 3}")], "pT" + u, alone=True)
            sl.read(f"bank{b}", "pT" + u)

        def values(n):
            t, j, k = units[n]
            u, b = f"{t}{j}{k}", 5
            for c in range(t + 1):
                s.op("t", lambda e, i, f, c=c: e.matmul(bk[b][32 * k:32 * k + 32, j * P:(j + 1) * P], v[:, c, 32 * k:32 * k + 32], pT[n % 3][:, c * P:(c + 1) * P], start=(c == 0), stop=(c == t)), ["pT" + u, "v", sl.free(f"bank{b}")], "av" + u if c == t else None)
            sl.read(f"pT{n % 3}", "av" + u)

        def gathered(t):
            s.op("s", lambda e, i, f: e.activation(oT[:, :, t * P:(t + 1) * P], bk[5][:].rearrange("p (j n) -> p j n", j=4), ACT.Copy), [f"av{t}33", ("ho3", 1)], f"oe{t}")
            sl.read("bank5", f"oe{t}")

        for n in range(len(units) + 4):
            yield
            if n == 20:
                s.dma("y", lambda e, i, f: e.dma_start(xn[:], rows(D["xn2"], i + batch)), [("st_h", 1)], "xn")
            if n < len(units):
                scores(n)
            if 0 <= n - 3 < len(units):
                transposes(n - 3)
            if n >= 4:
                values(n - 4)
                if (n - 4) % 16 == 15:
                    gathered((n - 4) // 16)
        s.op("v", lambda e, i, f: e.reciprocal(st[:, :, :, 3, :], st[:, :, :, 2, :]), ["ex333"], "rs")
        s.op("v", lambda e, i, f: e.tensor_copy(rsum[:].rearrange("p t (j k) -> p (t j) k", k=4), st[:, :, :, 3, :].rearrange("p t j k -> p (t j) k")), ["rs", ("rt3", 1)], "rsc", alone=True)
        yield
        for t in range(TPB):
            s.op("t", lambda e, i, f, t=t: e.transpose(bk[3][0:16, t * P:(t + 1) * P], rsum[:, t, :], g.ident[:]), ["rsc", sl.free("bank3")], f"rt{t}")
        s.op("s", lambda e, i, f: e.activation(rrow[:], bk[3][0:16, :], ACT.Copy), ["rt3", ("rb3", 1)], "rr")
        sl.read("bank3", "rr")
        yield
        yield
        for j in range(4):
            s.op("t", lambda e, i, f, j=j: e.matmul(bk[j][:], g.slot[:, j, :], rrow[:], start=True, stop=True), ["rr", sl.free(f"bank{j}")], f"rb{j}")
            s.op("v", lambda e, i, f, j=j: e.tensor_tensor(oT[:, j, :], bk[j][:], oT[:, j, :], ALU.mult), ["oe3", f"rb{j}"], f"oT{j}")
            sl.read(f"bank{j}", f"oT{j}")
        yield
        yield
        s.alias("last_scores", "sc333")
        s.alias("last_av", "av333")
        for t in range(TPB):
            b = 3 + t // 2
            for c in range(4):
                s.op("t", lambda e, i, f, t=t, c=c, b=b: e.matmul(bk[b][:, (t % 2) * 256:(t % 2) * 256 + 256], oT[:, c, t * P:(t + 1) * P], wo[:, c, :], start=(c == 0), stop=(c == 3)), [f"oT{c}", sl.free(f"bank{b}")], f"ho{t}" if c == 3 else None)
        for q in range(2):
            s.op("v", lambda e, i, f, q=q: e.tensor_tensor(xn[:, 2 * q:2 * q + 2, :], bk[3 + q][:].rearrange("p (t n) -> p t n", t=2), xn[:, 2 * q:2 * q + 2, :], ALU.add), [f"ho{2*q+1}", "xn"], f"h{q}")
            sl.read(f"bank{3+q}", f"h{q}")
        s.dma("s", lambda e, i, f: e.dma_start(rows(D["h"], i + batch), xn[:]), ["h0", "h1"], "st_h")

    def linear(s, sl):
        bk = g.bank[6:8]
        s.dma("y", lambda e, i, f: e.dma_start(xT[:], cols(D["xn2T"], i)), [("pv3", 1)], "xT")
        for t in range(TPB):
            yield
            b, b2 = 0, 1
            for c in range(KC):
                s.op("t", lambda e, i, f, t=t, c=c, b=b: e.matmul(bk[b][:], xT[:, c, t * P:(t + 1) * P], w_l[:, c, 0:512], start=(c == 0), stop=(c == 1)), ["xT", sl.free(f"bank{b}")], f"pq{t}" if c else None)
            for c in range(KC):
                s.op("t", lambda e, i, f, t=t, c=c, b2=b2: e.matmul(bk[b2][:, 0:256], xT[:, c, t * P:(t + 1) * P], w_l[:, c, 512:768], start=(c == 0), stop=(c == 1)), ["xT", sl.free(f"bank{b2}")], f"pv{t}" if c else None)
            s.op("v", lambda e, i, f, t=t, b=b: e.tensor_scalar(ex[:, t, :], bk[b][:], 0.0, None, ALU.min), [f"pq{t}", (f"feat{t}", 1)], f"mn{t}")
            s.op("s", lambda e, i, f, t=t: e.activation(ex[:, t, :], ex[:, t, :], ACT.Exp), [f"mn{t}"], f"ex{t}")
            s.op("v", lambda e, i, f, t=t, b=b: e.scalar_tensor_tensor(qk[:, t, :], bk[b][:], 0.0, ex[:, t, :], ALU.max, ALU.add), [f"ex{t}", (f"kvu{t}", 1), (f"tq{t}3", 1)], f"feat{t}")
            sl.read(f"bank{b}", f"feat{t}")
            s.op("v", lambda e, i, f, t=t, b2=b2: e.tensor_copy(va[:, t, :, 0:HD], bk[b2][:, 0:256].rearrange("p (h d) -> p h d", h=NH)), [f"pv{t}", (f"kvu{t}", 1), (f"o{t}3", 1)], f"va{t}", alone=True)
            sl.read(f"bank{b2}", f"va{t}")
            s.op("g", lambda e, i, f, t=t: e.tensor_tensor(sq[:, t, :], qk[:, t, :], qk[:, t, :], ALU.mult), [f"feat{t}", ("ssum", 1)], f"sq{t}")
        h8 = lambda a: a[:].rearrange("p t (h d) -> p (t h) d", d=HD)
        s.op("v", lambda e, i, f: e.tensor_reduce(ss[:], h8(sq), AX.X, ALU.add), ["sq3", ("un", 1)], "ssum")
        s.op("s", lambda e, i, f: e.activation(ss[:], ss[:], ACT.Sqrt), ["ssum"], "nrm")
        s.op("v", lambda e, i, f: e.tensor_scalar(ss[:], ss[:], 1e-6, None, ALU.add), ["nrm"], "nrm2")
        s.op("v", lambda e, i, f: e.reciprocal(ss[:], ss[:]), ["nrm2"], "rn")
        s.op("v", lambda e, i, f: e.tensor_tensor(h8(qk), h8(qk), ss[:, :, None].broadcast_to((P, TPB * 8, HD)), ALU.mult), ["rn", "sq3"], "un")
        s.op("g", lambda e, i, f: e.memset(kv[:], 0.0), [("kvn3", 1), ("o33", 1)], "kvn", alone=True)
        for _ in range(4):
            yield
        for t in range(TPB):
            yield
            yield
            b = t % 2
            for j in range(4):
                s.op("t", lambda e, i, f, t=t, j=j, b=b: e.transpose(bk[b][:, j * P:(j + 1) * P], qk[:, t, j * P:(j + 1) * P], g.ident[:]), ["un", sl.free(f"bank{b}")], f"tq{t}{j}")
            s.op("s", lambda e, i, f, t=t, b=b: e.activation(fT[:, t], bk[b][:].rearrange("p (j n) -> p j n", j=4), ACT.Copy), [f"tq{t}3", (f"o{t}3", 1)], f"qT{t}")
            sl.read(f"bank{b}", f"qT{t}")
            yield
            for q in range(2):
                for h in (q, q + 2):
                    a = q * HD
                    s.op("t", lambda e, i, f, t=t, h=h, a=a, q=q: e.matmul(bk[q][:, (h // 2) * P:(h // 2 + 1) * P], fT[a:a + HD, t, 2 + h // 2, :], fT[a:a + HD, t, h // 2, :], start=True, stop=True), [f"qT{t}", sl.free(f"bank{q}")], f"s{t}{h}")
                s.op("v", lambda e, i, f, t=t, q=q: e.tensor_tensor(sT[:, t, q], bk[q][:, 0:256].rearrange("p (h n) -> p h n", h=2), g.upper[:, None, :].broadcast_to((P, 2, P)), ALU.mult), [f"s{t}{q+2}", (f"o{t}3", 1)], f"sT{t}{q}")
                sl.read(f"bank{q}", f"sT{t}{q}")
        for t in range(TPB):
            yield
            prev = "kvn" if t == 0 else f"kvn{t-1}"
            b2 = 0
            for q in range(2):
                b, a = q, q * HD
                for h in (q, q + 2):
                    o = (h // 2) * 65
                    s.op("t", lambda e, i, f, t=t, h=h, o=o, b=b, q=q: e.matmul(bk[b][:, o:o + 65], sT[:, t, q, h // 2, :], va[:, t, h, :], start=True, stop=False), [f"sT{t}{q}", f"va{t}", sl.free(f"bank{b}")])
                    s.op("t", lambda e, i, f, t=t, h=h, o=o, b=b, a=a: e.matmul(bk[b][:, o:o + 65], fT[a:a + HD, t, h // 2, :], kv[a:a + HD, h // 2, :], start=False, stop=True), [prev], f"o{t}{h}")
            for q in range(2):
                b = q
                ov = bk[b][:, 0:130].rearrange("p (j n) -> p j n", j=2)
                s.op("v", lambda e, i, f, ov=ov, q=q: e.tensor_scalar(den[:, q, :, None], ov[:, :, HD:HD + 1], 1e-6, None, ALU.add), [f"o{t}{q+2}"] + ([f"y{t-1}{q}"] if t else [(f"y3{q}", 1)]), f"d{t}{q}")
                s.op("v", lambda e, i, f, q=q: e.reciprocal(den[:, q, :], den[:, q, :]), [f"d{t}{q}"], f"rd{t}{q}")
                s.op("v", lambda e, i, f, t=t, ov=ov, q=q: e.tensor_tensor(y_l[:, t, :].rearrange("p (j q d) -> p j q d", q=2, d=HD)[:, :, q, :], ov[:, :, 0:HD], den[:, q, :, None].broadcast_to((P, 2, HD)), ALU.mult), [f"rd{t}{q}", ("yTt13", 1)], f"y{t}{q}")
                sl.read(f"bank{b}", f"y{t}{q}")
            yield
            for h in range(NH):
                a = (h % 2) * HD
                s.op("t", lambda e, i, f, t=t, h=h, a=a, b2=b2: e.matmul(bk[b2][a:a + HD, (h // 2) * 65:(h // 2) * 65 + 65], qk[:, t, 256 + h * HD:256 + (h + 1) * HD], va[:, t, h, :], start=True, stop=True), [sl.free(f"bank{b2}")], f"kv{t}{h}")
            s.alias(f"kvu{t}", f"kv{t}3")
            s.op("v", lambda e, i, f, b2=b2: e.tensor_tensor(kv[:], bk[b2][:, 0:130].rearrange("p (j n) -> p j n", j=2), kv[:], ALU.add), [f"kv{t}3", f"o{t}3", prev], f"kvn{t}")
            sl.read(f"bank{b2}", f"kvn{t}")
        yield
        turn(g, bk, s, y_l, yT, (0, 1), "yT", ["y30", "y31"], sl, "sv", dst_wait=[("lo3", 1)])
        for t in range(TPB):
            yield
            b = t // 2
            for c in range(KC):
                s.op("t", lambda e, i, f, t=t, c=c, b=b: e.matmul(bk[b][:, (t % 2) * 256:(t % 2) * 256 + 256], yT[:, c, t * P:(t + 1) * P], wo_l[:, c, :], start=(c == 0), stop=(c == 1)), ["yT0", "yT1", sl.free(f"bank{b}")], f"lo{t}" if c else None)
        for q in range(2):
            s.op("s", lambda e, i, f, q=q: e.activation(lo[:, 2 * q:2 * q + 2, :], bk[q][:].rearrange("p (t n) -> p t n", t=2), ACT.Copy), [f"lo{2*q+1}", ("st_lo", 1)], f"loe{q}")
            sl.read(f"bank{q}", f"loe{q}")
        s.dma("s", lambda e, i, f: e.dma_start(rows(D["lin"], i), lo[:]), ["loe1", "loe0"], "st_lo")

    def experts(s, sl):
        bk = g.bank[6:8]
        s.dma("y", lambda e, i, f: e.dma_start(h[:], rows(D["h"], i)), [("s1", 1), ("tm3", 1), ("=st_h", 1)], "h")
        s.dma("y", lambda e, i, f: e.dma_start(x1[:], rows(D["x1"], i)), [("st_out", 1)], "x1")
        s.dma("y", lambda e, i, f: e.dma_start(lin[:], rows(D["lin"], i)), [("s2", 1), ("st_lo", 1)], "lin")
        yield
        rms(s, h, tt, t2, rs_e, w_e, g, ["h"], [("tTt13", 1)], "t")
        s.op("g", lambda e, i, f: e.tensor_tensor(x1[:], x1[:], h[:], ALU.add), ["x1", "h"], "s1")
        s.op("g", lambda e, i, f: e.tensor_tensor(x1[:], x1[:], lin[:], ALU.add), ["s1", "lin"], "s2")
        yield
        turn(g, bk, s, tt, tT, (0, 1), "tT", ["tm3"], sl, "sv", dst_wait=[("last_exp", 1)])
        for t in range(TPB):
            yield
            for c in range(KC):
                s.op("t", lambda e, i, f, t=t, c=c: e.matmul(bk[0][:, t * NE:(t + 1) * NE], tT[:, c, t * P:(t + 1) * P], wg[:, c, :], start=(c == 0), stop=(c == 1)), ["tT0", "tT1", sl.free("bank0")], f"lg{t}" if c else None)
        s.op("v", lambda e, i, f: e.tensor_copy(lg[:], bk[0][:, 0:TPB * NE].rearrange("p (t n) -> p t n", t=TPB)), ["lg3"], "lg", alone=True)
        sl.read("bank0", "lg")
        for t in range(TPB):
            yield
            s.op("v", lambda e, i, f, t=t: e.max(m8[:, t, :], lg[:, t, :]), ["lg"], f"m8{t}", alone=True)
        for t in range(TPB):
            yield
            s.op("v", lambda e, i, f, t=t: e.max_index(ix[:, t, :], m8[:, t, :], lg[:, t, :]), [f"m8{t}"], f"ix{t}", alone=True)
        s.op("v", lambda e, i, f: e.tensor_copy(ixf[:], ix[:]), ["ix3"], "ixf", alone=True)
        s.op("v", lambda e, i, f: e.tensor_tensor(cw[:, :, 0:1], m8[:, :, 1:2], m8[:, :, 0:1], ALU.subtract), ["m83"], "dm")
        s.op("s", lambda e, i, f: e.activation(cw[:, :, 1:2], cw[:, :, 0:1], ACT.Exp), ["dm"], "e2")
        s.op("v", lambda e, i, f: e.tensor_scalar(cw[:, :, 2:3], cw[:, :, 1:2], 1.0, None, ALU.add), ["e2"], "w0")
        s.op("v", lambda e, i, f: e.reciprocal(cw[:, :, 2:3], cw[:, :, 2:3]), ["w0"], "w1")
        s.op("v", lambda e, i, f: e.tensor_tensor(cw[:, :, 3:4], cw[:, :, 2:3], cw[:, :, 1:2], ALU.mult), ["w1"], "w2")
        io = g.iota[:, None, 0:NE].broadcast_to((P, TPB, NE))
        for k, (dst, nm) in enumerate(((c1, "c1"), (comb, "c2"))):
            s.op("v", lambda e, i, f, k=k, dst=dst: e.tensor_tensor(dst[:], ixf[:, :, k:k + 1].broadcast_to((P, TPB, NE)), io, ALU.is_equal), ["ixf", ("last_acc", 1)], nm + "a")
            s.op("v", lambda e, i, f, k=k, dst=dst: e.tensor_tensor(dst[:], dst[:], cw[:, :, 2 + k:3 + k].broadcast_to((P, TPB, NE)), ALU.mult), [nm + "a", "w2"], nm)
        s.op("v", lambda e, i, f: e.tensor_tensor(comb[:], comb[:], c1[:], ALU.add), ["c1", "c2"], "comb")
        for t in range(TPB):
            yield
            for q in range(4):
                yield
                b = q % 2
                for c in range(KC):
                    s.op("t", lambda e, i, f, t=t, q=q, c=c, b=b: e.matmul(bk[b][:], tT[:, c, t * P:(t + 1) * P], we[:, c, q * 512:(q + 1) * 512], start=(c == 0), stop=(c == 1)), ["tT0", "tT1", sl.free(f"bank{b}")], f"x{t}{q}" if c else None)
                for n in range(2):
                    k = 2 * q + n
                    prev = f"a{t}{k-1}" if k else "s2"
                    s.op("v", lambda e, i, f, t=t, n=n, k=k, b=b: e.scalar_tensor_tensor(x1[:, t, :], bk[b][:, n * 256:(n + 1) * 256], comb[:, t, k:k + 1], x1[:, t, :], ALU.mult, ALU.add), [f"x{t}{q}", "comb", prev], f"a{t}{k}")
                sl.read(f"bank{b}", f"a{t}{2*q+1}")
        s.alias("last_exp", "x33")
        s.alias("last_acc", "a37")
        s.dma("s", lambda e, i, f: e.dma_start(rows(D["out"], i), x1[:]), ["a37"], "st_out")

    for name, count, batch in (("second layer first", 1, 0), ("second layer", N_BATCH - 1, 1), ("second layer last", 1, N_BATCH)):
        s = pg.stage(name, count)
        sl = Slots(s)
        now = Side(s, "beside", lambda i, batch=batch: i + batch)
        before = Side(s, "beside", lambda i, batch=batch: i + batch - 1)
        sl2 = Slots(now)

        def others():
            first = linear(now, sl2) if batch < N_BATCH else iter(())
            then = experts(before, sl2) if batch > 0 else iter(())
            next(first, None)
            next(then, None)
            for n, _ in enumerate(first):
                if n == 8:
                    next(then, None)
                yield
            yield from then
        other = others()
        if batch < N_BATCH:
            side_by_side(grouped(s, sl, batch), (other, (0.5 if batch == 0 else 1.0)))
        finish(other)
        sl.close()
        sl2.close()


SCRATCH = {"xf": ((TOKENS, DIM), F32), "xnT": ((KC, P, TOKENS), F32), "xfT": ((KC, P, TOKENS), F32), "ab": ((N_BATCH, P, 64), F32), "kinds": ((2, P, KINDS, TILES, 4), F32), "og": ((TOKENS, 512), F32),
 "leaf": ((P, TILES), F32), "ohb": ((P, TILES * GROUPS), BF16), "xs": ((TOKENS, ROW), F32), "ys": ((TOKENS, DIM), F32), "qkv": ((3, TOKENS, DIM), F32), "ff": ((1, TOKENS, DIM), F32),
 "y": ((TOKENS, DIM), F32), "yT": ((KC, P, TOKENS), F32), "x1": ((TOKENS, DIM), F32), "xn2": ((TOKENS, DIM), F32), "xn2T": ((KC, P, TOKENS), F32), "aT": ((KC, P, TOKENS), F32), "lin": ((TOKENS, DIM), F32), "h": ((TOKENS, DIM), F32)}
def all_stages(g):
    norms(g)
    decays(g)
    delta(g)
    fff(g, "t3", 3, 0, "xf", "xfT", ACT.Relu, "qkv")
    attention(g)
    fff(g, "t1", 1, 3, "y", "yT", ACT.Gelu, "ff")
    combine(g)
    second_layer(g)


def build(nc, shapes, out_shapes):
    with ExitStack() as ctx:
        dram = {n: nc.dram_tensor(n, s, dt, kind="ExternalInput").ap() for n, (s, dt) in shapes.items()}
        for n, s in out_shapes.items():
            dram[n] = nc.dram_tensor(n, s, F32, kind="ExternalOutput").ap()

        def scratch(n, s, dt=F32):
            dram[n] = nc.dram_tensor(n, s, dt, kind="Internal").ap()

        for n, (s, dt) in SCRATCH.items():
            scratch(n, s, dt)
        pg = Program(nc, ctx)
        g = Kernel(nc, pg, ctx, dram)
        g.load_constants()
        all_stages(g)
        if g.open is not None:
            g.open.close()
        pg.number()
        block = ctx.enter_context(nc.Block())
        for e, on in (("y", block.sync), ("t", block.tensor), ("v", block.vector), ("s", block.scalar), ("g", block.gpsimd)):
            def body(eng, e=e):
                pg.emit(eng, e)
            on(body)


def constants():
    r = np.arange(P)
    c = {"ident": np.eye(P, dtype=np.float32), "ones": np.ones((P, P), np.float32)}
    c["upper"] = (r[:, None] <= r[None, :]).astype(np.float32)
    c["negm"] = np.where(r[:, None] <= r[None, :], 0.0, -1e30).astype(np.float32)
    c["negl"] = np.ascontiguousarray(c["negm"].T)
    c["pick"] = np.zeros((P, 15), np.float32)
    c["pick"][:, 7] = 1.0
    c["slot"] = np.zeros((16, 4, P), np.float32)
    for j in range(4):
        for k in range(4):
            c["slot"][4 * j + k, j, 32 * k:32 * k + 32] = 1.0
    c["lvw"] = np.array([2.0 ** (7 - int(np.log2(n + 1))) for n in range(255)] + [0.0], np.float32)
    c["iota"] = np.arange(64).astype(np.float32)
    c["iota128"] = (128 * np.arange(64)).astype(np.float32)
    mask = np.zeros((P, 7, 2, P), np.uint32)
    for l in range(7):
        m = 1 << l
        low = (r // m) % 2 == 0
        same = (r[:, None] // (2 * m)) == (r[None, :] // (2 * m))
        mask[:, l, 0] = same & low[:, None] & ~low[None, :]
        mask[:, l, 1] = mask[:, l, 0].T
    c["mask"] = mask
    return c


def lay_out(a):
    z = constants()
    z["x"] = a["L0_attn_x"].reshape(TOKENS, DIM)
    kp = lambda w: w.reshape(KC, P, -1).transpose(1, 0, 2)
    z["wab"] = kp(np.concatenate([a["L0_attn_Wa"], a["L0_attn_Wb"]], 1))
    q, k, v, gt = (a[f"L0_attn_W{n}"] for n in "qkvg")
    z["w_qkvg"] = np.stack([kp(np.concatenate([q[:, j * 512:][:, :512], k[:, j * 512:][:, :512], v[:, j * 256:][:, :256], gt[:, j * 256:][:, :256]], 1)) for j in range(2)])
    taps = lambda w, j, n: w[j * n * P:(j + 1) * n * P].reshape(n, P, 4).transpose(1, 0, 2).reshape(P, n * 4)
    z["conv_w"] = np.stack([np.concatenate([taps(a["L0_attn_conv_q"], j, 4), taps(a["L0_attn_conv_k"], j, 4), taps(a["L0_attn_conv_v"], j, 2)], 1) for j in range(2)])
    for n in ("L0_attn_dt_bias", "L0_attn_A_log", "L0_attn_o_norm_w"):
        z[n] = a[n]
    tree = lambda n: [a[f"L0_ffn_{t}_{n}"] for t in "qkvf"]
    z["nwT"] = np.stack([np.concatenate([kp(w.T), np.zeros((P, KC, 1), np.float32)], 2) for w in tree("nw")])
    z["nb"] = np.stack([np.concatenate([w, np.zeros(1, np.float32)]) for w in tree("nb")])
    leaf = np.arange(LEAVES, dtype=np.float32)
    z["w12p"] = np.concatenate([np.concatenate([
        w.reshape(GROUPS, GL, KC, P, LW).transpose(0, 3, 2, 1, 4).reshape(GROUPS, P, 256),
        b.reshape(GROUPS, P, 1), np.repeat(leaf, LW).reshape(GROUPS, P, 1), w2.reshape(GROUPS, P, DIM)], 2)
        for w, b, w2 in zip(tree("w1"), tree("b1"), tree("w2"))])
    z["b2p"] = np.concatenate([np.concatenate([b, leaf[:, None]], 1) for b in tree("b2")])
    z["wo0"] = a["L0_attn_Wo"].reshape(4, P, DIM).transpose(1, 0, 2)
    z["lin_w"] = kp(np.concatenate([a[f"L1_attn_W{n}"].T for n in "qkv"], 1))
    z["lin_wo"] = kp(a["L1_attn_Wo"].T)
    wq = a["L1_ffn_wq"].T.reshape(DIM, 4, 4, 16).transpose(0, 2, 1, 3)
    wk = a["L1_ffn_wk"].T.reshape(DIM, 1, 4, 16)
    qk = np.concatenate([wq, wk], 1)
    z["gqa_w"] = kp(np.concatenate([qk, np.zeros_like(qk)], 3).reshape(DIM, 5 * P))
    wv = a["L1_ffn_wv"].T.reshape(DIM, 4, 16)
    z["gqa_wv"] = kp(np.concatenate([wv, np.zeros_like(wv)], 2).reshape(DIM, P))
    wo = a["L1_ffn_wo"].T.reshape(4, 4, 16, DIM).transpose(1, 0, 2, 3)
    z["gqa_wo"] = np.concatenate([wo, np.zeros_like(wo)], 2).reshape(4, P, DIM).transpose(1, 0, 2)
    z["moe_w"] = kp(a["L1_ffn_expert_w"].transpose(2, 0, 1).reshape(DIM, 8 * DIM))
    z["moe_gate"] = kp(a["L1_ffn_gate_w"].T)
    for n in ("L1_ffn_attn_norm_w", "L1_ffn_ffn_norm_w"):
        z[n] = a[n]
    return {n: np.ascontiguousarray(v) for n, v in z.items()}


def kernel(**inputs):
    import concourse.bacc as bacc
    from concourse.bass_utils import run_bass_kernel_spmd

    arrays = lay_out({n: np.asarray(v) for n, v in inputs.items()})
    nc = bacc.Bacc("TRN2", target_bir_lowering=False, num_devices=1)
    build(nc, {n: (v.shape, mybir.dt.from_np(v.dtype)) for n, v in arrays.items()}, {"out": (TOKENS, DIM)})
    r = run_bass_kernel_spmd(nc, [arrays], core_ids=[0])
    return r.results[0]["out"].reshape(N_BATCH, SEQ, DIM)
```
